# Optimizing a Trainium2 kernel written in Bass

```python
import numpy as np
import jax
import jax.numpy as jnp

def _softmax(x, axis=-1):
    return jax.nn.softmax(x, axis=axis)

def _gelu(x):
    return jax.nn.gelu(x, approximate=True)

def _silu(x):
    return jax.nn.silu(x)

def _sigmoid(x):
    return jax.nn.sigmoid(x)

def _layernorm(x, axis=-1, eps=1e-05):
    m = jnp.mean(x, axis=axis, keepdims=True)
    v = jnp.var(x, axis=axis, keepdims=True)
    return (x - m) / jnp.sqrt(v + eps)

def _scatter_add(tgt, idx, src, axis=0):
    return tgt.at[idx].add(src)

def _segment_sum(src, seg, n):
    return jax.ops.segment_sum(src, seg, n)
kernel_name = 'mk_decoder_postln_d2_seqx_r8_53841f'

def setup_inputs(seed: int=0):
    np.random.seed(seed)
    _w = jnp.asarray

    def _rec_inputs():
        import jax
        import jax.numpy as jnp
        _rk = jax.random.key(seed)
        x = -0.0002928 + 1 * jax.random.normal(jax.random.fold_in(_rk, 1), (64, 64, 128), jnp.float32)
        _lenS = 64 - jax.random.randint(jax.random.fold_in(_rk, 7), (64,), 0, max(1, 64 // 4) + 1, jnp.int32)
        _lenS2 = 64 - jax.random.randint(jax.random.fold_in(_rk, 8), (64,), 0, max(1, 64 // 4) + 1, jnp.int32)
        _ctx_1024P = jax.random.normal(jax.random.fold_in(_rk, 11), (64, 16, 128), jnp.float32)
        _ctx_1024c = jax.random.dirichlet(jax.random.fold_in(_rk, 511), 0.3 * jnp.ones((16,), jnp.float32), (64, 64))
        _ctx_1024t = jnp.einsum('bsk,bkd->bsd', _ctx_1024c, _ctx_1024P)
        _ctx_1024t = _ctx_1024t * jax.lax.rsqrt(jnp.mean(jnp.square(_ctx_1024t)) + 1e-12) * 0.953939
        ctx_1024 = -1.39393e-06 + 0.999914 * (_ctx_1024t + 0.3 * jax.random.normal(jax.random.fold_in(_rk, 611), (64, 64, 128), jnp.float32))
        return (x, ctx_1024)
    x, ctx_1024 = _rec_inputs()

    def _L0_attn_setup():
        import jax, jax.numpy as jnp
        import numpy as np
        D_IN = 128
        D_OUT = 128
        H = 16
        G = 4
        LF = 2
        HEAD_OUT = D_OUT // H
        DQ = HEAD_OUT // LF
        B, T = (2, 256)

        def _alibi_bias(T, dtype):
            slopes = jnp.asarray(2.0 ** (-8.0 * np.arange(1, H + 1) / H), dtype=dtype)
            pos = jnp.arange(T)
            rel = (pos[None, :] - pos[:, None]).astype(dtype)
            return slopes[:, None, None] * rel[None, :, :]
        key = jax.random.key(seed)
        ks = jax.random.split(key, 7)
        s = 0.02
        return {'x': jax.random.normal(ks[0], (B, T, D_IN), dtype=jnp.float32), 'Wq': jax.random.normal(ks[1], (D_IN, D_OUT // LF), dtype=jnp.float32) * s, 'Wk': jax.random.normal(ks[2], (D_IN, D_OUT // LF // G), dtype=jnp.float32) * s, 'Wv': jax.random.normal(ks[3], (D_IN, D_OUT // G), dtype=jnp.float32) * s, 'Wp': jax.random.normal(ks[4], (D_OUT, D_OUT), dtype=jnp.float32) * s, 'bp': jnp.zeros((D_OUT,), dtype=jnp.float32)}
    _L0_attn_all = _L0_attn_setup()
    _L0_attn_in = {k: v for k, v in _L0_attn_all.items() if k in ('Wq', 'Wk', 'Wv', 'Wp', 'bp')}
    del _L0_attn_all

    def _L0_xattn_setup():
        import jax, jax.numpy as jnp
        import numpy as np
        EPS = 1e-06
        LN_EPS = 1e-06

        def _mlstm_parallel_stabilized(q, k, v, igate_preact, fgate_preact):
            B, NH, S, DH = q.shape
            log_fg = jax.nn.log_sigmoid(fgate_preact[..., 0])
            cs = jnp.cumsum(log_fg, axis=-1)
            fg_mat = cs[..., :, None] - cs[..., None, :]
            mask = jnp.tril(jnp.ones((S, S), dtype=bool))
            log_D = jnp.where(mask, fg_mat + igate_preact[..., 0][..., None, :], -jnp.inf)
            max_log_D = jnp.max(log_D, axis=-1, keepdims=True)
            D = jnp.exp(log_D - max_log_D)
            k_scaled = k / jnp.sqrt(jnp.float32(DH)).astype(k.dtype)
            qk = jnp.einsum('bhsd,bhtd->bhst', q, k_scaled)
            C = qk * D
            normalizer = jnp.maximum(jnp.abs(jnp.sum(C, axis=-1, keepdims=True)), jnp.exp(-max_log_D))
            C_norm = C / (normalizer + EPS)
            return jnp.einsum('bhst,bhtd->bhsd', C_norm, v)

        def _multihead_layernorm(x, weight):
            mu = jnp.mean(x, axis=-1, keepdims=True)
            var = jnp.mean(jnp.square(x - mu), axis=-1, keepdims=True)
            xn = (x - mu) * jax.lax.rsqrt(var + LN_EPS)
            return xn * weight[None, :, None, :]
        key = jax.random.key(seed)
        ks = jax.random.split(key, 6)
        B, S, E, NH = (2, 256, 128, 8)
        q = jax.random.normal(ks[0], (B, S, E), dtype=jnp.float32)
        k = jax.random.normal(ks[1], (B, S, E), dtype=jnp.float32)
        v = jax.random.normal(ks[2], (B, S, E), dtype=jnp.float32)
        igate_kernel = jnp.zeros((3 * E, NH), dtype=jnp.float32)
        igate_bias = 0.1 * jax.random.normal(ks[3], (NH,), dtype=jnp.float32)
        fgate_kernel = jnp.zeros((3 * E, NH), dtype=jnp.float32)
        fgate_bias = jnp.linspace(3.0, 6.0, NH, dtype=jnp.float32)
        outnorm_weight = jnp.ones((NH, E // NH), dtype=jnp.float32)
        return {'q': q, 'k': k, 'v': v, 'igate_kernel': igate_kernel, 'igate_bias': igate_bias, 'fgate_kernel': fgate_kernel, 'fgate_bias': fgate_bias, 'outnorm_weight': outnorm_weight}
    _L0_xattn_all = _L0_xattn_setup()
    _L0_xattn_in = {k: v for k, v in _L0_xattn_all.items() if k in ('igate_kernel', 'igate_bias', 'fgate_kernel', 'fgate_bias', 'outnorm_weight')}
    del _L0_xattn_all

    def _L0_ffn_setup():
        import jax, jax.numpy as jnp
        import numpy as np
        B, S, D_IN, D_OUT = (16, 512, 128, 128)
        ACT_BITS = 8
        QB = float(2 ** (ACT_BITS - 1) - 1)
        key = jax.random.key(seed)
        k1, k2, k3 = jax.random.split(key, 3)
        x = jax.random.normal(k1, (B, S, D_IN), dtype=jnp.float32)
        ternary_weight = jax.random.randint(k2, (D_OUT, D_IN), 0, 3, dtype=jnp.int32)
        bias = jax.random.normal(k3, (D_OUT,), dtype=jnp.float32)
        act_scale = (jnp.max(jnp.abs(x)) / QB).astype(jnp.float32)
        return {'x': x, 'ternary_weight': ternary_weight, 'bias': bias, 'act_scale': act_scale}
    _L0_ffn_all = _L0_ffn_setup()
    _L0_ffn_in = {k: v for k, v in _L0_ffn_all.items() if k in ('ternary_weight', 'bias', 'act_scale')}
    del _L0_ffn_all

    def _L1_attn_setup():
        import jax, jax.numpy as jnp
        import numpy as np
        import math
        D_MODEL = 128
        NUM_HEADS = 16
        HEAD_DIM = D_MODEL // NUM_HEADS
        REPETITIONS = 3
        NEG = -10000.0

        def _self_attention(q, k, v, mask):
            scale = 1.0 / math.sqrt(q.shape[-1])
            scores = jnp.einsum('bthd,bshd->bhts', q, k * scale) + mask
            attn = jax.nn.softmax(scores, axis=-1)
            return jnp.einsum('bhts,bshd->bthd', attn, v)
        key = jax.random.key(seed)
        ks = jax.random.split(key, 5)
        B, S = (2, 256)
        x = jax.random.normal(ks[0], (B, S, D_MODEL), dtype=jnp.float32)
        Wqkv_w = jax.random.normal(ks[1], (3 * D_MODEL, D_MODEL), dtype=jnp.float32) * (1.0 / math.sqrt(D_MODEL))
        Wqkv_b = jax.random.normal(ks[2], (3 * D_MODEL,), dtype=jnp.float32) * 0.02
        out_w = jax.random.normal(ks[3], (D_MODEL, D_MODEL), dtype=jnp.float32) * (1.0 / math.sqrt(D_MODEL))
        out_b = jax.random.normal(ks[4], (D_MODEL,), dtype=jnp.float32) * 0.02
        return {'x': x, 'Wqkv_w': Wqkv_w, 'Wqkv_b': Wqkv_b, 'out_w': out_w, 'out_b': out_b}
    _L1_attn_all = _L1_attn_setup()
    _L1_attn_in = {k: v for k, v in _L1_attn_all.items() if k in ('Wqkv_w', 'Wqkv_b', 'out_w', 'out_b')}
    del _L1_attn_all

    def _L1_xattn_setup():
        import jax, jax.numpy as jnp
        import numpy as np
        D_MODEL = 128
        NUM_HEADS = 16
        D_K = D_MODEL // NUM_HEADS
        B, N = (2, 256)
        key = jax.random.key(seed)
        ks = jax.random.split(key, 11)
        s = 1.0 / np.sqrt(D_MODEL)
        inp = {'query': jax.random.normal(ks[0], (B, N, D_MODEL), jnp.float32), 'key': jax.random.normal(ks[1], (B, N, D_MODEL), jnp.float32), 'value': jax.random.normal(ks[2], (B, N, D_MODEL), jnp.float32), 'w_q': jax.random.normal(ks[3], (D_MODEL, D_MODEL), jnp.float32) * s, 'b_q': jax.random.normal(ks[4], (D_MODEL,), jnp.float32) * s, 'w_k': jax.random.normal(ks[5], (D_MODEL, D_MODEL), jnp.float32) * s, 'b_k': jax.random.normal(ks[6], (D_MODEL,), jnp.float32) * s, 'w_v': jax.random.normal(ks[7], (D_MODEL, D_MODEL), jnp.float32) * s, 'b_v': jax.random.normal(ks[8], (D_MODEL,), jnp.float32) * s, 'w_o': jax.random.normal(ks[9], (D_MODEL, D_MODEL), jnp.float32) * s, 'b_o': jax.random.normal(ks[10], (D_MODEL,), jnp.float32) * s}
        return inp
    _L1_xattn_all = _L1_xattn_setup()
    _L1_xattn_in = {k: v for k, v in _L1_xattn_all.items() if k in ('w_q', 'b_q', 'w_k', 'b_k', 'w_v', 'b_v', 'w_o', 'b_o')}
    del _L1_xattn_all

    def _L1_ffn_setup():
        import jax, jax.numpy as jnp
        import numpy as np
        EMB_DIM = 128
        HIDDEN = int(2 / 3 * 4 * EMB_DIM)
        NUM_EXPERTS = 8
        TOP_K = 2
        B, S = (4, 128)
        key = jax.random.key(seed)
        ks = jax.random.split(key, 5)
        sc = 1.0 / np.sqrt(EMB_DIM)
        sh = 1.0 / np.sqrt(HIDDEN)
        return {'x': jax.random.normal(ks[0], (B, S, EMB_DIM), dtype=jnp.float32), 'Wg': jax.random.normal(ks[1], (NUM_EXPERTS, EMB_DIM), dtype=jnp.float32) * sc, 'W1': jax.random.normal(ks[2], (NUM_EXPERTS, HIDDEN, EMB_DIM), dtype=jnp.float32) * sc, 'W2': jax.random.normal(ks[3], (NUM_EXPERTS, HIDDEN, EMB_DIM), dtype=jnp.float32) * sc, 'W3': jax.random.normal(ks[4], (NUM_EXPERTS, EMB_DIM, HIDDEN), dtype=jnp.float32) * sh}
    _L1_ffn_all = _L1_ffn_setup()
    _L1_ffn_in = {k: v for k, v in _L1_ffn_all.items() if k in ('Wg', 'W1', 'W2', 'W3')}
    del _L1_ffn_all
    return {'x': x, 'ctx_1024': ctx_1024, 'L0_attn_Wq': _L0_attn_in['Wq'], 'L0_attn_Wk': _L0_attn_in['Wk'], 'L0_attn_Wv': _L0_attn_in['Wv'], 'L0_attn_Wp': _L0_attn_in['Wp'], 'L0_attn_bp': _L0_attn_in['bp'], 'L0_xattn_igate_kernel': _L0_xattn_in['igate_kernel'], 'L0_xattn_igate_bias': _L0_xattn_in['igate_bias'], 'L0_xattn_fgate_kernel': _L0_xattn_in['fgate_kernel'], 'L0_xattn_fgate_bias': _L0_xattn_in['fgate_bias'], 'L0_xattn_outnorm_weight': _L0_xattn_in['outnorm_weight'], 'L0_ffn_ternary_weight': _L0_ffn_in['ternary_weight'], 'L0_ffn_bias': _L0_ffn_in['bias'], 'L0_ffn_act_scale': _L0_ffn_in['act_scale'], 'L1_attn_Wqkv_w': _L1_attn_in['Wqkv_w'], 'L1_attn_Wqkv_b': _L1_attn_in['Wqkv_b'], 'L1_attn_out_w': _L1_attn_in['out_w'], 'L1_attn_out_b': _L1_attn_in['out_b'], 'L1_xattn_w_q': _L1_xattn_in['w_q'], 'L1_xattn_b_q': _L1_xattn_in['b_q'], 'L1_xattn_w_k': _L1_xattn_in['w_k'], 'L1_xattn_b_k': _L1_xattn_in['b_k'], 'L1_xattn_w_v': _L1_xattn_in['w_v'], 'L1_xattn_b_v': _L1_xattn_in['b_v'], 'L1_xattn_w_o': _L1_xattn_in['w_o'], 'L1_xattn_b_o': _L1_xattn_in['b_o'], 'L1_ffn_Wg': _L1_ffn_in['Wg'], 'L1_ffn_W1': _L1_ffn_in['W1'], 'L1_ffn_W2': _L1_ffn_in['W2'], 'L1_ffn_W3': _L1_ffn_in['W3']}

def reference(x, ctx_1024, L0_attn_Wq, L0_attn_Wk, L0_attn_Wv, L0_attn_Wp, L0_attn_bp, L0_xattn_igate_kernel, L0_xattn_igate_bias, L0_xattn_fgate_kernel, L0_xattn_fgate_bias, L0_xattn_outnorm_weight, L0_ffn_ternary_weight, L0_ffn_bias, L0_ffn_act_scale, L1_attn_Wqkv_w, L1_attn_Wqkv_b, L1_attn_out_w, L1_attn_out_b, L1_xattn_w_q, L1_xattn_b_q, L1_xattn_w_k, L1_xattn_b_k, L1_xattn_w_v, L1_xattn_b_v, L1_xattn_w_o, L1_xattn_b_o, L1_ffn_Wg, L1_ffn_W1, L1_ffn_W2, L1_ffn_W3):
    import jax
    import jax.numpy as jnp

    def _L0_attn_ref(x, Wq, Wk, Wv, Wp, bp):
        import jax, jax.numpy as jnp
        import numpy as np
        D_IN = 128
        D_OUT = 128
        H = 16
        G = 4
        LF = 2
        HEAD_OUT = D_OUT // H
        DQ = HEAD_OUT // LF
        B, T = (2, 256)

        def _alibi_bias(T, dtype):
            slopes = jnp.asarray(2.0 ** (-8.0 * np.arange(1, H + 1) / H), dtype=dtype)
            pos = jnp.arange(T)
            rel = (pos[None, :] - pos[:, None]).astype(dtype)
            return slopes[:, None, None] * rel[None, :, :]
        b, t, _ = x.shape
        q = x @ Wq
        k = jnp.tile(x @ Wk, (1, 1, G))
        v = jnp.tile(x @ Wv, (1, 1, G))
        q = q.reshape(b, t, H, DQ).transpose(0, 2, 1, 3)
        k = k.reshape(b, t, H, DQ).transpose(0, 2, 1, 3)
        v = v.reshape(b, t, H, HEAD_OUT).transpose(0, 2, 1, 3)
        scores = jnp.einsum('bhqd,bhkd->bhqk', q, k)
        causal = jnp.triu(jnp.ones((t, t), dtype=bool), k=1)
        scores = jnp.where(causal, -jnp.inf, scores)
        scores = (scores + _alibi_bias(t, scores.dtype)) / jnp.sqrt(jnp.asarray(DQ, scores.dtype))
        w = jax.nn.softmax(scores, axis=-1)
        ctx = jnp.einsum('bhqk,bhkd->bqhd', w, v).reshape(b, t, D_OUT)
        return ctx @ Wp + bp

    def _L0_xattn_ref(q, k, v, igate_kernel, igate_bias, fgate_kernel, fgate_bias, outnorm_weight):
        import jax, jax.numpy as jnp
        import numpy as np
        EPS = 1e-06
        LN_EPS = 1e-06

        def _mlstm_parallel_stabilized(q, k, v, igate_preact, fgate_preact):
            B, NH, S, DH = q.shape
            log_fg = jax.nn.log_sigmoid(fgate_preact[..., 0])
            cs = jnp.cumsum(log_fg, axis=-1)
            fg_mat = cs[..., :, None] - cs[..., None, :]
            mask = jnp.tril(jnp.ones((S, S), dtype=bool))
            log_D = jnp.where(mask, fg_mat + igate_preact[..., 0][..., None, :], -jnp.inf)
            max_log_D = jnp.max(log_D, axis=-1, keepdims=True)
            D = jnp.exp(log_D - max_log_D)
            k_scaled = k / jnp.sqrt(jnp.float32(DH)).astype(k.dtype)
            qk = jnp.einsum('bhsd,bhtd->bhst', q, k_scaled)
            C = qk * D
            normalizer = jnp.maximum(jnp.abs(jnp.sum(C, axis=-1, keepdims=True)), jnp.exp(-max_log_D))
            C_norm = C / (normalizer + EPS)
            return jnp.einsum('bhst,bhtd->bhsd', C_norm, v)

        def _multihead_layernorm(x, weight):
            mu = jnp.mean(x, axis=-1, keepdims=True)
            var = jnp.mean(jnp.square(x - mu), axis=-1, keepdims=True)
            xn = (x - mu) * jax.lax.rsqrt(var + LN_EPS)
            return xn * weight[None, :, None, :]
        B, S, E = q.shape
        NH = igate_bias.shape[0]
        qkv = jnp.concatenate([q, k, v], axis=-1)
        igate_preact = qkv @ igate_kernel + igate_bias
        fgate_preact = qkv @ fgate_kernel + fgate_bias
        qh = q.reshape(B, S, NH, -1).transpose(0, 2, 1, 3)
        kh = k.reshape(B, S, NH, -1).transpose(0, 2, 1, 3)
        vh = v.reshape(B, S, NH, -1).transpose(0, 2, 1, 3)
        ig = igate_preact.transpose(0, 2, 1)[..., None]
        fg = fgate_preact.transpose(0, 2, 1)[..., None]
        h = _mlstm_parallel_stabilized(qh, kh, vh, ig, fg)
        h_norm = _multihead_layernorm(h, outnorm_weight)
        return h_norm.transpose(0, 2, 1, 3).reshape(B, S, -1)

    def _L0_ffn_ref(x, ternary_weight, bias, act_scale):
        import jax, jax.numpy as jnp
        import numpy as np
        B, S, D_IN, D_OUT = (16, 512, 128, 128)
        ACT_BITS = 8
        QB = float(2 ** (ACT_BITS - 1) - 1)
        scale = jnp.maximum(act_scale, 1e-05)
        x_int = jnp.clip(jnp.round(x / scale), -QB, QB)
        x_dq = jnp.nan_to_num(x_int * scale, nan=0.0, posinf=10000.0, neginf=-10000.0)
        w = ternary_weight.astype(jnp.float32) - 1.0
        return jnp.einsum('bsi,oi->bso', x_dq, w) + bias

    def _L1_attn_ref(x, Wqkv_w, Wqkv_b, out_w, out_b):
        import jax, jax.numpy as jnp
        import numpy as np
        import math
        D_MODEL = 128
        NUM_HEADS = 16
        HEAD_DIM = D_MODEL // NUM_HEADS
        REPETITIONS = 3
        NEG = -10000.0

        def _self_attention(q, k, v, mask):
            scale = 1.0 / math.sqrt(q.shape[-1])
            scores = jnp.einsum('bthd,bshd->bhts', q, k * scale) + mask
            attn = jax.nn.softmax(scores, axis=-1)
            return jnp.einsum('bhts,bshd->bthd', attn, v)
        B, S, _ = x.shape
        qkv = x @ Wqkv_w.T + Wqkv_b
        qkv = qkv.reshape(B, S, 3, NUM_HEADS, HEAD_DIM)
        q, k, v = (qkv[:, :, 0], qkv[:, :, 1], qkv[:, :, 2])
        mask = jnp.triu(jnp.full((S, S), NEG, dtype=x.dtype), 1)
        context = _self_attention(q, k, v, mask)
        for _ in range(REPETITIONS - 1):
            context = _self_attention(context, k, v, mask)
        out = context.reshape(B, S, D_MODEL) @ out_w.T + out_b
        return out

    def _L1_xattn_ref(query, key, value, w_q, b_q, w_k, b_k, w_v, b_v, w_o, b_o):
        import jax, jax.numpy as jnp
        import numpy as np
        D_MODEL = 128
        NUM_HEADS = 16
        D_K = D_MODEL // NUM_HEADS
        B, N = (2, 256)
        Bq, Nq, _ = query.shape
        Q = (query @ w_q.T + b_q).reshape(Bq, Nq, NUM_HEADS, D_K).transpose(0, 2, 1, 3)
        K = (key @ w_k.T + b_k).reshape(Bq, -1, NUM_HEADS, D_K).transpose(0, 2, 1, 3)
        V = (value @ w_v.T + b_v).reshape(Bq, -1, NUM_HEADS, D_K).transpose(0, 2, 1, 3)
        scores = jnp.einsum('bhqd,bhkd->bhqk', Q, K) / np.sqrt(D_K).astype(np.float32)
        attn = jax.nn.softmax(scores, axis=-1)
        ctx = jnp.einsum('bhqk,bhkd->bhqd', attn, V)
        ctx = ctx.transpose(0, 2, 1, 3).reshape(Bq, Nq, D_MODEL)
        return ctx @ w_o.T + b_o

    def _L1_ffn_ref(x, Wg, W1, W2, W3):
        import jax, jax.numpy as jnp
        import numpy as np
        EMB_DIM = 128
        HIDDEN = int(2 / 3 * 4 * EMB_DIM)
        NUM_EXPERTS = 8
        TOP_K = 2
        B, S = (4, 128)
        gate_logits = jnp.einsum('bsd,ed->bse', x, Wg)
        top_v, top_i = jax.lax.top_k(gate_logits, TOP_K)
        mask = jnp.any(top_i[..., :, None] == jnp.arange(NUM_EXPERTS), axis=-2)
        sparse_logits = jnp.where(mask, gate_logits, -jnp.inf)
        gating = jax.nn.softmax(sparse_logits, axis=-1)
        h1 = jnp.einsum('bsd,ehd->bseh', x, W1)
        h2 = jnp.einsum('bsd,ehd->bseh', x, W2)
        hidden = jax.nn.silu(h1) * h2
        expert_out = jnp.einsum('bseh,edh->bsed', hidden, W3)
        return jnp.einsum('bsed,bse->bsd', expert_out, gating)
    x = _layernorm(x + _L0_attn_ref(x, L0_attn_Wq, L0_attn_Wk, L0_attn_Wv, L0_attn_Wp, L0_attn_bp), axis=-1)
    x = _layernorm(x + _L0_xattn_ref(x, ctx_1024, ctx_1024, L0_xattn_igate_kernel, L0_xattn_igate_bias, L0_xattn_fgate_kernel, L0_xattn_fgate_bias, L0_xattn_outnorm_weight), axis=-1)
    x = _layernorm(x + _L0_ffn_ref(x, L0_ffn_ternary_weight, L0_ffn_bias, L0_ffn_act_scale), axis=-1)
    x = _layernorm(x + _L1_attn_ref(x, L1_attn_Wqkv_w, L1_attn_Wqkv_b, L1_attn_out_w, L1_attn_out_b), axis=-1)
    x = _layernorm(x + _L1_xattn_ref(x, ctx_1024, ctx_1024, L1_xattn_w_q, L1_xattn_b_q, L1_xattn_w_k, L1_xattn_b_k, L1_xattn_w_v, L1_xattn_b_v, L1_xattn_w_o, L1_xattn_b_o), axis=-1)
    x = _layernorm(x + _L1_ffn_ref(x, L1_ffn_Wg, L1_ffn_W1, L1_ffn_W2, L1_ffn_W3), axis=-1)
    return x

_drawn_inputs = setup_inputs


def setup_inputs(seed=0):
    import zlib

    import numpy as np

    out = dict(_drawn_inputs(seed))
    spreads = {'L0_attn_bp': (0.0, 0.1),
     'L0_xattn_igate_kernel': (0.0, 0.1),
     'L0_xattn_fgate_kernel': (0.0, 0.1),
     'L0_xattn_outnorm_weight': (1.0, 0.2)}
    factors = {'L0_attn_Wq': 2.944,
     'L0_attn_Wk': 3.358,
     'L0_xattn_igate_bias': 36.969,
     'L1_xattn_b_k': 64.0}
    for name, (base, spread) in spreads.items():
        noise = np.random.default_rng([zlib.crc32(name.encode()), seed]).standard_normal(out[name].shape)
        drawn = base * np.exp(spread * noise) if base else spread * noise
        out[name] = jnp.asarray(drawn.astype(out[name].dtype))
    for name, factor in factors.items():
        out[name] = (out[name] * factor).astype(out[name].dtype)
    return out
```

```python
from contextlib import ExitStack

import concourse.bass as bass
from concourse import mybir

ALU = mybir.AluOpType
ACT = mybir.ActivationFunctionType
AX = mybir.AxisListType
F32 = mybir.dt.float32
BF16 = mybir.dt.bfloat16
U32 = mybir.dt.uint32

P = 128
SEQ = 64
TPC = 4
CW = TPC * P
NCH = 8
NT = NCH * TPC
HALVES = 2
DH = 8
LN_EPS = 1e-5
ROUND = 12582912.0
FMAX = 3.4028234663852886e38
NEXP = 8
HID = 341
HCS = [114, 114, 113]
HO = [0, 114, 228]

C_ID, C_MB, C_ONE, C_CUM, C_PV, C_SEL, C_DEL, C_RST, C_HALF, C_IOTA = 0, 128, 130, 162, 290, 418, 674, 682, 810, 842
C_N = 850
W_Q, W_CQ, W_K, W_CK, W_V, W_BV, W_O, W_BO, W_N = 0, 256, 512, 768, 896, 1024, 1152, 1408, 1536


def need(eng, sem, value):
    if isinstance(value, int) and value <= 0:
        return
    eng.wait_ge(sem, value)


def of_parity(c, u, each):
    return c * (each // 2) + (each - u * (each // 2))


def spread(ap, shape):
    return ap.broadcast_to(shape)


class Chain:

    def __init__(self, eng, sem):
        self.eng, self.sem, self.base, self.n = eng, sem, 0, 0

    def at(self, base):
        self.base, self.n = base, 0

    def link(self, ins):
        ins.then_inc(self.sem, 1)
        self.n += 1
        self.eng.wait_ge(self.sem, self.base + self.n)


def over_chunks(eng, chain, prep_len, body_len, prologue, body):
    if chain:
        chain.at(0)
    prologue()
    if chain:
        assert chain.n == prep_len, (chain.n, prep_len)
        chain.at(prep_len)
    body(0, 0, True)
    if chain:
        assert chain.n == body_len, (chain.n, body_len)
    with eng.Fori(0, (NCH - 2) // 2) as it:
        for u in range(2):
            c = it * 2 + (1 + u)
            if chain:
                chain.at(it * (2 * body_len) + ((1 + u) * body_len + prep_len))
            body(c, (1 + u) % 2, True)
    if chain:
        chain.at((NCH - 1) * body_len + prep_len)
    body(NCH - 1, (NCH - 1) % 2, False)


class Attn:

    def __init__(self, name, reps, scale, mask, kv_ctx, first):
        self.name, self.reps, self.scale, self.mask, self.kv_ctx, self.first = name, reps, scale, mask, kv_ctx, first
        self.phases = ["x"] + (["ctx"] if first else []) + ["k0", "k1", "v", "q0", "q1"]
        self.steps = reps * TPC
        self.plan = {i: [] for i in range(self.steps + 2)}
        if first:
            self.plan[0] = self.phases[:2]
            for i, ph in enumerate(self.phases[2:]):
                self.plan[i + 1] = [ph]
        else:
            for i, ph in enumerate(self.phases):
                self.plan[i] = [ph]

    def use(self, c, phase):
        before = c - 1 if not isinstance(c, int) else max(c - 1, 0)
        return c * len(self.phases) + before + self.phases.index(phase)

    def use_out(self, c):
        n = len(self.phases)
        if isinstance(c, int) and c == NCH - 1:
            return NCH * n + NCH - 1
        return (c + 2) * n + c


def decoder(nc, x_in, ctx_in, c32, c16, attn_w, ml_w, ffn_w, ffn_t, ffn_s, moe_g, moe_w1, moe_w2, moe_w3, out):
    x_t = x_in.rearrange("(n p) d -> p n d", p=P)
    ctx_t = ctx_in.rearrange("(n p) d -> p n d", p=P)
    out_t = out.rearrange("(n p) d -> p n d", p=P)
    with ExitStack() as stack:
        def sb(name, shape, dt=F32):
            return stack.enter_context(nc.sbuf_tensor(name, shape, dt))

        def sem(name):
            return stack.enter_context(nc.semaphore(name))

        cst = sb("cst", [P, C_N])
        cmask = sb("cmask", [P, 256], BF16)
        wts = [sb(f"wts{i}", [P, W_N]) for i in range(3)]
        mlw = sb("mlw", [P, 48 + 16 + P])
        ffw = sb("ffw", [P, P + 1])
        fft = sb("fft", [P, P], mybir.dt.int32)
        fftf = sb("fftf", [P, P])
        ffT = sb("ffT", [P, P])
        scl = sb("scl", [P, 4])
        mog = sb("mog", [P, NEXP])
        w3 = sb("w3", [HCS[0], 3 * NEXP * P])
        xres = sb("xres", [P, NT, P])
        ctxT = sb("ctxT", [P, NT * P])
        xs = sb("xs", [P, 2, CW])
        xT = sb("xT", [P, 2, CW])
        kd = sb("kd", [P, 2, HALVES, CW])
        q = sb("q", [P, 2, HALVES, CW])
        kbd = [sb(f"kbd{i}", [P, HALVES, 8, CW]) for i in range(2)]
        vbd = sb("vbd", [P, 2, TPC, 8, 32])
        vm = sb("vm", [P, 2, TPC, 4, 66])
        work = sb("work", [P, 8 * CW])
        abd = sb("abd", [P, 2, 2, 8, SEQ])
        tmp = sb("tmp", [P, CW])
        tmp2 = sb("tmp2", [P, CW])
        small = sb("small", [P, 16 * 64])
        stats = sb("stats", [P, TPC, 6])
        spare = sb("spare", [P, 2])
        mvs = sb("mvs", [P, TPC, 2])
        mv = sb("mv", [P, NT, 2])
        rstd = sb("rstd", [P, NT])
        gate = sb("gate", [P, NT, NEXP])

        psS = [stack.enter_context(nc.psum_tensor(f"psS{i}", [P, 2 * CW], F32)) for i in range(2)]
        psT = stack.enter_context(nc.psum_tensor("psT", [P, 2 * CW], F32))
        psV = stack.enter_context(nc.psum_tensor("psV", [P, CW], F32))
        psX = stack.enter_context(nc.psum_tensor("psX", [P, CW], F32))

        ident = cst[:, C_ID:C_ID + P]
        prob = [work[:, i * 2 * CW:(i + 1) * 2 * CW] for i in range(2)]
        probT = [work[:, (2 + i) * 2 * CW:(3 + i) * 2 * CW] for i in range(2)]

        def cols(a, n):
            return small[:, a:a + n]
        rmax = [cols(16 * i, 16) for i in range(2)]
        recip = cols(32, 256)
        lnv = cols(288, 8)

        w1v = kbd[0][:, :, :, :].rearrange("p a b c -> p (a b c)")[:, 0:NEXP * HID]
        w2v = kbd[1][:, :, :, :].rearrange("p a b c -> p (a b c)")[:, 0:NEXP * HID]
        ZEROED = 7

        pre = cols(320, 64).rearrange("p (t g) -> p t g", t=TPC)
        fabs = cols(384, 32).rearrange("p (t g) -> p t g", t=TPC)
        flog = cols(416, 32).rearrange("p (t g) -> p t g", t=TPC)
        lf = cols(448, 32).rearrange("p (t g) -> p t g", t=TPC)
        cum = cols(480, 32)
        agate = cols(512, 32)
        negM = [cols(544 + 32 * i, 32).rearrange("p (t g) -> p t g", t=TPC) for i in range(2)]
        enm = [cols(608 + 32 * i, 32).rearrange("p (t g) -> p t g", t=TPC) for i in range(2)]
        aT = tmp2[0:32, 0:P]
        MT = tmp2[0:32, P:2 * P]
        nrm = cols(672, 8)
        hmu = cols(680, 32)
        hvar = cols(712, 32)
        hrs = cols(744, 32)
        gl = cols(776, 32).rearrange("p (t g) -> p t g", t=TPC)
        g1 = cols(808, 32).rearrange("p (t g) -> p t g", t=TPC)
        g2 = cols(840, 32).rearrange("p (t g) -> p t g", t=TPC)
        g3 = cols(872, 32).rearrange("p (t g) -> p t g", t=TPC)
        gm = cols(904, 4)
        gn = cols(908, 4)

        def hid(par, p):
            return work[:, (3 * par + p) * CW:(3 * par + p + 1) * CW]

        def sil(par):
            return work[:, (6 + par) * CW:(7 + par) * CW]

        kvst = [kd[:, i, 0, :] for i in range(2)]
        ctx_st = [vm[:, i, :, :, :].rearrange("p t j k -> p (t j k)")[:, 0:CW] for i in range(2)]

        w_in = sem("w_in")
        zeroed = sem("zeroed")
        scaled = sem("scaled")
        tern_f, tern_T = sem("tern_f"), sem("tern_T")
        N_W = 16 * 11

        stages = [Attn("a0", 1, 0.5, 1, False, True),
                  Attn("a1", 3, 8 ** -0.5, 0, False, False),
                  Attn("a2", 1, 8 ** -0.5, None, True, False)]
        S = {}
        for st in stages:
            S[st.name] = {k: sem(f"{st.name}_{k}") for k in (
                "x_in0", "x_in1", "staged", "x_norm", "x_kept", "mix_full", "mix_free", "k_spread0", "k_spread1", "score", "shifted", "prob",
                "turned", "turned_out", "ctx_full", "ctx_done", "stat", "rstd", "dve")}
        M = {k: sem(f"m_{k}") for k in (
            "x_norm", "x_kept", "mix_full", "mix_free", "k_spread0", "k_spread1", "gate_abs", "gate_exp", "gate_ln", "gate_lf",
            "score", "decay", "prod", "turned", "turned_out", "ctx_full", "ctx_done", "nm", "enm", "a_up", "cum_up",
            "pow", "stat", "rstd", "dve", "var")}
        F = {k: sem(f"f_{k}") for k in (
            "x_norm", "x_kept", "x_turned", "quant", "out", "taken", "stat", "rstd", "dve")}
        G = {k: sem(f"g_{k}") for k in (
            "x_norm", "x_turned", "x_up", "logit", "logit_up", "shift", "exp", "w_in", "h1", "sil", "h2", "hid",
            "out", "taken", "var", "rstd", "dve", "normed", "stored", "fin")}

        block = stack.enter_context(nc.Block())

        def alone(dve):
            dve.memset(spare[:, 0:1], 0.0)

        @block.sync
        def _(sp):
            sp.dma_start(cst[:, :], c32).then_inc(w_in, 16)
            sp.dma_start(wts[0][:, :], attn_w[0]).then_inc(w_in, 16)
            for dst, src in ((cmask, c16), (wts[1], attn_w[1]), (wts[2], attn_w[2]), (mlw, ml_w), (ffw, ffn_w),
                             (fft, ffn_t), (mog, moe_g), (w3, moe_w3)):
                sp.dma_start(dst[:, :], src).then_inc(w_in, 16)
            sp.dma_start(scl[:, 0:1], ffn_s).then_inc(w_in, 16)

            raw = [vm[:, i, :, :, :].rearrange("p t j k -> p (t j k)")[:, 0:CW].rearrange("p (n d) -> p n d", n=TPC)
                   for i in range(2)]

            def keys(st, c, u):
                s = S[st.name]
                need(sp, s["score"], c * st.steps - st.steps)
                sp.wait_ge(s["mix_free"], st.use(c, "k1") + 1)
                for hh in range(8):
                    rows = slice(16 * hh, 16 * hh + 16)
                    sp.dma_start(kbd[u][rows, :, hh, :], kd[rows, u, :, :]).then_inc(s[f"k_spread{u}"], 16)

            def load(st, c, u):
                s = S[st.name]
                if not (isinstance(c, int) and c < 2):
                    sp.wait_ge(s["mix_full"], st.use(c - 2, "ctx") + 1)
                    sp.wait_ge(s["x_kept"], c * 2 - 2)
                sp.dma_start(xs[:, u, :].rearrange("p (n d) -> p n d", n=TPC),
                             x_t[:, bass.ts(c, TPC), :]).then_inc(s[f"x_in{u}"], 16)
                sp.dma_start(raw[u], ctx_t[:, bass.ts(c, TPC), :]).then_inc(s[f"x_in{u}"], 16)

            st = stages[0]
            load(st, 0, 0)
            load(st, 1, 1)
            sp.wait_ge(zeroed, ZEROED)
            keys(st, 0, 0)
            load(st, 2, 0)
            keys(st, 1, 1)
            with sp.Fori(0, (NCH - 4) // 2) as it:
                for u in range(2):
                    load(st, it * 2 + (3 + u), 1 - u)
                    keys(st, it * 2 + (2 + u), u)
            load(st, NCH - 1, 1)
            keys(st, NCH - 2, 0)
            keys(st, NCH - 1, 1)

            sp.wait_ge(S["a0"]["score"], stages[0].steps * NCH)

            def ml_keys(c, u):
                need(sp, M["score"], (c - 1) * TPC)
                for h in range(8):
                    rows = slice(16 * h, 16 * h + 16)
                    sp.dma_start(kbd[u][rows, 0, h, :], ctxT[rows, bass.ts(c, CW)]).then_inc(M[f"k_spread{u}"], 16)

            sp.wait_ge(S["a0"]["mix_free"], stages[0].use(NCH - 1, "ctx") + 1)
            over_chunks(sp, None, 0, 0, lambda: ml_keys(0, 0),
                        lambda c, u, more: ml_keys(c + 1, 1 - u) if more else None)
            for st, before, n in ((stages[1], M["score"], NCH * TPC), (stages[2], S["a1"]["score"], stages[1].steps * NCH)):
                sp.wait_ge(before, n)
                over_chunks(sp, None, 0, 0, lambda: keys(st, 0, 0),
                            lambda c, u, more: keys(st, c + 1, 1 - u) if more else None)
            sp.wait_ge(S["a2"]["score"], stages[2].steps * NCH)
            sp.dma_start(w1v, moe_w1).then_inc(G["w_in"], 16)
            sp.dma_start(w2v, moe_w2).then_inc(G["w_in"], 16)

            def store(c):
                sp.wait_ge(G["normed"], c + 1)
                sp.dma_start(out_t[:, bass.ts(c, TPC), :],
                             xres[:, bass.ts(c, TPC), :]).then_inc(G["stored"], 16)

            with sp.Fori(0, NCH) as c:
                store(c)
            sp.wait_ge(G["stored"], 16 * NCH)

        @block.gpsimd
        def _(g):
            for ap in (kbd[0][:, :, :, :], kbd[1][:, :, :, :], vbd[:, :, :, :, :], abd[:, :, :, :, :],
                       work[:, :], small[:, :], tmp2[:, :]):
                g.memset(ap, 0.0).then_inc(zeroed, 1)
            g.wait_ge(w_in, N_W)

            def rstd_of(c, stat, done):
                g.wait_ge(stat, c + 1)
                g.tensor_tensor(rstd[:, bass.ts(c, TPC)], mv[:, bass.ts(c, TPC), 1], cst[:, C_HALF:C_HALF + TPC],
                                ALU.pow).then_inc(done, 1)

            def keep(c, u, s, bias):
                g.wait_ge(s["x_norm"], c + 1)
                dst = xres[:, bass.ts(c, TPC), :]
                src = xs[:, u, :].rearrange("p (n d) -> p n d", n=TPC)
                if bias is None:
                    g.tensor_copy(dst, src).then_inc(s["x_kept"], 1)
                else:
                    g.tensor_tensor(dst, src, spread(bias.unsqueeze(1), [P, TPC, P]), ALU.add).then_inc(s["x_kept"], 1)

            def attention(st, wt):
                s = S[st.name]
                bias = wt[:, W_BO:W_BO + P]

                def prologue():
                    if st.first:
                        keep_first(0, 0)
                    else:
                        keep(0, 0, s, bias)

                def keep_first(c, u):
                    g.wait_ge(s[f"x_in{u}"], of_parity(c, u, 32))
                    g.tensor_tensor(xres[:, bass.ts(c, TPC), :], xs[:, u, :].rearrange("p (n d) -> p n d", n=TPC),
                                    spread(bias.unsqueeze(1), [P, TPC, P]), ALU.add).then_inc(s["x_kept"], 2)

                def body(c, u, more):
                    if more:
                        if st.first:
                            keep_first(c + 1, 1 - u)
                        else:
                            keep(c + 1, 1 - u, s, bias)
                    rstd_of(c, s["stat"], s["rstd"])

                over_chunks(g, None, 0, 0, prologue, body)

            attention(stages[0], wts[0])

            def ml_body(c, u, more):
                if more:
                    keep(c + 1, 1 - u, M, None)
                g.wait_ge(M["var"], c + 1)
                g.tensor_tensor(hrs, hvar, cst[:, C_HALF:C_HALF + 32], ALU.pow).then_inc(M["pow"], 1)
                rstd_of(c, M["stat"], M["rstd"])

            over_chunks(g, None, 0, 0, lambda: keep(0, 0, M, None), ml_body)

            def ff_body(c, u, more):
                if more:
                    keep(c + 1, 1 - u, F, ffw[:, 0:P])
                rstd_of(c, F["stat"], F["rstd"])

            over_chunks(g, None, 0, 0, lambda: keep(0, 0, F, ffw[:, 0:P]), ff_body)
            attention(stages[1], wts[1])
            attention(stages[2], wts[2])
            with g.Fori(0, NCH) as c:
                rstd_of(c, G["var"], G["rstd"])

        @block.tensor
        def _(pe):
            pe.wait_ge(w_in, N_W)
            pe.wait_ge(zeroed, ZEROED)
            pe.wait_ge(tern_f, 1)
            pe.transpose(psV[:, 0:P], fftf[:, :], ident).then_inc(tern_T, 1)
            pe.wait_ge(scaled, 6)

            def turn_chunk(u, src):
                for t in range(TPC):
                    mm = pe.transpose(psX[:, t * P:(t + 1) * P], src[:, t * P:(t + 1) * P], ident)
                return mm

            def values(src, wv):
                for t in range(TPC):
                    for h2 in range(2):
                        for b in range(2):
                            o = t * P + b * SEQ
                            mm = pe.matmul(psX[h2 * SEQ:(h2 + 1) * SEQ, o:o + SEQ], src[:, o:o + SEQ],
                                           wv[:, h2 * SEQ:(h2 + 1) * SEQ], start=True, stop=True)
                return mm

            def attention(st, wt, prev):
                s = S[st.name]

                def prepare(c, u, ph):
                    n = st.use(c, ph)
                    need(pe, s["mix_free"], n)
                    if ph == "x":
                        if st.first:
                            pe.wait_ge(s[f"x_in{u}"], of_parity(c, u, 32))
                        else:
                            pe.wait_ge(s["x_norm"], c + 1)
                        mm = turn_chunk(u, xs[:, u, :])
                    elif ph == "ctx":
                        mm = turn_chunk(u, vm[:, u, :, :, :].rearrange("p t j k -> p (t j k)"))
                    else:
                        pe.wait_ge(s["mix_free"], st.use(c, "x") + 1)
                        kv = ctxT[:, bass.ts(c, CW)] if st.kv_ctx else xT[:, u, :]
                        if ph[0] == "k":
                            w = W_K + P * int(ph[1])
                            mm = pe.matmul(psX[:, :], wt[:, w:w + P], kv, start=True, stop=True)
                        elif ph[0] == "q":
                            w = W_Q + P * int(ph[1])
                            mm = pe.matmul(psX[:, :], wt[:, w:w + P], xT[:, u, :], start=True, stop=True)
                        else:
                            if st.kv_ctx:
                                pe.wait_ge(s["staged"], c + 1)
                            mm = values(ctx_st[u] if st.kv_ctx else xT[:, u, :], wt[:, W_V:W_V + P])
                    mm.then_inc(s["mix_full"], 1)

                def score(c, u, i):
                    n = c * st.steps + i
                    r, t = divmod(i, TPC)
                    if not (isinstance(c, int) and c == 0 and i < 2):
                        pe.wait_ge(s["shifted"], n - 1)
                    if r:
                        pe.wait_ge(s["ctx_done"], n - TPC + 1)
                    if i == 0:
                        pe.wait_ge(s["mix_free"], st.use(c, "q1") + 1)
                        pe.wait_ge(s[f"k_spread{u}"], of_parity(c, u, 128))
                    bank = psS[i % 2]
                    if st.mask is not None:
                        m = cmask[:, P + SEQ * st.mask:P + SEQ * (st.mask + 1)]
                        for h in range(HALVES):
                            pe.matmul(bank[:, h * CW:(h + 1) * CW].rearrange("p (a k) -> p a k", a=8), cmask[:, 0:P],
                                      spread(m.unsqueeze(1), [P, 8, SEQ]), start=True, stop=False,
                                      skip_group_check=True)
                    for h in range(HALVES):
                        for b in range(2):
                            o = t * P + b * SEQ
                            mm = pe.matmul(bank[b * SEQ:(b + 1) * SEQ, h * CW:(h + 1) * CW].rearrange("p (a k) -> p a k", a=8),
                                           q[:, u, h, o:o + SEQ], kbd[u][:, h, :, o:o + SEQ],
                                           start=st.mask is None, stop=True, skip_group_check=True)
                    mm.then_inc(s["score"], 1)

                def turn(c, i):
                    n = c * st.steps + i
                    pe.wait_ge(s["prob"], n + 1)
                    need(pe, s["turned_out"], n)
                    for j in range(8):
                        mm = pe.transpose(psT[:, j * P:(j + 1) * P], prob[i % 2][:, j * P:(j + 1) * P], ident)
                    mm.then_inc(s["turned"], 1)

                def mix(c, u, i):
                    n = c * st.steps + i
                    t = i % TPC
                    pe.wait_ge(s["turned_out"], n + 1)
                    need(pe, s["ctx_done"], n)
                    for j in range(8):
                        rows = slice(32 * (j % 4), 32 * (j % 4) + 32)
                        o = (j // 4) * P
                        pt = probT[i % 2][:, j * P:(j + 1) * P]
                        pe.matmul(psV[rows, o:o + P], vbd[:, u, t, j, :], pt, start=True, stop=True, tile_position=(0, 32 * (j % 4)))
                        mm = pe.matmul(psV[rows, 256 + o:256 + o + P], cst[:, C_ONE:C_ONE + 32], pt,
                                       start=True, stop=True, tile_position=(0, 32 * (j % 4)))
                    mm.then_inc(s["ctx_full"], 1)

                def body(c, u, more):
                    for i in range(st.steps + 2):
                        if more:
                            for ph in st.plan[i]:
                                prepare(c + 1, 1 - u, ph)
                        if i < st.steps:
                            score(c, u, i)
                        if 1 <= i <= st.steps:
                            turn(c, i - 1)
                        if i >= 2:
                            mix(c, u, i - 2)
                    n = st.use_out(c)
                    pe.wait_ge(s["mix_free"], n)
                    pe.wait_ge(s["ctx_done"], (c + 1) * st.steps)
                    for t in range(TPC):
                        for h in range(HALVES):
                            mm = pe.matmul(psX[:, t * P:(t + 1) * P], q[:, u, h, t * P:(t + 1) * P],
                                           wt[:, W_O + h * P:W_O + (h + 1) * P], start=h == 0, stop=h == 1)
                    mm.then_inc(s["mix_full"], 1)

                def prologue():
                    for ph in st.phases:
                        prepare(0, 0, ph)

                over_chunks(pe, None, 0, 0, prologue, body)

            attention(stages[0], wts[0], None)

            NP_ = 6
            MP = ["x", "v", "pre", "cum", "a", "m"]

            def ml_prepare(c, u, ph):
                n = c * NP_ + MP.index(ph)
                need(pe, M["mix_free"], n)
                if ph == "x":
                    pe.wait_ge(M["x_norm"], c + 1)
                    mm = turn_chunk(u, xs[:, u, :])
                elif ph == "v":
                    pe.wait_ge(M["a_up"], c + 1)
                    mm = values(kvst[u], cst[:, C_PV:C_PV + P])
                elif ph == "pre":
                    for t in range(TPC):
                        o = psX[:, t * 16:(t + 1) * 16]
                        pe.matmul(o, xT[:, u, t * P:(t + 1) * P], mlw[:, 0:16], start=True, stop=False)
                        pe.matmul(o, kvst[u][:, t * P:(t + 1) * P], mlw[:, 16:32], start=False, stop=False)
                        mm = pe.matmul(o, kvst[u][:, t * P:(t + 1) * P], mlw[:, 32:48], start=False, stop=True)
                elif ph == "cum":
                    pe.wait_ge(M["gate_lf"], c + 1)
                    mm = pe.matmul(psX[:, 0:32], cst[:, C_CUM:C_CUM + P], lf.rearrange("p t g -> p (t g)"), start=True, stop=True)
                elif ph == "a":
                    mm = pe.transpose(psX[0:32, 0:P], agate, ident)
                else:
                    mm = pe.transpose(psX[:, 0:P], tmp2[:, P:2 * P], ident)
                mm.then_inc(M["mix_full"], 1)

            def ml_score(c, u, t):
                n = c * TPC + t
                if not (isinstance(c, int) and c == 0 and t < 2):
                    pe.wait_ge(M["prod"], n - 1)
                if t == 0:
                    pe.wait_ge(M["mix_free"], (c + 1) * NP_)
                    pe.wait_ge(M[f"k_spread{u}"], of_parity(c, u, 128))
                bank = psS[t % 2]
                qk = bank[:, 0:CW]
                dec = bank[:, CW:2 * CW].rearrange("p (a k) -> p a k", a=8)
                m = cmask[:, P + SEQ:P + 2 * SEQ]
                pe.matmul(dec, cmask[:, 0:P], spread(m.unsqueeze(1), [P, 8, SEQ]), start=True, stop=False, skip_group_check=True)
                for b in range(2):
                    pe.matmul(bank[b * SEQ:(b + 1) * SEQ, CW:2 * CW].rearrange("p (a k) -> p a k", a=8),
                              cst[:, C_SEL + t * SEQ:C_SEL + (t + 1) * SEQ], abd[:, u, b, :, :], start=False, stop=False,
                              skip_group_check=True)
                pe.matmul(dec, ident, spread(negM[u][:, t, :].unsqueeze(2), [P, 8, SEQ]), start=False, stop=True,
                          skip_group_check=True)
                for b in range(2):
                    o = t * P + b * SEQ
                    mm = pe.matmul(bank[b * SEQ:(b + 1) * SEQ, 0:CW].rearrange("p (a k) -> p a k", a=8),
                                   xT[:, u, o:o + SEQ], kbd[u][:, 0, :, o:o + SEQ], start=True, stop=True,
                                   skip_group_check=True)
                mm.then_inc(M["score"], 1)

            def ml_turn(c, t):
                n = c * TPC + t
                pe.wait_ge(M["prod"], n + 1)
                need(pe, M["turned_out"], n)
                for j in range(4):
                    mm = pe.transpose(psT[:, j * P:(j + 1) * P], prob[t % 2][:, j * P:(j + 1) * P], ident)
                mm.then_inc(M["turned"], 1)

            def ml_mix(c, u, t):
                n = c * TPC + t
                pe.wait_ge(M["turned_out"], n + 1)
                need(pe, M["ctx_done"], n)
                for j in range(4):
                    mm = pe.matmul(psV[:, j * 66:(j + 1) * 66], probT[t % 2][:, j * P:(j + 1) * P], vm[:, u, t, j, :],
                                   start=True, stop=True)
                mm.then_inc(M["ctx_full"], 1)

            def ml_body(c, u, more):
                for i in range(TPC + 2):
                    if more:
                        ml_prepare(c + 1, 1 - u, MP[i])
                    if i < TPC:
                        ml_score(c, u, i)
                    if 1 <= i <= TPC:
                        ml_turn(c, i - 1)
                    if i >= 2:
                        ml_mix(c, u, i - 2)

            over_chunks(pe, None, 0, 0, lambda: [ml_prepare(0, 0, ph) for ph in MP], ml_body)

            def ff_turn(c, u):
                pe.wait_ge(F["x_norm"], c + 1)
                if not (isinstance(c, int) and c < 2):
                    pe.wait_ge(F["quant"], c - 1)
                for t in range(TPC):
                    mm = pe.transpose(psS[u][:, t * P:(t + 1) * P], xs[:, u, t * P:(t + 1) * P], ident)
                mm.then_inc(F["x_turned"], 1)

            def ff_body(c, u, more):
                if more:
                    ff_turn(c + 1, 1 - u)
                pe.wait_ge(F["quant"], c + 1)
                need(pe, F["taken"], c)
                for t in range(TPC):
                    mm = pe.matmul(psV[:, t * P:(t + 1) * P], xT[:, u, t * P:(t + 1) * P], ffT[:, :], start=True, stop=True)
                mm.then_inc(F["out"], 1)

            over_chunks(pe, None, 0, 0, lambda: ff_turn(0, 0), ff_body)
            attention(stages[1], wts[1], None)
            attention(stages[2], wts[2], None)

            def g_turn(c, u):
                pe.wait_ge(G["x_norm"], c + 1)
                if not (isinstance(c, int) and c < 2):
                    pe.wait_ge(G["x_up"], (c - 1) * 2)
                for t in range(TPC):
                    mm = pe.transpose(psS[u][:, t * P:(t + 1) * P], xs[:, u, t * P:(t + 1) * P], ident)
                mm.then_inc(G["x_turned"], 1)

            def g_body(c, u, more):
                if more:
                    g_turn(c + 1, 1 - u)
                pe.wait_ge(G["x_up"], (c + 1) * 2)
                need(pe, G["logit_up"], c)
                for t in range(TPC):
                    mm = pe.matmul(psX[:, t * NEXP:(t + 1) * NEXP], xT[:, u, t * P:(t + 1) * P], mog[:, :], start=True, stop=True)
                mm.then_inc(G["logit"], 1)

            over_chunks(pe, None, 0, 0, lambda: g_turn(0, 0), g_body)

            NU = NEXP * 3
            pe.wait_ge(G["w_in"], 32)

            def hidden(c, k, first):
                e, p = divmod(k, 3)
                n = c * NU + k
                m = HCS[p]
                if not (first and k < 2):
                    pe.wait_ge(G["hid"], n - 1)
                w = e * HID + HO[p]
                rhs = ctxT[:, bass.ts(c, CW)]
                pe.matmul(psS[k % 2][0:m, 0:CW], w1v[:, w:w + m], rhs, start=True, stop=True).then_inc(G["h1"], 1)
                pe.matmul(psS[k % 2][0:m, CW:2 * CW], w2v[:, w:w + m], rhs, start=True, stop=True).then_inc(G["h2"], 1)

            def down(c, e, first):
                n = c * NEXP + e
                pe.wait_ge(G["hid"], c * NU + 3 * e + 3)
                if not (first and e < 2):
                    pe.wait_ge(G["taken"], n - 1)
                for t in range(TPC):
                    for p in range(3):
                        m = HCS[p]
                        mm = pe.matmul(psT[:, (e % 2) * CW + t * P:(e % 2) * CW + (t + 1) * P],
                                       hid(e % 2, p)[0:m, t * P:(t + 1) * P], w3[0:m, (e * 3 + p) * P:(e * 3 + p + 1) * P],
                                       start=p == 0, stop=p == 2)
                mm.then_inc(G["out"], 1)

            def expert_chunk(c, first):
                for k in range(NU):
                    hidden(c, k, first)
                    if k >= 3 and k % 3 == 0:
                        down(c, k // 3 - 1, first)
                down(c, NEXP - 1, first)

            expert_chunk(0, True)
            with pe.Fori(1, NCH) as c:
                expert_chunk(c, False)

        @block.scalar
        def _(act):
            def attention(st):
                s = S[st.name]

                def prepare(c, u, ph):
                    if ph not in ("x", "ctx"):
                        return
                    act.wait_ge(s["mix_full"], st.use(c, ph) + 1)
                    if ph == "x":
                        if st.kv_ctx:
                            act.copy(ctx_st[u], ctxT[:, bass.ts(c, CW)]).then_inc(s["staged"], 1)
                        dst = xT[:, u, :]
                    else:
                        dst = ctxT[:, bass.ts(c, CW)]
                    act.copy(dst, psX[:, :]).then_inc(s["mix_free"], 1)

                def exps(c, i):
                    n = c * st.steps + i
                    act.wait_ge(s["shifted"], n + 1)
                    act.activation(prob[i % 2], prob[i % 2], ACT.Exp).then_inc(s["prob"], 1)

                def turned(c, i):
                    n = c * st.steps + i
                    act.wait_ge(s["turned"], n + 1)
                    if not (isinstance(c, int) and c == 0 and i < 2):
                        act.wait_ge(s["ctx_full"], n - 1)
                    act.copy(probT[i % 2], psT[:, :]).then_inc(s["turned_out"], 1)

                def body(c, u, more):
                    for i in range(st.steps + 2):
                        if more:
                            for ph in st.plan[i]:
                                prepare(c + 1, 1 - u, ph)
                        if 1 <= i <= st.steps:
                            turned(c, i - 1)
                        if i < st.steps:
                            exps(c, i)

                over_chunks(act, None, 0, 0, lambda: [prepare(0, 0, ph) for ph in st.phases], body)

            act.wait_ge(zeroed, ZEROED)
            attention(stages[0])

            NP_ = 6
            MP = ["x", "v", "pre", "cum", "a", "m"]

            def ml_prepare(c, u, ph):
                n = c * NP_ + MP.index(ph)
                if ph == "x":
                    act.wait_ge(M["mix_full"], n + 1)
                    act.copy(kvst[u], ctxT[:, bass.ts(c, CW)]).then_inc(M["a_up"], 1)
                    act.copy(xT[:, u, :], psX[:, :]).then_inc(M["mix_free"], 1)
                elif ph == "pre":
                    act.wait_ge(M["gate_abs"], c + 1)
                    act.activation(flog, fabs, ACT.Exp).then_inc(M["gate_exp"], 1)
                    act.wait_ge(M["gate_exp"], c + 1)
                    act.activation(flog, flog, ACT.Ln, bias=1.0).then_inc(M["gate_ln"], 1)
                elif ph == "m":
                    act.wait_ge(M["nm"], c + 1)
                    act.activation(enm[u], enm[u], ACT.Exp).then_inc(M["enm"], 1)

            def ml_body(c, u, more):
                for i in range(TPC + 2):
                    if more:
                        ml_prepare(c + 1, 1 - u, MP[i])
                    if 1 <= i <= TPC:
                        n = c * TPC + i - 1
                        act.wait_ge(M["turned"], n + 1)
                        if not (isinstance(c, int) and c == 0 and i < 3):
                            act.wait_ge(M["ctx_full"], n - 1)
                        act.copy(probT[(i - 1) % 2][:, 0:CW], psT[:, 0:CW]).then_inc(M["turned_out"], 1)
                    if i < TPC:
                        n = c * TPC + i
                        act.wait_ge(M["score"], n + 1)
                        if not (isinstance(c, int) and c == 0 and i < 2):
                            act.wait_ge(M["turned"], n - 1)
                        act.activation(prob[i % 2][:, 0:CW], psS[i % 2][:, CW:2 * CW], ACT.Exp).then_inc(M["decay"], 1)

            for u in range(2):
                act.wait_ge(S["a0"][f"k_spread{u}"], 128 * NCH // 2)
            over_chunks(act, None, 0, 0, lambda: [ml_prepare(0, 0, ph) for ph in MP], ml_body)
            attention(stages[1])
            attention(stages[2])

            def g_body(c, u):
                act.wait_ge(G["x_turned"], c + 1)
                act.copy(xT[:, u, :], psS[u][:, 0:CW]).then_inc(G["x_up"], 1)
                act.copy(ctxT[:, bass.ts(c, CW)], psS[u][:, 0:CW]).then_inc(G["x_up"], 1)

            def g_exp(c):
                act.wait_ge(G["shift"], c + 1)
                act.activation(gate[:, bass.ts(c, TPC), :], gate[:, bass.ts(c, TPC), :], ACT.Exp).then_inc(G["exp"], 1)

            g_body(0, 0)
            with act.Fori(0, 3) as it:
                for u in range(2):
                    g_body(it * 2 + (1 + u), (1 + u) % 2)
                    g_exp(it * 2 + u)
            g_body(7, 1)
            g_exp(6)
            g_exp(7)
            NU = NEXP * 3

            def sils(c, first):
                for k in range(NU):
                    n = c * NU + k
                    m = HCS[k % 3]
                    act.wait_ge(G["h1"], n + 1)
                    if not (first and k < 2):
                        act.wait_ge(G["hid"], n - 1)
                    act.activation(sil(k % 2)[0:m, :], psS[k % 2][0:m, 0:CW], ACT.Silu).then_inc(G["sil"], 1)

            sils(0, True)
            with act.Fori(1, NCH) as c:
                sils(c, False)

        @block.vector
        def _(dve):
            dve.wait_ge(w_in, N_W)
            for i, st in enumerate(stages):
                dve.tensor_scalar(wts[i][:, W_K:W_V], wts[i][:, W_K:W_V], st.scale, None, ALU.mult).then_inc(scaled, 1)
            dve.tensor_scalar(fftf[:, :], fft[:, :], -1.0, None, ALU.add).then_inc(tern_f, 1)
            dve.tensor_scalar(scl[:, 1:2], scl[:, 0:1], 1e-5, None, ALU.max).then_inc(scaled, 1)
            dve.wait_ge(scaled, 4)
            dve.reciprocal(scl[:, 2:3], scl[:, 1:2]).then_inc(scaled, 1)
            dve.wait_ge(tern_T, 1)
            dve.tensor_copy(ffT[:, :], psV[:, 0:P]).then_inc(scaled, 1)
            dve.wait_ge(zeroed, ZEROED)

            def normalise(c, u, s, prev):
                dve.wait_ge(prev, c + 1)
                if not (isinstance(c, int) and c < 2):
                    dve.wait_ge(s["x_kept"], c - 1)
                for t in range(TPC):
                    n = c * TPC + t
                    ins = dve.tensor_scalar(xs[:, u, t * P:(t + 1) * P], xres[:, n, :], mv[:, n, 0:1],
                                            rstd[:, bass.ts(n, 1)], ALU.subtract, ALU.mult)
                ins.then_inc(s["x_norm"], 1)

            def moments(chain, c, done):
                alone(dve)
                for t in range(TPC):
                    ins = dve.bn_stats(stats[:, t, :], xres[:, c * TPC + t, :])
                chain.link(ins)
                alone(dve)
                for t in range(TPC):
                    ins = dve.bn_aggr(mvs[:, t, :], stats[:, t, :])
                chain.link(ins)
                dve.tensor_scalar(mv[:, bass.ts(c, TPC), 0], mvs[:, :, 0], 0.0, None, ALU.add)
                dve.tensor_scalar(mv[:, bass.ts(c, TPC), 1], mvs[:, :, 1], LN_EPS, None, ALU.add).then_inc(done, 1)

            def values_out(u, wv, s):
                src = psX[:, :].rearrange("p (t b j d) -> p t b j d", t=TPC, b=2, j=8)
                for h2 in range(2):
                    rows = slice(h2 * SEQ, (h2 + 1) * SEQ)
                    for b in range(2):
                        o = h2 * 16 + b * 8
                        bv = wv[rows, h2 * SEQ:(h2 + 1) * SEQ].rearrange("p (j d) -> p j d", j=8)
                        ins = dve.tensor_tensor(vbd[rows, u, :, :, o:o + 8], src[rows, :, b, :, :],
                                                spread(bv.unsqueeze(1), [SEQ, TPC, 8, DH]), ALU.add)
                ins.then_inc(s["mix_free"], 1)

            def attention(st, wt, prev):
                s = S[st.name]
                chain = Chain(dve, s["dve"])

                def prepare(c, u, ph):
                    if ph == "x":
                        if not st.first:
                            normalise(c, u, s, prev)
                        return
                    if ph == "ctx":
                        return
                    dve.wait_ge(s["mix_full"], st.use(c, ph) + 1)
                    if ph[0] == "k":
                        h = int(ph[1])
                        if h == 0 and not (isinstance(c, int) and c < 2):
                            dve.wait_ge(s[f"k_spread{u}"], of_parity(c - 2, u, 128))
                        ck = wt[:, W_CK + h * SEQ:W_CK + (h + 1) * SEQ]
                        dve.tensor_tensor(kd[:, u, h, :].rearrange("p (b k) -> p b k", b=8),
                                          psX[:, :].rearrange("p (b k) -> p b k", b=8),
                                          spread(ck.unsqueeze(1), [P, 8, SEQ]), ALU.add).then_inc(s["mix_free"], 1)
                    elif ph[0] == "q":
                        h = int(ph[1])
                        for b in range(2):
                            o = W_CQ + (h * 2 + b) * SEQ
                            cq = wt[:, o:o + SEQ]
                            ins = dve.scalar_tensor_tensor(
                                q[:, u, h, :].rearrange("p (t b k) -> p t b k", t=TPC, b=2)[:, :, b, :],
                                psX[:, :].rearrange("p (t b k) -> p t b k", t=TPC, b=2)[:, :, b, :],
                                cst[:, C_MB + b:C_MB + b + 1], spread(cq.unsqueeze(1), [P, TPC, SEQ]), ALU.mult, ALU.add)
                        ins.then_inc(s["mix_free"], 1)
                    else:
                        values_out(u, wt[:, W_BV:W_BV + P], s)

                def shift(c, i):
                    n = c * st.steps + i
                    sc = psS[i % 2][:, :].rearrange("p (h k) -> p h k", h=16)
                    dve.wait_ge(s["score"], n + 1)
                    chain.link(dve.tensor_reduce(rmax[i % 2], sc, AX.X, ALU.max))
                    if not (isinstance(c, int) and c == 0 and i < 2):
                        dve.wait_ge(s["turned"], n - 1)
                    dve.tensor_tensor(prob[i % 2].rearrange("p (h k) -> p h k", h=16), sc,
                                      spread(rmax[i % 2].unsqueeze(2), [P, 16, SEQ]), ALU.subtract).then_inc(s["shifted"], 1)

                def context(c, u, i):
                    n = c * st.steps + i
                    t = i % TPC
                    dve.wait_ge(s["ctx_full"], n + 1)
                    chain.link(dve.reciprocal(recip, psV[:, 256:512]))
                    for b in range(2):
                        o = t * P + b * SEQ
                        ins = dve.scalar_tensor_tensor(
                            q[:, u, :, o:o + SEQ], psV[:, 0:256].rearrange("p (h k) -> p h k", h=2)[:, :, b * SEQ:(b + 1) * SEQ],
                            cst[:, C_MB + b:C_MB + b + 1],
                            recip.rearrange("p (h k) -> p h k", h=2)[:, :, b * SEQ:(b + 1) * SEQ], ALU.mult, ALU.mult)
                    ins.then_inc(s["ctx_done"], 1)

                def body(c, u, more):
                    for i in range(st.steps + 2):
                        if more:
                            for ph in st.plan[i]:
                                prepare(c + 1, 1 - u, ph)
                        if i < st.steps:
                            shift(c, i)
                        if i >= 2:
                            context(c, u, i - 2)
                    dve.wait_ge(s["x_kept"], c * 2 + 2 if st.first else c + 1)
                    dve.wait_ge(s["mix_full"], st.use_out(c) + 1)
                    ins = dve.tensor_tensor(xres[:, bass.ts(c, TPC), :], psX[:, :].rearrange("p (n d) -> p n d", n=TPC),
                                            xres[:, bass.ts(c, TPC), :], ALU.add)
                    ins.then_inc(s["mix_free"], 1)
                    dve.wait_ge(s["mix_free"], st.use_out(c) + 1)
                    moments(chain, c, s["stat"])

                over_chunks(dve, chain, 0, 2 * st.steps + 2, lambda: [prepare(0, 0, ph) for ph in st.phases], body)

            attention(stages[0], wts[0], None)

            NP_ = 6
            MP = ["x", "v", "pre", "cum", "a", "m"]
            chain = Chain(dve, M["dve"])
            dve.wait_ge(S["a0"]["mix_full"], stages[0].use(NCH - 1, "ctx") + 1)
            dve.memset(vm[:, :, :, :, :], 0.0).then_inc(M["cum_up"], 1)
            dve.wait_ge(M["cum_up"], 1)
            for h2 in range(2):
                dve.memset(vm[h2 * SEQ:(h2 + 1) * SEQ, :, :, :, 64 + h2], 1.0)

            def ml_prepare(c, u, ph):
                n = c * NP_ + MP.index(ph)
                if ph == "x":
                    normalise(c, u, M, S["a0"]["rstd"])
                    return
                dve.wait_ge(M["mix_full"], n + 1)
                if ph == "v":
                    src = psX[:, :].rearrange("p (t b j d) -> p t b j d", t=TPC, b=2, j=4)
                    for h2 in range(2):
                        rows = slice(h2 * SEQ, (h2 + 1) * SEQ)
                        for b in range(2):
                            o = h2 * 32 + b * 16
                            ins = dve.tensor_copy(vm[rows, u, :, :, o:o + 16], src[rows, :, b, :, :])
                    ins.then_inc(M["mix_free"], 1)
                elif ph == "pre":
                    dve.tensor_tensor(pre, psX[:, 0:64].rearrange("p (t g) -> p t g", t=TPC),
                                      spread(mlw[:, 48:64].unsqueeze(1), [P, TPC, 16]), ALU.add).then_inc(M["mix_free"], 1)
                    dve.wait_ge(M["mix_free"], n + 1)
                    dve.scalar_tensor_tensor(fabs, pre[:, :, 8:16], -1.0, pre[:, :, 8:16], ALU.mult, ALU.min).then_inc(M["gate_abs"], 1)
                    dve.wait_ge(M["gate_ln"], c + 1)
                    dve.scalar_tensor_tensor(lf, pre[:, :, 8:16], 0.0, flog, ALU.min, ALU.subtract).then_inc(M["gate_lf"], 1)
                elif ph == "cum":
                    chain.link(dve.tensor_copy(cum, psX[:, 0:32]))
                    dve.tensor_tensor(agate.rearrange("p (t g) -> p t g", t=TPC), pre[:, :, 0:8],
                                      cum.rearrange("p (t g) -> p t g", t=TPC), ALU.subtract).then_inc(M["mix_free"], 1)
                elif ph == "a":
                    chain.link(dve.tensor_copy(aT, psX[0:32, 0:P]))
                    chain.link(dve.tensor_tensor_scan(MT, cst[0:32, C_RST:C_RST + P], aT, 0.0, ALU.add, ALU.max))
                    a4 = aT.rearrange("p (b k) -> p b k", b=2).unsqueeze(2)
                    d4 = cst[0:32, C_DEL:C_DEL + 8].unsqueeze(1).unsqueeze(3)
                    dve.tensor_tensor(abd[0:32, u, :, :, :], spread(a4, [32, 2, 8, SEQ]), spread(d4, [32, 2, 8, SEQ]),
                                      ALU.mult).then_inc(M["mix_free"], 1)
                else:
                    dve.tensor_scalar(negM[u], psX[:, 0:32].rearrange("p (t g) -> p t g", t=TPC), -1.0, None,
                                      ALU.mult).then_inc(M["mix_free"], 1)
                    dve.wait_ge(M["mix_free"], n + 1)
                    dve.tensor_tensor(enm[u], negM[u], cum.rearrange("p (t g) -> p t g", t=TPC), ALU.subtract)\
                       .then_inc(M["nm"], 1)

            hb = tmp[:, :].rearrange("p (t h d) -> p t h d", t=TPC, h=8)
            hb3 = tmp[:, :].rearrange("p (g d) -> p g d", g=32)
            sq3 = tmp2[:, :].rearrange("p (g d) -> p g d", g=32)
            head = lambda a: spread(a.unsqueeze(2), [P, 32, 16])

            def ml_ctx(c, u, t):
                n = c * TPC + t
                dve.wait_ge(M["ctx_full"], n + 1)
                pv = psV[:, 0:264].rearrange("p (j k) -> p j k", j=4)
                nr = nrm.rearrange("p (j k) -> p j k", j=4)
                if t == 0:
                    dve.wait_ge(M["enm"], c + 1)
                en = enm[u][:, t, :].rearrange("p (j k) -> p j k", j=4)
                chain.link(dve.scalar_tensor_tensor(nr, pv[:, :, 64:66], -1.0, en, ALU.mult, ALU.max))
                chain.link(dve.tensor_tensor(nr, pv[:, :, 64:66], nr, ALU.max))
                chain.link(dve.tensor_scalar(nrm, nrm, 1e-6, None, ALU.add))
                chain.link(dve.reciprocal(nrm, nrm))
                for b in range(2):
                    rows = slice(b * SEQ, (b + 1) * SEQ)
                    src = pv[rows, :, 0:64].rearrange("p j (h b d) -> p j h b d", h=2, b=2)[:, :, :, b, :]
                    rec = nrm[rows, :].rearrange("p (j h) -> p j h", j=4).unsqueeze(3)
                    ins = dve.tensor_tensor(hb[rows, t, :, :].rearrange("p (j h) d -> p j h d", j=4), src,
                                            spread(rec, [SEQ, 4, 2, 16]), ALU.mult)
                ins.then_inc(M["ctx_done"], 1)

            def ml_body(c, u, more):
                for i in range(TPC + 2):
                    if more:
                        ml_prepare(c + 1, 1 - u, MP[i])
                    if i < TPC:
                        n = c * TPC + i
                        dve.wait_ge(M["decay"], n + 1)
                        dve.scalar_tensor_tensor(prob[i % 2][:, 0:CW], psS[i % 2][:, 0:CW], 0.25, prob[i % 2][:, 0:CW],
                                                 ALU.mult, ALU.mult).then_inc(M["prod"], 1)
                    if i >= 2:
                        ml_ctx(c, u, i - 2)
                dve.wait_ge(M["ctx_done"], (c + 1) * TPC)
                chain.link(dve.tensor_reduce(hmu, hb3, AX.X, ALU.add))
                chain.link(dve.tensor_scalar(hmu, hmu, 1.0 / 16, None, ALU.mult))
                chain.link(dve.tensor_tensor(hb3, hb3, head(hmu), ALU.subtract))
                chain.link(dve.tensor_tensor(sq3, hb3, hb3, ALU.mult))
                chain.link(dve.tensor_reduce(hvar, sq3, AX.X, ALU.add))
                dve.tensor_scalar(hvar, hvar, 1.0 / 16, 1e-6, ALU.mult, ALU.add).then_inc(M["var"], 1)
                dve.wait_ge(M["pow"], c + 1)
                chain.link(dve.tensor_tensor(hb3, hb3, head(hrs), ALU.mult))
                w3d = spread(mlw[:, 64:64 + P].unsqueeze(1), [P, TPC, P])
                h3 = tmp[:, :].rearrange("p (t d) -> p t d", t=TPC)
                chain.link(dve.tensor_tensor(h3, h3, w3d, ALU.mult))
                dve.wait_ge(M["x_kept"], c + 1)
                chain.link(dve.tensor_tensor(xres[:, bass.ts(c, TPC), :], h3, xres[:, bass.ts(c, TPC), :], ALU.add))
                moments(chain, c, M["stat"])

            prep_links = 3
            over_chunks(dve, chain, prep_links, prep_links + 4 * TPC + 8 + 2,
                        lambda: [ml_prepare(0, 0, ph) for ph in MP], ml_body)

            chain = Chain(dve, F["dve"])

            def ff_prepare(c, u):
                normalise(c, u, F, M["rstd"])
                dve.wait_ge(F["x_turned"], c + 1)
                qn, sat = tmp[:, :], tmp2[:, :]
                chain.link(dve.tensor_scalar(qn, psS[u][:, 0:CW], scl[:, 2:3], ROUND, ALU.mult, ALU.add))
                chain.link(dve.tensor_scalar(qn, qn, -ROUND, 127.0, ALU.add, ALU.min))
                chain.link(dve.tensor_scalar(qn, qn, -127.0, scl[:, 1:2], ALU.max, ALU.mult))
                chain.link(dve.tensor_scalar(sat, qn, FMAX, 10000.0, ALU.is_gt, ALU.mult))
                chain.link(dve.tensor_scalar(xT[:, u, :], qn, -FMAX, -10000.0, ALU.is_lt, ALU.mult))
                chain.link(dve.tensor_tensor(xT[:, u, :], xT[:, u, :], sat, ALU.add))
                chain.link(dve.tensor_scalar(sat, qn, FMAX, -FMAX, ALU.min, ALU.max))
                chain.link(dve.tensor_tensor(sat.bitcast(U32), sat, qn, ALU.is_equal))
                alone(dve)
                dve.copy_predicated(xT[:, u, :], sat.bitcast(U32), qn).then_inc(F["quant"], 1)

            def ff_body(c, u, more):
                if more:
                    ff_prepare(c + 1, 1 - u)
                dve.wait_ge(F["x_kept"], c + 1)
                dve.wait_ge(F["out"], c + 1)
                dve.tensor_tensor(xres[:, bass.ts(c, TPC), :], psV[:, :].rearrange("p (n d) -> p n d", n=TPC),
                                  xres[:, bass.ts(c, TPC), :], ALU.add).then_inc(F["taken"], 1)
                dve.wait_ge(F["taken"], c + 1)
                moments(chain, c, F["stat"])

            over_chunks(dve, chain, 8, 10, lambda: ff_prepare(0, 0), ff_body)
            attention(stages[1], wts[1], F["rstd"])
            attention(stages[2], wts[2], S["a1"]["rstd"])

            chain = Chain(dve, G["dve"])

            def g_norm(c, u):
                dve.wait_ge(S["a2"]["rstd"], c + 1)
                if not (isinstance(c, int) and c < 2):
                    dve.wait_ge(G["x_turned"], c - 1)
                for t in range(TPC):
                    n = c * TPC + t
                    dve.tensor_scalar(xs[:, u, t * P:(t + 1) * P], xres[:, n, :], mv[:, n, 0:1],
                                      rstd[:, bass.ts(n, 1)], ALU.subtract, ALU.mult)
                    ins = dve.tensor_scalar(xres[:, n, :], xres[:, n, :], mv[:, n, 0:1],
                                            rstd[:, bass.ts(n, 1)], ALU.subtract, ALU.mult)
                ins.then_inc(G["x_norm"], 1)

            iota = spread(cst[:, C_IOTA:C_IOTA + 8].unsqueeze(1), [P, TPC, NEXP])

            def each(a):
                return spread(a.unsqueeze(2), [P, TPC, NEXP])

            def g_body(c, u, more):
                if more:
                    g_norm(c + 1, 1 - u)
                dve.wait_ge(G["logit"], c + 1)
                dve.tensor_copy(gl, psX[:, 0:32].rearrange("p (t g) -> p t g", t=TPC)).then_inc(G["logit_up"], 1)
                dve.wait_ge(G["logit_up"], c + 1)
                chain.link(dve.tensor_reduce(gm, gl, AX.X, ALU.max))
                chain.link(dve.tensor_tensor(g1, gl, each(gm), ALU.is_equal))
                chain.link(dve.tensor_tensor(g1, g1, iota, ALU.mult))
                chain.link(dve.tensor_reduce(gn, g1, AX.X, ALU.max))
                chain.link(dve.tensor_tensor(g1, iota, each(gn), ALU.is_equal))
                chain.link(dve.scalar_tensor_tensor(g2, g1, -1e30, gl, ALU.mult, ALU.add))
                chain.link(dve.tensor_reduce(gn, g2, AX.X, ALU.max))
                chain.link(dve.tensor_tensor(g2, g2, each(gn), ALU.is_equal))
                chain.link(dve.tensor_tensor(g2, g2, iota, ALU.mult))
                chain.link(dve.tensor_reduce(gn, g2, AX.X, ALU.max))
                chain.link(dve.tensor_tensor(g2, iota, each(gn), ALU.is_equal))
                chain.link(dve.tensor_tensor(g1, g1, g2, ALU.add))
                dve.tensor_tensor(gate[:, bass.ts(c, TPC), :], gl, each(gm), ALU.subtract).then_inc(G["shift"], 1)
                dve.wait_ge(G["exp"], c + 1)
                chain.link(dve.tensor_tensor(g1, g1, gate[:, bass.ts(c, TPC), :], ALU.mult))
                chain.link(dve.tensor_reduce(gn, g1, AX.X, ALU.add))
                chain.link(dve.reciprocal(gn, gn))
                chain.link(dve.tensor_tensor(gate[:, bass.ts(c, TPC), :], g1, each(gn), ALU.mult))

            over_chunks(dve, chain, 0, 16, lambda: g_norm(0, 0), g_body)

            NU = NEXP * 3
            fin = Chain(dve, G["fin"])

            def expert_chunk(c, first):
                def take(e):
                    dve.wait_ge(G["out"], c * NEXP + e + 1)
                    if not (first and e == 0):
                        dve.wait_ge(G["taken"], c * NEXP + e)
                    for t in range(TPC):
                        n = c * TPC + t
                        ins = dve.scalar_tensor_tensor(xres[:, n, :], psT[:, (e % 2) * CW + t * P:(e % 2) * CW + (t + 1) * P],
                                                       gate[:, n, e:e + 1], xres[:, n, :], ALU.mult, ALU.add)
                    ins.then_inc(G["taken"], 1)

                for k in range(NU):
                    n = c * NU + k
                    e, p = divmod(k, 3)
                    m = HCS[p]
                    dve.wait_ge(G["sil"], n + 1)
                    dve.wait_ge(G["h2"], n + 1)
                    if p == 0 and not (first and e < 2):
                        dve.wait_ge(G["out"], c * NEXP + e - 1)
                    dve.tensor_tensor(hid(e % 2, p)[0:m, :], sil(k % 2)[0:m, :], psS[k % 2][0:m, CW:2 * CW],
                                      ALU.mult).then_inc(G["hid"], 1)
                    if k >= 5 and k % 3 == 2:
                        take(k // 3 - 1)
                take(NEXP - 1)
                dve.wait_ge(G["taken"], (c + 1) * NEXP)
                moments(fin, c, G["var"])
                dve.wait_ge(G["rstd"], c + 1)
                for t in range(TPC):
                    n = c * TPC + t
                    ins = dve.tensor_scalar(xres[:, n, :], xres[:, n, :], mv[:, n, 0:1], rstd[:, bass.ts(n, 1)],
                                            ALU.subtract, ALU.mult)
                ins.then_inc(G["normed"], 1)

            fin.at(0)
            expert_chunk(0, True)
            with dve.Fori(1, NCH) as c:
                fin.at(c * 2)
                expert_chunk(c, False)


def kernel(**inputs):
    import numpy as np
    import ml_dtypes
    import concourse.bacc as bacc
    from concourse.bass_utils import run_bass_kernel_spmd

    i = {k: np.asarray(v) for k, v in inputs.items()}
    f32 = np.float32
    row_head = np.array([[(8 * half + 2 * (r // 32) + (r // 16) % 2) for r in range(P)] for half in range(2)])
    row_b = np.array([(r // 8) % 2 for r in range(P)])
    row_d = np.array([r % 8 for r in range(P)])
    col = [row_head[h] * 8 + row_d for h in range(2)]
    vcol = np.array([[(2 * j + h2) * 8 + d for j in range(8) for d in range(8)] for h2 in range(2)]).reshape(-1)

    def blob(wq, bq, wk, bk, wv, bv, wo, bo):
        b = np.zeros((P, W_N), f32)
        for h in range(2):
            b[:, W_Q + h * P:W_Q + (h + 1) * P] = wq[:, col[h]]
            b[:, W_K + h * P:W_K + (h + 1) * P] = wk[:, col[h]]
            b[:, W_CK + h * SEQ:W_CK + (h + 1) * SEQ] = bk[col[h]]
            b[:, W_O + h * P:W_O + (h + 1) * P] = wo[col[h]]
            for s in range(2):
                o = W_CQ + (2 * h + s) * SEQ
                mine = row_b == s
                b[mine, o:o + SEQ] = bq[col[h]][mine]
        b[:, W_V:W_V + P] = wv[:, vcol]
        b[:, W_BV:W_BV + P] = np.broadcast_to(bv[vcol], (P, P))
        b[:, W_BO:W_BO + P] = np.broadcast_to(bo, (P, P))
        return b

    def along(v):
        return np.broadcast_to(v[:, None], (P, SEQ))

    slopes = (2.0 ** (-8.0 * np.arange(1, 17) / 16)).astype(f32)
    pos = np.arange(SEQ, dtype=f32)
    wq = np.zeros((P, 16, 8), f32)
    wk = np.zeros((P, 16, 8), f32)
    wq[:, :, 0:4] = i["L0_attn_Wq"].reshape(P, 16, 4)
    wk[:, :, 0:4] = np.tile(i["L0_attn_Wk"], (1, 4)).reshape(P, 16, 4)
    qc = np.zeros((16, 8, SEQ), f32)
    kc = np.zeros((16, 8, SEQ), f32)
    qc[:, 4] = 1.0
    kc[:, 4] = slopes[:, None] * pos
    qc[:, 5] = -pos
    kc[:, 5] = slopes[:, None]
    b0 = blob(wq.reshape(P, P), qc.reshape(P, SEQ), wk.reshape(P, P), kc.reshape(P, SEQ),
              np.tile(i["L0_attn_Wv"], (1, 4)), np.zeros(P, f32), i["L0_attn_Wp"], i["L0_attn_bp"])
    qkv, bqkv = i["L1_attn_Wqkv_w"], i["L1_attn_Wqkv_b"]
    b1 = blob(qkv[0:P].T, along(bqkv[0:P]), qkv[P:2 * P].T, along(bqkv[P:2 * P]), qkv[2 * P:].T, bqkv[2 * P:],
              i["L1_attn_out_w"].T, i["L1_attn_out_b"])
    b2 = blob(i["L1_xattn_w_q"].T, along(i["L1_xattn_b_q"]), i["L1_xattn_w_k"].T, along(i["L1_xattn_b_k"]),
              i["L1_xattn_w_v"].T, i["L1_xattn_b_v"], i["L1_xattn_w_o"].T, i["L1_xattn_b_o"])

    ml = np.zeros((P, 48 + 16 + P), f32)
    for s in range(3):
        ml[:, 16 * s:16 * s + 8] = i["L0_xattn_igate_kernel"][P * s:P * (s + 1)]
        ml[:, 16 * s + 8:16 * s + 16] = i["L0_xattn_fgate_kernel"][P * s:P * (s + 1)]
    ml[:, 48:56] = i["L0_xattn_igate_bias"]
    ml[:, 56:64] = i["L0_xattn_fgate_bias"]
    ml[:, 64:] = i["L0_xattn_outnorm_weight"].reshape(-1)
    ffw = np.zeros((P, P + 1), f32)
    ffw[:, 0:P] = i["L0_ffn_bias"]

    r = np.arange(P)
    c = np.zeros((P, C_N), f32)
    c[:, C_ID:C_ID + P] = np.eye(P)
    c[:, C_MB] = row_b == 0
    c[:, C_MB + 1] = row_b == 1
    c[:, C_ONE:C_ONE + 32] = (r[:, None] // SEQ) == (np.arange(32)[None, :] // 16)
    c[:, C_CUM:C_CUM + P] = (r[:, None] <= r[None, :]) & (r[:, None] // SEQ == r[None, :] // SEQ)
    mcol = np.array([(2 * j + h2) * 16 + d for h2 in range(2) for j in range(4) for d in range(16)])
    c[mcol, C_PV + r] = 1.0
    for t in range(TPC):
        c[8 * t:8 * t + 8, C_SEL + t * SEQ:C_SEL + (t + 1) * SEQ] = 1.0
    c[0:32, C_DEL:C_DEL + 8] = (r[0:32, None] % 8) == np.arange(8)[None, :]
    c[:, C_RST:C_RST + P] = np.where(r % SEQ == 0, f32(-1e30), f32(0))
    c[:, C_HALF:C_HALF + 32] = -0.5
    c[:, C_IOTA:C_IOTA + 8] = 8 - np.arange(8)
    m16 = np.zeros((P, 256), f32)
    m16[:, 0:P] = -80.0 * np.eye(P)
    upper = np.arange(SEQ)[None, :] > (r % SEQ)[:, None]
    m16[:, P:P + SEQ] = 125.0 * upper
    m16[:, P + SEQ:P + 2 * SEQ] = 1e28 * upper
    m16 = m16.astype(ml_dtypes.bfloat16)

    w3 = np.zeros((HCS[0], NEXP, 3, P), f32)
    for p in range(3):
        w3[0:HCS[p], :, p] = i["L1_ffn_W3"][:, :, HO[p]:HO[p] + HCS[p]].transpose(2, 0, 1)
    arrays = {
        "x": i["x"].reshape(-1, P), "ctx": i["ctx_1024"].reshape(-1, P), "c32": c, "c16": m16,
        "w_a0": b0, "w_a1": b1, "w_a2": b2, "w_ml": ml, "w_ff": ffw,
        "w_tern": i["L0_ffn_ternary_weight"], "w_scale": np.broadcast_to(i["L0_ffn_act_scale"].reshape(1, 1), (P, 1)),
        "w_gate": i["L1_ffn_Wg"].T,
        "w_e1": i["L1_ffn_W1"].reshape(-1, P).T, "w_e2": i["L1_ffn_W2"].reshape(-1, P).T,
        "w_e3": w3.reshape(HCS[0], -1),
    }
    arrays = {k: np.ascontiguousarray(v) for k, v in arrays.items()}
    nc = bacc.Bacc("TRN2", target_bir_lowering=False, num_devices=1)
    a = {k: nc.dram_tensor(f"in_{k}", v.shape, mybir.dt.from_np(v.dtype), kind="ExternalInput").ap()
         for k, v in arrays.items()}
    o = nc.dram_tensor("out_0", (NT * P, P), F32, kind="ExternalOutput").ap()
    decoder(nc, a["x"], a["ctx"], a["c32"], a["c16"], [a["w_a0"], a["w_a1"], a["w_a2"]], a["w_ml"], a["w_ff"],
            a["w_tern"], a["w_scale"], a["w_gate"], a["w_e1"], a["w_e2"], a["w_e3"], o)
    res = run_bass_kernel_spmd(nc, [{f"in_{k}": v for k, v in arrays.items()}], core_ids=[0])
    return res.results[0]["out_0"].reshape(64, SEQ, P)
```

```python
from contextlib import ExitStack

import concourse.bass as bass
from concourse import mybir

ALU = mybir.AluOpType
ACT = mybir.ActivationFunctionType
AX = mybir.AxisListType
F32 = mybir.dt.float32
BF16 = mybir.dt.bfloat16
U32 = mybir.dt.uint32

P = 128
SEQ = 64
TPC = 4
CW = TPC * P
NCH = 8
NT = NCH * TPC
HALVES = 2
DH = 8
LN_EPS = 1e-5
ROUND = 12582912.0
FMAX = 3.4028234663852886e38
NEXP = 8
HID = 341
HCS = [114, 114, 113]
HO = [0, 114, 228]

C_ID, C_MB, C_ONE, C_CUM, C_PV, C_SEL, C_DEL, C_RST, C_HALF, C_IOTA = 0, 128, 130, 162, 290, 418, 674, 682, 810, 842
C_N = 850
W_Q, W_CQ, W_K, W_CK, W_V, W_BV, W_O, W_BO, W_N = 0, 256, 512, 768, 896, 1024, 1152, 1408, 1536


def need(eng, sem, value):
    if isinstance(value, int) and value <= 0:
        return
    eng.wait_ge(sem, value)


def of_parity(c, u, each):
    return c * (each // 2) + (each - u * (each // 2))


def spread(ap, shape):
    return ap.broadcast_to(shape)


class Chain:

    def __init__(self, eng, sem):
        self.eng, self.sem, self.base, self.n = eng, sem, 0, 0

    def at(self, base):
        self.base, self.n = base, 0

    def link(self, ins):
        ins.then_inc(self.sem, 1)
        self.n += 1
        self.eng.wait_ge(self.sem, self.base + self.n)


def over_chunks(eng, chain, lens, prologue, body, epilogue=None):
    first, each = lens
    if chain:
        chain.at(0)
    prologue()
    body(0, 0, True)
    if chain:
        assert chain.n == first, (chain.n, first)
    with eng.Fori(0, (NCH - 2) // 2) as it:
        for u in range(2):
            if chain:
                chain.at(it * (2 * each) + (u * each + first))
            body(it * 2 + (1 + u), (1 + u) % 2, True)
            if chain:
                assert chain.n == each, (chain.n, each)
    if chain:
        chain.at((NCH - 2) * each + first)
    body(NCH - 1, (NCH - 1) % 2, False)
    if epilogue:
        epilogue()


def behind(c, u, i, lag, steps, what):
    k = i - lag
    if k >= 0:
        what(c * steps + k, u, k)
    elif not is_first(c):
        what(c * steps + k, 1 - u, k + steps)


def is_first(c):
    return isinstance(c, int) and c == 0


MP = ["x", "pre", "cum", "v", "a", "m"]
NP_ = len(MP)
MSLOT = {(0, 1): "x", (1, 0): "pre", (2, 0): "cum", (2, 1): "v", (3, 0): "a", (3, 1): "m"}


class Attn:

    def __init__(self, name, reps, scale, mask, kv_ctx, first):
        self.name, self.reps, self.scale, self.mask, self.kv_ctx, self.first = name, reps, scale, mask, kv_ctx, first
        self.steps = reps * TPC
        self.phases = ["x"] + (["ctx"] if first else []) + ["k0", "k1", "q0", "q1", "v"]
        if reps > 1:
            self.slots = {(0, 1): "x", (1, 0): "k0", (2, 0): "out", (3, 0): "k1", (4, 0): "q0", (5, 0): "q1", (6, 0): "v"}
        elif first:
            self.slots = {(0, 0): "x", (0, 1): "ctx", (1, 0): "k0", (1, 1): "k1", (2, 0): "out", (2, 1): "q0",
                          (3, 0): "q1", (3, 1): "v"}
        else:
            self.slots = {(0, 1): "x", (1, 0): "k0", (1, 1): "k1", (2, 0): "out", (2, 1): "q0", (3, 0): "q1", (3, 1): "v"}

        def order(prev, more):
            uses = []
            for i in range(self.steps):
                if i >= 3 or prev:
                    uses.append(("turn", i))
                for at in (0, 1):
                    ph = self.slots.get((i, at))
                    if ph == "out" and prev or ph not in (None, "out") and more:
                        uses.append(ph)
            return uses
        self.orders = {"first": order(False, True), "mid": order(True, True), "last": order(True, False)}

    def base(self, c):
        n = len(self.phases)
        if is_first(c):
            return n
        return (c - 1) * len(self.orders["mid"]) + (n + len(self.orders["first"]))

    def use(self, c, key):
        kind = "first" if is_first(c) else "last" if isinstance(c, int) and c == NCH - 1 else "mid"
        return self.base(c) + self.orders[kind].index(key)

    def prep(self, c, phase):
        if is_first(c):
            return self.phases.index(phase)
        return self.use(c - 1, phase)

    def tail(self, k):
        return self.base(NCH - 1) + len(self.orders["last"]) + k


def decoder(nc, x_in, ctx_in, c32, c16, attn_w, ml_w, ffn_w, ffn_t, ffn_s, moe_g, moe_w1, moe_w2, moe_w3, out):
    x_t = x_in.rearrange("(n p) d -> p n d", p=P)
    ctx_t = ctx_in.rearrange("(n p) d -> p n d", p=P)
    out_t = out.rearrange("(n p) d -> p n d", p=P)
    with ExitStack() as stack:
        def sb(name, shape, dt=F32):
            return stack.enter_context(nc.sbuf_tensor(name, shape, dt))

        def sem(name):
            return stack.enter_context(nc.semaphore(name))

        cst = sb("cst", [P, C_N])
        cmask = sb("cmask", [P, 256], BF16)
        wts = [sb(f"wts{i}", [P, W_N]) for i in range(3)]
        mlw = sb("mlw", [P, 48 + 16 + P])
        ffw = sb("ffw", [P, P + 1])
        fft = sb("fft", [P, P], mybir.dt.int32)
        fftf = sb("fftf", [P, P])
        ffT = sb("ffT", [P, P])
        scl = sb("scl", [P, 8])
        mog = sb("mog", [P, NEXP])
        w3 = sb("w3", [HCS[0], 3 * NEXP * P])
        xres = sb("xres", [P, NT, P])
        ctxT = sb("ctxT", [P, NT * P])
        xs = sb("xs", [P, 2, CW])
        xT = sb("xT", [P, 2, CW])
        kd = sb("kd", [P, 2, HALVES, CW])
        q = sb("q", [P, 2, HALVES, CW])
        kbd = [sb(f"kbd{i}", [P, HALVES, 8, CW]) for i in range(2)]
        vbd = sb("vbd", [P, 2, TPC, 8, 34])
        vm = sb("vm", [P, 2, TPC, 4, 66])
        work = sb("work", [P, 8 * CW])
        abd = q[:, :, :, :].rearrange("p u h k -> p u (h k)").rearrange("p u (b a k) -> p u b a k", b=2, a=8)
        cn = sb("cn", [P, 2, 256])
        gT = sb("gT", [P, 2 * P])
        tmp = sb("tmp", [P, 2, CW])
        tmp2 = sb("tmp2", [P, CW])
        small = sb("small", [P, 16 * 64])
        stats = sb("stats", [P, TPC, 6])
        spare = sb("spare", [P, 2])
        mvs = sb("mvs", [P, TPC, 2])
        mv = sb("mv", [P, NT, 2])
        rstd = sb("rstd", [P, NT])
        gate = sb("gate", [P, NT, NEXP])

        psS = [stack.enter_context(nc.psum_tensor(f"psS{i}", [P, 2 * CW], F32)) for i in range(2)]
        psT = stack.enter_context(nc.psum_tensor("psT", [P, 2 * CW], F32))
        psV = stack.enter_context(nc.psum_tensor("psV", [P, CW], F32))
        psX = stack.enter_context(nc.psum_tensor("psX", [P, CW], F32))

        ident = cst[:, C_ID:C_ID + P]
        prob = [work[:, i * 2 * CW:(i + 1) * 2 * CW] for i in range(2)]
        probT = [work[:, (2 + i) * 2 * CW:(3 + i) * 2 * CW] for i in range(2)]

        def cols(a, n):
            return small[:, a:a + n]
        rmax = [cols(16 * i, 16) for i in range(2)]
        recip = cols(32, 16)

        w1v = kbd[0][:, :, :, :].rearrange("p a b c -> p (a b c)")[:, 0:NEXP * HID]
        w2v = kbd[1][:, :, :, :].rearrange("p a b c -> p (a b c)")[:, 0:NEXP * HID]
        ZEROED = 7

        pre = cols(320, 64).rearrange("p (t g) -> p t g", t=TPC)
        fabs = cols(384, 32).rearrange("p (t g) -> p t g", t=TPC)
        flog = cols(416, 32).rearrange("p (t g) -> p t g", t=TPC)
        lf = cols(448, 32).rearrange("p (t g) -> p t g", t=TPC)
        cum = cols(480, 32)
        agate = cols(512, 32)
        negM = [cols(544 + 32 * i, 32).rearrange("p (t g) -> p t g", t=TPC) for i in range(2)]
        enm = [cols(608 + 32 * i, 32).rearrange("p (t g) -> p t g", t=TPC) for i in range(2)]
        aT = gT[0:32, 0:P]
        MT = gT[0:32, P:2 * P]
        nrm = cols(672, 8)
        hmu = cols(680, 32)
        hvar = cols(712, 32)
        hrs = cols(744, 32)
        def ofwork(a):
            return work[:, a:a + NT * NEXP].rearrange("p (t g) -> p t g", t=NT)
        gl, g1, g2 = (ofwork(k * NT * NEXP) for k in range(3))
        gm, gn = cols(776, NT), cols(776 + NT, NT)

        def head(a):
            return spread(a.unsqueeze(2), [P, 32, 16])

        def hid(par, p):
            return work[:, (3 * par + p) * CW:(3 * par + p + 1) * CW]

        def sil(par):
            return work[:, (6 + par) * CW:(7 + par) * CW]

        kvst = [kd[:, i, 0, :] for i in range(2)]
        ctx_st = [vm[:, i, :, :, :].rearrange("p t j k -> p (t j k)")[:, 0:CW] for i in range(2)]


        w_in = sem("w_in")
        zeroed = sem("zeroed")
        scaled = sem("scaled")
        scl_done = sem("scl_done")
        tern_f, tern_T = sem("tern_f"), sem("tern_T")
        N_W = 16 * 11

        stages = [Attn("a0", 1, 0.5, 1, False, True),
                  Attn("a1", 3, 8 ** -0.5, 0, False, False),
                  Attn("a2", 1, 8 ** -0.5, None, True, False)]
        S = {}
        for st in stages:
            S[st.name] = {k: sem(f"{st.name}_{k}") for k in (
                "x_in0", "x_in1", "staged", "x_norm", "x_kept", "mix_full", "mix_free", "k_spread0", "k_spread1", "score", "shifted", "prob",
                "turned", "turned_out", "ctx_full", "ctx_done", "stat", "rstd", "dve")}
        M = {k: sem(f"m_{k}") for k in (
            "x_norm", "x_kept", "mix_full", "mix_free", "k_spread0", "k_spread1", "gate_abs", "gate_exp", "gate_ln", "gate_lf",
            "score", "decay", "prod", "turned", "turned_out", "ctx_full", "ctx_done", "nm", "enm", "a_up", "cum_up",
            "pool", "summed", "stat", "rstd", "dve", "var")}
        F = {k: sem(f"f_{k}") for k in (
            "x_norm", "x_kept", "x_turned", "quant", "out", "taken", "stat", "rstd", "dve")}
        G = {k: sem(f"g_{k}") for k in (
            "x_norm", "x_turned", "x_up", "logit", "logit_up", "shift", "exp", "w_in", "h1", "sil", "h2", "hid",
            "out", "taken", "var", "rstd", "dve", "normed", "stored", "fin")}

        block = stack.enter_context(nc.Block())

        def alone(dve):
            dve.memset(spare[:, 0:1], 0.0)

        @block.sync
        def _(sp):
            for dst, src in ((cst, c32), (wts[0], attn_w[0]), (cmask, c16), (wts[1], attn_w[1]), (wts[2], attn_w[2]), (mlw, ml_w), (ffw, ffn_w),
                             (fft, ffn_t), (mog, moe_g), (w3, moe_w3)):
                sp.dma_start(dst[:, :], src).then_inc(w_in, 16)
            sp.dma_start(scl[:, 0:1], ffn_s).then_inc(w_in, 16)

            raw = [vm[:, i, :, :, :].rearrange("p t j k -> p (t j k)")[:, 0:CW].rearrange("p (n d) -> p n d", n=TPC)
                   for i in range(2)]

            def keys(st, c, u):
                s = S[st.name]
                need(sp, s["score"], c * st.steps - st.steps)
                sp.wait_ge(s["mix_free"], st.prep(c, "k1") + 1)
                for hh in range(8):
                    rows = slice(16 * hh, 16 * hh + 16)
                    sp.dma_start(kbd[u][rows, :, hh, :], kd[rows, u, :, :]).then_inc(s[f"k_spread{u}"], 16)

            def load(st, c, u):
                s = S[st.name]
                if not (isinstance(c, int) and c < 2):
                    sp.wait_ge(s["mix_full"], st.prep(c - 2, "ctx") + 1)
                    sp.wait_ge(s["x_kept"], c * 2 - 2)
                sp.dma_start(xs[:, u, :].rearrange("p (n d) -> p n d", n=TPC),
                             x_t[:, bass.ts(c, TPC), :]).then_inc(s[f"x_in{u}"], 16)
                sp.dma_start(raw[u], ctx_t[:, bass.ts(c, TPC), :]).then_inc(s[f"x_in{u}"], 16)

            st = stages[0]
            load(st, 0, 0)
            load(st, 1, 1)
            sp.wait_ge(zeroed, ZEROED)
            keys(st, 0, 0)
            load(st, 2, 0)
            keys(st, 1, 1)
            load(st, 3, 1)
            keys(st, 2, 0)
            with sp.Fori(0, (NCH - 4) // 2) as it:
                for u in range(2):
                    load(st, it * 2 + (4 + u), u)
                    keys(st, it * 2 + (3 + u), 1 - u)
            keys(st, NCH - 1, 1)

            sp.wait_ge(S["a0"]["score"], stages[0].steps * NCH)

            def ml_keys(c, u):
                need(sp, M["score"], (c - 1) * TPC)
                for h in range(8):
                    rows = slice(16 * h, 16 * h + 16)
                    sp.dma_start(kbd[u][rows, 0, h, :], ctxT[rows, bass.ts(c, CW)]).then_inc(M[f"k_spread{u}"], 16)

            sp.wait_ge(S["a0"]["mix_free"], stages[0].prep(NCH - 1, "ctx") + 1)
            over_chunks(sp, None, (0, 0), lambda: ml_keys(0, 0),
                        lambda c, u, more: ml_keys(c + 1, 1 - u) if more else None)
            for st, before, n in ((stages[1], M["score"], NCH * TPC), (stages[2], S["a1"]["score"], stages[1].steps * NCH)):
                sp.wait_ge(before, n)
                over_chunks(sp, None, (0, 0), lambda: keys(st, 0, 0),
                            lambda c, u, more: keys(st, c + 1, 1 - u) if more else None)
            sp.wait_ge(S["a2"]["score"], stages[2].steps * NCH)
            sp.dma_start(w1v, moe_w1).then_inc(G["w_in"], 16)
            sp.dma_start(w2v, moe_w2).then_inc(G["w_in"], 16)

            def store(c):
                sp.wait_ge(G["normed"], c + 1)
                sp.dma_start(out_t[:, bass.ts(c, TPC), :],
                             xres[:, bass.ts(c, TPC), :]).then_inc(G["stored"], 16)

            with sp.Fori(0, NCH) as c:
                store(c)
            sp.wait_ge(G["stored"], 16 * NCH)

        @block.gpsimd
        def _(g):
            for ap in (kbd[0][:, :, :, :], vbd[:, :, :, :, :], cn[:, :, :], gT[:, :]):
                g.memset(ap, 0.0).then_inc(zeroed, 1)
            g.wait_ge(zeroed, 5)
            for h2 in range(2):
                g.memset(vbd[h2 * SEQ:(h2 + 1) * SEQ, :, :, :, 32 + h2], 1.0).then_inc(zeroed, 1)
            g.wait_ge(zeroed, ZEROED)
            g.wait_ge(w_in, N_W)

            def rstd_of(c, stat, done):
                g.wait_ge(stat, c + 1)
                g.tensor_tensor(rstd[:, bass.ts(c, TPC)], mv[:, bass.ts(c, TPC), 1], cst[:, C_HALF:C_HALF + TPC],
                                ALU.pow).then_inc(done, 1)

            def keep(c, u, s, bias):
                g.wait_ge(s["x_norm"], c + 1)
                dst = xres[:, bass.ts(c, TPC), :]
                src = xs[:, u, :].rearrange("p (n d) -> p n d", n=TPC)
                if bias is None:
                    g.tensor_copy(dst, src).then_inc(s["x_kept"], 1)
                else:
                    g.tensor_tensor(dst, src, spread(bias.unsqueeze(1), [P, TPC, P]), ALU.add).then_inc(s["x_kept"], 1)

            def stage(c, u, dst, free, done):
                if free is not None:
                    g.wait_ge(*free)
                g.tensor_copy(dst[u], ctxT[:, bass.ts(c, CW)]).then_inc(done, 1)

            def attention(st, wt):
                s = S[st.name]
                bias = wt[:, W_BO:W_BO + P]

                def prologue():
                    if st.first:
                        keep_first(0, 0)
                    else:
                        if st.kv_ctx:
                            stage(0, 0, ctx_st, None, s["staged"])
                        keep(0, 0, s, bias)

                def keep_first(c, u):
                    g.wait_ge(s[f"x_in{u}"], of_parity(c, u, 32))
                    g.tensor_tensor(xres[:, bass.ts(c, TPC), :], xs[:, u, :].rearrange("p (n d) -> p n d", n=TPC),
                                    spread(bias.unsqueeze(1), [P, TPC, P]), ALU.add).then_inc(s["x_kept"], 2)

                def body(c, u, more):
                    if more:
                        if st.first:
                            keep_first(c + 1, 1 - u)
                        else:
                            if st.kv_ctx:
                                stage(c + 1, 1 - u, ctx_st, None if is_first(c) else (s["mix_full"], st.base(c)), s["staged"])
                            keep(c + 1, 1 - u, s, bias)
                    if not is_first(c):
                        rstd_of(c - 1, s["stat"], s["rstd"])

                over_chunks(g, None, (0, 0), prologue, body, lambda: rstd_of(NCH - 1, s["stat"], s["rstd"]))

            attention(stages[0], wts[0])

            chain = Chain(g, M["pool"])

            def ml_finish(c, u):
                hb3 = tmp[:, u, :].rearrange("p (g d) -> p g d", g=32)
                h3 = tmp[:, u, :].rearrange("p (t d) -> p t d", t=TPC)
                g.wait_ge(M["var"], c + 1)
                chain.link(g.tensor_tensor(hrs, hvar, cst[:, C_HALF:C_HALF + 32], ALU.pow))
                chain.link(g.tensor_tensor(hb3, hb3, head(hrs), ALU.mult))
                chain.link(g.tensor_tensor(h3, h3, spread(mlw[:, 64:64 + P].unsqueeze(1), [P, TPC, P]), ALU.mult))
                g.wait_ge(M["x_kept"], c + 1)
                g.tensor_tensor(xres[:, bass.ts(c, TPC), :], h3, xres[:, bass.ts(c, TPC), :], ALU.add).then_inc(M["summed"], 1)
                rstd_of(c, M["stat"], M["rstd"])

            def ml_body(c, u, more):
                if more:
                    stage(c + 1, 1 - u, kvst, None if is_first(c) else (M["mix_full"], (c + 1) * NP_), M["a_up"])
                    keep(c + 1, 1 - u, M, None)
                if not is_first(c):
                    ml_finish(c - 1, 1 - u)

            g.wait_ge(S["a0"]["mix_free"], stages[0].prep(NCH - 1, "ctx") + 1)
            for u in range(2):
                g.wait_ge(S["a0"][f"k_spread{u}"], 128 * NCH // 2)
            over_chunks(g, chain, (0, 3), lambda: [stage(0, 0, kvst, None, M["a_up"]), keep(0, 0, M, None)],
                        ml_body, lambda: ml_finish(NCH - 1, 1))

            def ff_body(c, u, more):
                if more:
                    keep(c + 1, 1 - u, F, ffw[:, 0:P])
                rstd_of(c, F["stat"], F["rstd"])

            over_chunks(g, None, (0, 0), lambda: keep(0, 0, F, ffw[:, 0:P]), ff_body)
            attention(stages[1], wts[1])
            attention(stages[2], wts[2])
            with g.Fori(0, NCH) as c:
                rstd_of(c, G["var"], G["rstd"])

        @block.tensor
        def _(pe):
            pe.wait_ge(w_in, N_W)
            pe.wait_ge(zeroed, ZEROED)
            pe.wait_ge(tern_f, 1)
            pe.transpose(psV[:, 0:P], fftf[:, :], ident).then_inc(tern_T, 1)
            pe.wait_ge(scaled, 6)

            def turn_chunk(u, src):
                for t in range(TPC):
                    mm = pe.transpose(psX[:, t * P:(t + 1) * P], src[:, t * P:(t + 1) * P], ident)
                return mm

            def values(src, wv):
                for t in range(TPC):
                    for h2 in range(2):
                        for b in range(2):
                            o = t * P + b * SEQ
                            mm = pe.matmul(psX[h2 * SEQ:(h2 + 1) * SEQ, o:o + SEQ], src[:, o:o + SEQ],
                                           wv[:, h2 * SEQ:(h2 + 1) * SEQ], start=True, stop=True)
                return mm

            def attention(st, wt):
                s = S[st.name]

                def prepare(c, u, ph):
                    need(pe, s["mix_free"], st.prep(c, ph))
                    if ph == "x":
                        if st.first:
                            pe.wait_ge(s[f"x_in{u}"], of_parity(c, u, 32))
                        else:
                            pe.wait_ge(s["x_norm"], c + 1)
                        mm = turn_chunk(u, xs[:, u, :])
                    elif ph == "ctx":
                        mm = turn_chunk(u, ctx_st[u])
                    elif ph[0] in "kq":
                        w = (W_K if ph[0] == "k" else W_Q) + P * int(ph[1])
                        src = ctxT[:, bass.ts(c, CW)] if st.kv_ctx and ph[0] == "k" else xT[:, u, :]
                        mm = pe.matmul(psX[:, :], wt[:, w:w + P], src, start=True, stop=True)
                    else:
                        if st.kv_ctx:
                            pe.wait_ge(s["staged"], c + 1)
                        mm = values(ctx_st[u] if st.kv_ctx else xT[:, u, :], wt[:, W_V:W_V + P])
                    mm.then_inc(s["mix_full"], 1)

                def score(c, u, i):
                    n = c * st.steps + i
                    r, t = divmod(i, TPC)
                    if not (is_first(c) and i < 2):
                        pe.wait_ge(s["shifted"], n - 1)
                    if r:
                        pe.wait_ge(s["mix_free"], st.use(c, ("turn", i - 1)) + 1)
                    if i == 0:
                        pe.wait_ge(s["mix_free"], st.prep(c, "q1") + 1)
                        pe.wait_ge(s[f"k_spread{u}"], of_parity(c, u, 128))
                    bank = psS[i % 2]
                    if st.mask is not None:
                        m = cmask[:, P + SEQ * st.mask:P + SEQ * (st.mask + 1)]
                        for h in range(HALVES):
                            pe.matmul(bank[:, h * CW:(h + 1) * CW].rearrange("p (a k) -> p a k", a=8), cmask[:, 0:P],
                                      spread(m.unsqueeze(1), [P, 8, SEQ]), start=True, stop=False,
                                      skip_group_check=True)
                    for h in range(HALVES):
                        for b in range(2):
                            o = t * P + b * SEQ
                            mm = pe.matmul(bank[b * SEQ:(b + 1) * SEQ, h * CW:(h + 1) * CW].rearrange("p (a k) -> p a k", a=8),
                                           q[:, u, h, o:o + SEQ], kbd[u][:, h, :, o:o + SEQ],
                                           start=st.mask is None, stop=True, skip_group_check=True)
                    mm.then_inc(s["score"], 1)

                def turn(n, i):
                    pe.wait_ge(s["prob"], n + 1)
                    need(pe, s["turned_out"], n)
                    for j in range(8):
                        mm = pe.transpose(psT[:, j * P:(j + 1) * P], prob[i % 2][:, j * P:(j + 1) * P], ident)
                    mm.then_inc(s["turned"], 1)

                def mix(n, u, i, c=None):
                    if i == 0:
                        pe.wait_ge(s["mix_free"], st.prep(c, "v") + 1)
                    pe.wait_ge(s["turned_out"], n + 1)
                    need(pe, s["ctx_done"], n)
                    for j in range(8):
                        mm = pe.matmul(psV[:, j * 34:(j + 1) * 34], probT[i % 2][:, j * P:(j + 1) * P],
                                       vbd[:, u, i % TPC, j, :], start=True, stop=True)
                    mm.then_inc(s["ctx_full"], 1)

                def turn_back(n, i, use):
                    pe.wait_ge(s["ctx_done"], n + 1)
                    pe.wait_ge(s["mix_free"], use)
                    for h in range(HALVES):
                        mm = pe.transpose(psX[:, h * P:(h + 1) * P], cn[:, i % 2, h * P:(h + 1) * P], ident)
                    mm.then_inc(s["mix_full"], 1)

                def project(u, use):
                    pe.wait_ge(s["mix_free"], use)
                    for t in range(TPC):
                        for h in range(HALVES):
                            mm = pe.matmul(psX[:, t * P:(t + 1) * P], q[:, u, h, t * P:(t + 1) * P],
                                           wt[:, W_O + h * P:W_O + (h + 1) * P], start=h == 0, stop=h == 1)
                    mm.then_inc(s["mix_full"], 1)

                def slot(c, u, i, at, more):
                    ph = st.slots.get((i, at))
                    if ph == "out" and not is_first(c):
                        project(1 - u, st.use(c, "out"))
                    elif ph not in (None, "out") and more:
                        prepare(c + 1, 1 - u, ph)

                def body(c, u, more):
                    for i in range(st.steps):
                        score(c, u, i)
                        behind(c, u, i, 3, st.steps, lambda n, uu, k: turn_back(n, k, st.use(c, ("turn", i))))
                        behind(c, u, i, 1, st.steps, lambda n, uu, k: turn(n, k))
                        slot(c, u, i, 0, more)
                        behind(c, u, i, 2, st.steps, lambda n, uu, k: mix(n, uu, k, c))
                        slot(c, u, i, 1, more)

                def epilogue():
                    u, n = (NCH - 1) % 2, NCH * st.steps
                    for d in range(3):
                        turn_back(n - 3 + d, st.steps - 3 + d, st.tail(d))
                        if d == 0:
                            turn(n - 1, st.steps - 1)
                        if d < 2:
                            mix(n - 2 + d, u, st.steps - 2 + d)
                    project(u, st.tail(3))

                over_chunks(pe, None, (0, 0), lambda: [prepare(0, 0, ph) for ph in st.phases], body, epilogue)

            attention(stages[0], wts[0])

            def ml_prepare(c, u, ph):
                n = c * NP_ + MP.index(ph)
                need(pe, M["mix_free"], n)
                if ph == "x":
                    pe.wait_ge(M["x_norm"], c + 1)
                    mm = turn_chunk(u, xs[:, u, :])
                elif ph == "v":
                    mm = values(kvst[u], cst[:, C_PV:C_PV + P])
                elif ph == "pre":
                    pe.wait_ge(M["a_up"], c + 1)
                    for t in range(TPC):
                        o = psX[:, t * 16:(t + 1) * 16]
                        pe.matmul(o, xT[:, u, t * P:(t + 1) * P], mlw[:, 0:16], start=True, stop=False)
                        mm = pe.matmul(o, kvst[u][:, t * P:(t + 1) * P], mlw[:, 16:32], start=False, stop=True)
                elif ph == "cum":
                    pe.wait_ge(M["gate_lf"], c + 1)
                    mm = pe.matmul(psX[:, 0:32], cst[:, C_CUM:C_CUM + P], lf.rearrange("p t g -> p (t g)"), start=True, stop=True)
                elif ph == "a":
                    mm = pe.transpose(psX[0:32, 0:P], agate, ident)
                else:
                    mm = pe.transpose(psX[:, 0:P], gT[:, P:2 * P], ident)
                mm.then_inc(M["mix_full"], 1)

            def ml_score(c, u, t):
                n = c * TPC + t
                if not (isinstance(c, int) and c == 0 and t < 2):
                    pe.wait_ge(M["prod"], n - 1)
                if t == 0:
                    pe.wait_ge(M["mix_free"], (c + 1) * NP_ - 1)
                    pe.wait_ge(M[f"k_spread{u}"], of_parity(c, u, 128))
                bank = psS[t % 2]
                qk = bank[:, 0:CW]
                dec = bank[:, CW:2 * CW].rearrange("p (a k) -> p a k", a=8)
                m = cmask[:, P + SEQ:P + 2 * SEQ]
                for b in range(2):
                    o = t * P + b * SEQ
                    pe.matmul(bank[b * SEQ:(b + 1) * SEQ, 0:CW].rearrange("p (a k) -> p a k", a=8),
                              xT[:, u, o:o + SEQ], kbd[u][:, 0, :, o:o + SEQ], start=True, stop=True,
                              skip_group_check=True)
                pe.matmul(dec, cmask[:, 0:P], spread(m.unsqueeze(1), [P, 8, SEQ]), start=True, stop=False, skip_group_check=True)
                for b in range(2):
                    pe.matmul(bank[b * SEQ:(b + 1) * SEQ, CW:2 * CW].rearrange("p (a k) -> p a k", a=8),
                              cst[:, C_SEL + t * SEQ:C_SEL + (t + 1) * SEQ], abd[:, u, b, :, :], start=False, stop=False,
                              skip_group_check=True)
                if t == 0:
                    pe.wait_ge(M["mix_free"], (c + 1) * NP_)
                mm = pe.matmul(dec, ident, spread(negM[u][:, t, :].unsqueeze(2), [P, 8, SEQ]), start=False, stop=True,
                          skip_group_check=True)
                mm.then_inc(M["score"], 1)

            def ml_turn(n, t):
                pe.wait_ge(M["prod"], n + 1)
                need(pe, M["turned_out"], n)
                for j in range(4):
                    mm = pe.transpose(psT[:, j * P:(j + 1) * P], prob[t % 2][:, j * P:(j + 1) * P], ident)
                mm.then_inc(M["turned"], 1)

            def ml_mix(n, u, t):
                pe.wait_ge(M["turned_out"], n + 1)
                need(pe, M["ctx_done"], n)
                for j in range(4):
                    mm = pe.matmul(psV[:, j * 66:(j + 1) * 66], probT[t % 2][:, j * P:(j + 1) * P], vm[:, u, t, j, :],
                                   start=True, stop=True)
                mm.then_inc(M["ctx_full"], 1)

            def ml_body(c, u, more):
                for i in range(TPC):
                    ml_score(c, u, i)
                    behind(c, u, i, 1, TPC, lambda n, uu, k: ml_turn(n, k))
                    if more and (i, 0) in MSLOT:
                        ml_prepare(c + 1, 1 - u, MSLOT[i, 0])
                    behind(c, u, i, 2, TPC, ml_mix)
                    if more and (i, 1) in MSLOT:
                        ml_prepare(c + 1, 1 - u, MSLOT[i, 1])

            def ml_epilogue():
                n = NCH * TPC
                ml_turn(n - 1, 3)
                ml_mix(n - 2, 1, 2)
                ml_mix(n - 1, 1, 3)

            over_chunks(pe, None, (0, 0), lambda: [ml_prepare(0, 0, ph) for ph in MP], ml_body, ml_epilogue)

            def ff_turn(c, u):
                pe.wait_ge(F["x_norm"], c + 1)
                if not (isinstance(c, int) and c < 2):
                    pe.wait_ge(F["quant"], c - 1)
                for t in range(TPC):
                    mm = pe.transpose(psS[u][:, t * P:(t + 1) * P], xs[:, u, t * P:(t + 1) * P], ident)
                mm.then_inc(F["x_turned"], 1)

            def ff_body(c, u, more):
                if more:
                    ff_turn(c + 1, 1 - u)
                pe.wait_ge(F["quant"], c + 1)
                need(pe, F["taken"], c)
                for t in range(TPC):
                    mm = pe.matmul(psV[:, t * P:(t + 1) * P], xT[:, u, t * P:(t + 1) * P], ffT[:, :], start=True, stop=True)
                mm.then_inc(F["out"], 1)

            over_chunks(pe, None, (0, 0), lambda: ff_turn(0, 0), ff_body)
            attention(stages[1], wts[1])
            attention(stages[2], wts[2])

            def g_turn(c, u):
                pe.wait_ge(G["x_norm"], c + 1)
                if not (isinstance(c, int) and c < 2):
                    pe.wait_ge(G["x_up"], (c - 1) * 2)
                for t in range(TPC):
                    mm = pe.transpose(psS[u][:, t * P:(t + 1) * P], xs[:, u, t * P:(t + 1) * P], ident)
                mm.then_inc(G["x_turned"], 1)

            def g_body(c, u, more):
                if more:
                    g_turn(c + 1, 1 - u)
                pe.wait_ge(G["x_up"], (c + 1) * 2)
                need(pe, G["logit_up"], c)
                for t in range(TPC):
                    mm = pe.matmul(psX[:, t * NEXP:(t + 1) * NEXP], xT[:, u, t * P:(t + 1) * P], mog[:, :], start=True, stop=True)
                mm.then_inc(G["logit"], 1)

            over_chunks(pe, None, (0, 0), lambda: g_turn(0, 0), g_body)

            NU = NEXP * 3
            pe.wait_ge(G["w_in"], 32)

            def hidden(c, k, first):
                e, p = divmod(k, 3)
                n = c * NU + k
                m = HCS[p]
                if not (first and k < 2):
                    pe.wait_ge(G["hid"], n - 1)
                w = e * HID + HO[p]
                rhs = ctxT[:, bass.ts(c, CW)]
                pe.matmul(psS[k % 2][0:m, 0:CW], w1v[:, w:w + m], rhs, start=True, stop=True).then_inc(G["h1"], 1)
                pe.matmul(psS[k % 2][0:m, CW:2 * CW], w2v[:, w:w + m], rhs, start=True, stop=True).then_inc(G["h2"], 1)

            def down(c, e, first):
                n = c * NEXP + e
                pe.wait_ge(G["hid"], c * NU + 3 * e + 3)
                if not (first and e < 2):
                    pe.wait_ge(G["taken"], n - 1)
                for t in range(TPC):
                    for p in range(3):
                        m = HCS[p]
                        mm = pe.matmul(psT[:, (e % 2) * CW + t * P:(e % 2) * CW + (t + 1) * P],
                                       hid(e % 2, p)[0:m, t * P:(t + 1) * P], w3[0:m, (e * 3 + p) * P:(e * 3 + p + 1) * P],
                                       start=p == 0, stop=p == 2)
                mm.then_inc(G["out"], 1)

            def expert_chunk(c, first):
                for k in range(NU):
                    hidden(c, k, first)
                    if k >= 3 and k % 3 == 0:
                        down(c, k // 3 - 1, first)
                down(c, NEXP - 1, first)

            expert_chunk(0, True)
            with pe.Fori(1, NCH) as c:
                expert_chunk(c, False)

        @block.scalar
        def _(act):
            def attention(st, wt):
                s = S[st.name]

                def prepare(c, u, ph):
                    if ph == "v" or st.first and ph not in ("x", "ctx"):
                        return
                    act.wait_ge(s["mix_full"], st.prep(c, ph) + 1)
                    if ph == "x":
                        ins = act.copy(xT[:, u, :], psX[:, :])
                    elif ph == "ctx":
                        ins = act.copy(ctxT[:, bass.ts(c, CW)], psX[:, :])
                    elif ph[0] == "k":
                        h = int(ph[1])
                        if h == 0 and not (isinstance(c, int) and c < 2):
                            act.wait_ge(s[f"k_spread{u}"], of_parity(c - 2, u, 128))
                        o = W_CK + h * SEQ
                        ins = act.activation(kd[:, u, h, :], psX[:, :], ACT.Identity, bias=wt[:, o:o + 1])
                    else:
                        h = int(ph[1])
                        for b in range(2):
                            o = W_CQ + (h * 2 + b) * SEQ
                            ins = act.activation(
                                q[:, u, h, :].rearrange("p (t b k) -> p t b k", t=TPC, b=2)[:, :, b, :],
                                psX[:, :].rearrange("p (t b k) -> p t b k", t=TPC, b=2)[:, :, b, :],
                                ACT.Identity, bias=wt[:, o:o + 1], scale=cst[:, C_MB + b:C_MB + b + 1])
                    ins.then_inc(s["mix_free"], 1)

                def exps(c, i):
                    act.wait_ge(s["shifted"], c * st.steps + i + 1)
                    act.activation(prob[i % 2], prob[i % 2], ACT.Exp).then_inc(s["prob"], 1)

                def turned(n, i, early):
                    act.wait_ge(s["turned"], n + 1)
                    if not early:
                        act.wait_ge(s["ctx_full"], n - 1)
                    act.copy(probT[i % 2], psT[:, :]).then_inc(s["turned_out"], 1)

                def turned_back(u, i, use):
                    t = i % TPC
                    act.wait_ge(s["mix_full"], use + 1)
                    act.copy(q[:, u, :, t * P:(t + 1) * P], psX[:, 0:2 * P].rearrange("p (h k) -> p h k", h=2))\
                       .then_inc(s["mix_free"], 1)

                def body(c, u, more):
                    for i in range(st.steps):
                        behind(c, u, i, 3, st.steps, lambda n, uu, k: turned_back(uu, k, st.use(c, ("turn", i))))
                        behind(c, u, i, 1, st.steps, lambda n, uu, k: turned(n, k, is_first(c) and k < 2))
                        for at in range(2):
                            ph = st.slots.get((i, at))
                            if more and ph not in (None, "out"):
                                prepare(c + 1, 1 - u, ph)
                            if at == 0:
                                exps(c, i)

                def epilogue():
                    u, n = (NCH - 1) % 2, NCH * st.steps
                    turned_back(u, st.steps - 3, st.tail(0))
                    turned(n - 1, st.steps - 1, False)
                    turned_back(u, st.steps - 2, st.tail(1))
                    turned_back(u, st.steps - 1, st.tail(2))

                over_chunks(act, None, (0, 0), lambda: [prepare(0, 0, ph) for ph in st.phases], body, epilogue)

            act.wait_ge(zeroed, ZEROED)
            attention(stages[0], wts[0])


            def ml_prepare(c, u, ph):
                n = c * NP_ + MP.index(ph)
                if ph == "x":
                    act.wait_ge(M["mix_full"], n + 1)
                    act.copy(xT[:, u, :], psX[:, :]).then_inc(M["mix_free"], 1)
                elif ph == "pre":
                    act.wait_ge(M["gate_abs"], c + 1)
                    act.activation(flog, fabs, ACT.Exp).then_inc(M["gate_exp"], 1)
                    act.wait_ge(M["gate_exp"], c + 1)
                    act.activation(flog, flog, ACT.Ln, bias=1.0).then_inc(M["gate_ln"], 1)
                elif ph == "m":
                    act.wait_ge(M["nm"], c + 1)
                    act.activation(enm[u], enm[u], ACT.Exp).then_inc(M["enm"], TPC)

            def ml_turned(n, t, early):
                act.wait_ge(M["turned"], n + 1)
                if not early:
                    act.wait_ge(M["ctx_full"], n - 1)
                act.copy(probT[t % 2][:, 0:CW], psT[:, 0:CW]).then_inc(M["turned_out"], 1)

            def ml_decay(c, t):
                n = c * TPC + t
                act.wait_ge(M["score"], n + 1)
                if not (is_first(c) and t < 2):
                    act.wait_ge(M["turned"], n - 1)
                act.activation(prob[t % 2][:, 0:CW], psS[t % 2][:, CW:2 * CW], ACT.Exp).then_inc(M["decay"], 1)

            def ml_body(c, u, more):
                for i in range(TPC):
                    ml_decay(c, i)
                    behind(c, u, i, 1, TPC, lambda n, uu, k: ml_turned(n, k, is_first(c) and k < 2))
                    for ph in (("x",), ("pre",), (), ("m",))[i]:
                        if more:
                            ml_prepare(c + 1, 1 - u, ph)

            over_chunks(act, None, (0, 0), lambda: [ml_prepare(0, 0, ph) for ph in MP], ml_body,
                        lambda: ml_turned(NCH * TPC - 1, 3, False))
            attention(stages[1], wts[1])
            attention(stages[2], wts[2])

            def g_body(c, u):
                act.wait_ge(G["x_turned"], c + 1)
                act.copy(xT[:, u, :], psS[u][:, 0:CW]).then_inc(G["x_up"], 1)
                act.copy(ctxT[:, bass.ts(c, CW)], psS[u][:, 0:CW]).then_inc(G["x_up"], 1)

            g_body(0, 0)
            with act.Fori(0, 3) as it:
                for u in range(2):
                    g_body(it * 2 + (1 + u), (1 + u) % 2)
            g_body(NCH - 1, 1)
            act.wait_ge(G["shift"], 1)
            act.activation(gate[:, :, :], gate[:, :, :], ACT.Exp).then_inc(G["exp"], 1)
            NU = NEXP * 3

            def sils(c, first):
                for k in range(NU):
                    n = c * NU + k
                    m = HCS[k % 3]
                    act.wait_ge(G["h1"], n + 1)
                    if not (first and k < 2):
                        act.wait_ge(G["hid"], n - 1)
                    act.activation(sil(k % 2)[0:m, :], psS[k % 2][0:m, 0:CW], ACT.Silu).then_inc(G["sil"], 1)

            sils(0, True)
            with act.Fori(1, NCH) as c:
                sils(c, False)

        @block.vector
        def _(dve):
            dve.memset(kbd[1][:, :, :, :], 0.0).then_inc(zeroed, 1)
            dve.wait_ge(w_in, N_W)
            for i, st in enumerate(stages):
                dve.tensor_scalar(wts[i][:, W_K:W_V], wts[i][:, W_K:W_V], st.scale, None, ALU.mult).then_inc(scaled, 1)
            dve.tensor_tensor(mlw[:, 16:32], mlw[:, 16:32], mlw[:, 32:48], ALU.add).then_inc(scaled, 1)
            dve.tensor_scalar(fftf[:, :], fft[:, :], -1.0, None, ALU.add).then_inc(tern_f, 1)
            scale, finite = Chain(dve, scl_done), scl[:, 3:4]
            scale.link(dve.memset(scl[:, 1:3], 0.0))
            scale.link(dve.tensor_scalar(scl[:, 4:5], scl[:, 0:1], 1e-5, None, ALU.max))
            scale.link(dve.reciprocal(scl[:, 5:6], scl[:, 4:5]))
            scale.link(dve.tensor_scalar(scl[:, 6:7], scl[:, 4:5], FMAX, None, ALU.is_le))
            scale.link(dve.tensor_tensor(finite, scl[:, 0:1], scl[:, 0:1], ALU.is_equal))
            scale.link(dve.tensor_tensor(finite, finite, scl[:, 6:7], ALU.mult))
            scale.link(dve.copy_predicated(scl[:, 1:2], finite.bitcast(U32), scl[:, 4:5]))
            dve.copy_predicated(scl[:, 2:3], finite.bitcast(U32), scl[:, 5:6]).then_inc(scaled, 1)
            dve.wait_ge(tern_T, 1)
            dve.tensor_copy(ffT[:, :], psV[:, 0:P]).then_inc(scaled, 1)
            dve.wait_ge(zeroed, ZEROED)

            def normalise(c, u, s, prev):
                dve.wait_ge(prev, c + 1)
                if not (isinstance(c, int) and c < 2):
                    dve.wait_ge(s["x_kept"], c - 1)
                for t in range(TPC):
                    n = c * TPC + t
                    ins = dve.tensor_scalar(xs[:, u, t * P:(t + 1) * P], xres[:, n, :], mv[:, n, 0:1],
                                            rstd[:, bass.ts(n, 1)], ALU.subtract, ALU.mult)
                ins.then_inc(s["x_norm"], 1)

            def moments(chain, c, done):
                alone(dve)
                for t in range(TPC):
                    ins = dve.bn_stats(stats[:, t, :], xres[:, c * TPC + t, :])
                chain.link(ins)
                alone(dve)
                for t in range(TPC):
                    ins = dve.bn_aggr(mvs[:, t, :], stats[:, t, :])
                chain.link(ins)
                dve.tensor_scalar(mv[:, bass.ts(c, TPC), 0], mvs[:, :, 0], 0.0, None, ALU.add)
                dve.tensor_scalar(mv[:, bass.ts(c, TPC), 1], mvs[:, :, 1], LN_EPS, None, ALU.add).then_inc(done, 1)

            def values_out(u, wv, s):
                src = psX[:, :].rearrange("p (t b j d) -> p t b j d", t=TPC, b=2, j=8)
                for h2 in range(2):
                    rows = slice(h2 * SEQ, (h2 + 1) * SEQ)
                    for b in range(2):
                        o = h2 * 16 + b * 8
                        bv = wv[rows, h2 * SEQ:(h2 + 1) * SEQ].rearrange("p (j d) -> p j d", j=8)
                        ins = dve.tensor_tensor(vbd[rows, u, :, :, o:o + 8], src[rows, :, b, :, :],
                                                spread(bv.unsqueeze(1), [SEQ, TPC, 8, DH]), ALU.add)
                ins.then_inc(s["mix_free"], 1)

            def attention(st, wt, prev):
                s = S[st.name]
                chain = Chain(dve, s["dve"])

                def prepare(c, u, ph):
                    if ph == "norm" and not st.first:
                        normalise(c, u, s, prev)
                    if ph in ("norm", "x", "ctx") or not st.first and ph != "v":
                        return
                    dve.wait_ge(s["mix_full"], st.prep(c, ph) + 1)
                    if ph[0] == "k":
                        h = int(ph[1])
                        if h == 0 and not (isinstance(c, int) and c < 2):
                            dve.wait_ge(s[f"k_spread{u}"], of_parity(c - 2, u, 128))
                        ck = wt[:, W_CK + h * SEQ:W_CK + (h + 1) * SEQ]
                        dve.tensor_tensor(kd[:, u, h, :].rearrange("p (b k) -> p b k", b=8),
                                          psX[:, :].rearrange("p (b k) -> p b k", b=8),
                                          spread(ck.unsqueeze(1), [P, 8, SEQ]), ALU.add).then_inc(s["mix_free"], 1)
                    elif ph[0] == "q":
                        h = int(ph[1])
                        for b in range(2):
                            o = W_CQ + (h * 2 + b) * SEQ
                            cq = wt[:, o:o + SEQ]
                            ins = dve.scalar_tensor_tensor(
                                q[:, u, h, :].rearrange("p (t b k) -> p t b k", t=TPC, b=2)[:, :, b, :],
                                psX[:, :].rearrange("p (t b k) -> p t b k", t=TPC, b=2)[:, :, b, :],
                                cst[:, C_MB + b:C_MB + b + 1], spread(cq.unsqueeze(1), [P, TPC, SEQ]), ALU.mult, ALU.add)
                        ins.then_inc(s["mix_free"], 1)
                    else:
                        values_out(u, wt[:, W_BV:W_BV + P], s)

                def shift(c, i):
                    n = c * st.steps + i
                    sc = psS[i % 2][:, :].rearrange("p (h k) -> p h k", h=16)
                    dve.wait_ge(s["score"], n + 1)
                    chain.link(dve.tensor_reduce(rmax[i % 2], sc, AX.X, ALU.max))
                    if not (isinstance(c, int) and c == 0 and i < 2):
                        dve.wait_ge(s["turned"], n - 1)
                    dve.tensor_tensor(prob[i % 2].rearrange("p (h k) -> p h k", h=16), sc,
                                      spread(rmax[i % 2].unsqueeze(2), [P, 16, SEQ]), ALU.subtract).then_inc(s["shifted"], 1)

                def context(n, i):
                    dve.wait_ge(s["ctx_full"], n + 1)
                    pv = psV[:, 0:8 * 34].rearrange("p (j k) -> p j k", j=8)
                    chain.link(dve.reciprocal(recip.rearrange("p (j h) -> p j h", j=8), pv[:, :, 32:34]))
                    for b in range(2):
                        rows = slice(b * SEQ, (b + 1) * SEQ)
                        src = pv[rows, :, 0:32].rearrange("p j (h b d) -> p j h b d", h=2, b=2)[:, :, :, b, :]
                        dst = cn[rows, i % 2, :].rearrange("p (j h b d) -> p j h b d", j=8, h=2, b=2)[:, :, :, b, :]
                        rec = recip[rows, :].rearrange("p (j h) -> p j h", j=8).unsqueeze(3)
                        ins = dve.tensor_tensor(dst, src, spread(rec, [SEQ, 8, 2, DH]), ALU.mult)
                    ins.then_inc(s["ctx_done"], 1)

                def residual(c, use):
                    dve.wait_ge(s["x_kept"], c * 2 + 2 if st.first else c + 1)
                    dve.wait_ge(s["mix_full"], use + 1)
                    dve.tensor_tensor(xres[:, bass.ts(c, TPC), :], psX[:, :].rearrange("p (n d) -> p n d", n=TPC),
                                      xres[:, bass.ts(c, TPC), :], ALU.add).then_inc(s["mix_free"], 1)
                    dve.wait_ge(s["mix_free"], use + 1)
                    moments(chain, c, s["stat"])

                def slot(c, u, i, at, more):
                    ph = st.slots.get((i, at))
                    if ph == "out" and not is_first(c):
                        residual(c - 1, st.use(c, "out"))
                    elif ph not in (None, "out") and more:
                        prepare(c + 1, 1 - u, ph)

                def body(c, u, more):
                    for i in range(st.steps):
                        shift(c, i)
                        if i == 0 and more:
                            prepare(c + 1, 1 - u, "norm")
                        slot(c, u, i, 0, more)
                        behind(c, u, i, 2, st.steps, lambda n, uu, k: context(n, k))
                        slot(c, u, i, 1, more)

                def epilogue():
                    for d in (2, 1):
                        context(NCH * st.steps - d, st.steps - d)
                    residual(NCH - 1, st.tail(3))

                over_chunks(dve, chain, (2 * st.steps - 2, 2 * st.steps + 2),
                            lambda: [prepare(0, 0, ph) for ph in ["norm"] + st.phases], body, epilogue)

            attention(stages[0], wts[0], None)

            chain = Chain(dve, M["dve"])
            dve.wait_ge(S["a0"]["mix_full"], stages[0].prep(NCH - 1, "ctx") + 1)
            dve.memset(q[:, :, :, :], 0.0)
            dve.memset(vm[:, :, :, :, :], 0.0).then_inc(M["cum_up"], 1)
            dve.wait_ge(M["cum_up"], 1)
            for h2 in range(2):
                dve.memset(vm[h2 * SEQ:(h2 + 1) * SEQ, :, :, :, 64 + h2], 1.0)

            def ml_prepare(c, u, ph):
                n = c * NP_ + MP.index(ph) if ph in MP else None
                if ph == "norm":
                    normalise(c, u, M, S["a0"]["rstd"])
                if ph == "lf":
                    dve.wait_ge(M["gate_ln"], c + 1)
                    dve.scalar_tensor_tensor(lf, pre[:, :, 8:16], 0.0, flog, ALU.min, ALU.subtract).then_inc(M["gate_lf"], 1)
                if ph in ("norm", "lf", "x"):
                    return
                dve.wait_ge(M["mix_full"], n + 1)
                if ph == "v":
                    src = psX[:, :].rearrange("p (t b j d) -> p t b j d", t=TPC, b=2, j=4)
                    for h2 in range(2):
                        rows = slice(h2 * SEQ, (h2 + 1) * SEQ)
                        for b in range(2):
                            o = h2 * 32 + b * 16
                            ins = dve.tensor_copy(vm[rows, u, :, :, o:o + 16], src[rows, :, b, :, :])
                    ins.then_inc(M["mix_free"], 1)
                elif ph == "pre":
                    dve.tensor_tensor(pre, psX[:, 0:64].rearrange("p (t g) -> p t g", t=TPC),
                                      spread(mlw[:, 48:64].unsqueeze(1), [P, TPC, 16]), ALU.add).then_inc(M["mix_free"], 1)
                    dve.wait_ge(M["mix_free"], n + 1)
                    dve.scalar_tensor_tensor(fabs, pre[:, :, 8:16], -1.0, pre[:, :, 8:16], ALU.mult, ALU.min).then_inc(M["gate_abs"], 1)
                elif ph == "cum":
                    chain.link(dve.tensor_copy(cum, psX[:, 0:32]))
                    dve.tensor_tensor(agate.rearrange("p (t g) -> p t g", t=TPC), pre[:, :, 0:8],
                                      cum.rearrange("p (t g) -> p t g", t=TPC), ALU.subtract).then_inc(M["mix_free"], 1)
                elif ph == "a":
                    chain.link(dve.tensor_copy(aT, psX[0:32, 0:P]))
                    chain.link(dve.tensor_tensor_scan(MT, cst[0:32, C_RST:C_RST + P], aT, 0.0, ALU.add, ALU.max))
                    a4 = aT.rearrange("p (b k) -> p b k", b=2).unsqueeze(2)
                    d4 = cst[0:32, C_DEL:C_DEL + 8].unsqueeze(1).unsqueeze(3)
                    dve.tensor_tensor(abd[0:32, u, :, :, :], spread(a4, [32, 2, 8, SEQ]), spread(d4, [32, 2, 8, SEQ]),
                                      ALU.mult).then_inc(M["mix_free"], 1)
                else:
                    dve.tensor_scalar(negM[u], psX[:, 0:32].rearrange("p (t g) -> p t g", t=TPC), -1.0, None,
                                      ALU.mult).then_inc(M["mix_free"], 1)
                    dve.wait_ge(M["mix_free"], n + 1)
                    dve.tensor_tensor(enm[u], negM[u], cum.rearrange("p (t g) -> p t g", t=TPC), ALU.subtract)\
                       .then_inc(M["nm"], 1)

            def ml_ctx(n, u, t):
                hb = tmp[:, u, :].rearrange("p (t h d) -> p t h d", t=TPC, h=8)
                dve.wait_ge(M["ctx_full"], n + 1)
                pv = psV[:, 0:264].rearrange("p (j k) -> p j k", j=4)
                nr = nrm.rearrange("p (j k) -> p j k", j=4)
                if t == 0:
                    dve.wait_ge(M["enm"], n + 4)
                en = enm[u][:, t, :].rearrange("p (j k) -> p j k", j=4)
                chain.link(dve.scalar_tensor_tensor(nr, pv[:, :, 64:66], -1.0, en, ALU.mult, ALU.max))
                chain.link(dve.tensor_tensor(nr, pv[:, :, 64:66], nr, ALU.max))
                chain.link(dve.tensor_scalar(nrm, nrm, 1e-6, None, ALU.add))
                chain.link(dve.reciprocal(nrm, nrm))
                for b in range(2):
                    rows = slice(b * SEQ, (b + 1) * SEQ)
                    src = pv[rows, :, 0:64].rearrange("p j (h b d) -> p j h b d", h=2, b=2)[:, :, :, b, :]
                    rec = nrm[rows, :].rearrange("p (j h) -> p j h", j=4).unsqueeze(3)
                    ins = dve.tensor_tensor(hb[rows, t, :, :].rearrange("p (j h) d -> p j h d", j=4), src,
                                            spread(rec, [SEQ, 4, 2, 16]), ALU.mult)
                ins.then_inc(M["ctx_done"], 1)

            def ml_heads(c, u):
                hb3 = tmp[:, u, :].rearrange("p (g d) -> p g d", g=32)
                sq3 = tmp2[:, :].rearrange("p (g d) -> p g d", g=32)
                dve.wait_ge(M["ctx_done"], c * TPC + TPC)
                chain.link(dve.tensor_reduce(hmu, hb3, AX.X, ALU.add))
                chain.link(dve.tensor_scalar(hmu, hmu, 1.0 / 16, None, ALU.mult))
                chain.link(dve.tensor_tensor(hb3, hb3, head(hmu), ALU.subtract))
                chain.link(dve.tensor_tensor(sq3, hb3, hb3, ALU.mult))
                chain.link(dve.tensor_reduce(hvar, sq3, AX.X, ALU.add))
                dve.tensor_scalar(hvar, hvar, 1.0 / 16, 1e-6, ALU.mult, ALU.add).then_inc(M["var"], 1)

            def ml_moments(c):
                dve.wait_ge(M["summed"], c + 1)
                moments(chain, c, M["stat"])

            def ml_body(c, u, more):
                for i in range(TPC):
                    if more and i in (0, 2):
                        ml_prepare(c + 1, 1 - u, "lf" if i else "norm")
                    n = c * TPC + i
                    dve.wait_ge(M["decay"], n + 1)
                    dve.scalar_tensor_tensor(prob[i % 2][:, 0:CW], psS[i % 2][:, 0:CW], 0.25, prob[i % 2][:, 0:CW],
                                             ALU.mult, ALU.mult).then_inc(M["prod"], 1)
                    if more and (i, 0) in MSLOT:
                        ml_prepare(c + 1, 1 - u, MSLOT[i, 0])
                    behind(c, u, i, 2, TPC, ml_ctx)
                    if more and (i, 1) in MSLOT:
                        ml_prepare(c + 1, 1 - u, MSLOT[i, 1])
                    if i == 1 and not is_first(c):
                        ml_heads(c - 1, 1 - u)
                    if i == 3 and not is_first(c):
                        ml_moments(c - 1)

            def ml_epilogue():
                ml_ctx(NCH * TPC - 2, 1, 2)
                ml_ctx(NCH * TPC - 1, 1, 3)
                ml_heads(NCH - 1, 1)
                ml_moments(NCH - 1)

            over_chunks(dve, chain, (3 + 3 + 8, 3 + 16 + 5 + 2),
                        lambda: [ml_prepare(0, 0, ph) for ph in ("norm", "x", "pre", "lf", "cum", "v", "a", "m")],
                        ml_body, ml_epilogue)

            chain = Chain(dve, F["dve"])

            def ff_prepare(c, u):
                normalise(c, u, F, M["rstd"])
                dve.wait_ge(F["x_turned"], c + 1)
                qn = tmp[:, u, :]
                chain.link(dve.tensor_scalar(qn, psS[u][:, 0:CW], scl[:, 2:3], ROUND, ALU.mult, ALU.add))
                chain.link(dve.tensor_scalar(qn, qn, -ROUND, 127.0, ALU.add, ALU.min))
                dve.tensor_scalar(xT[:, u, :], qn, -127.0, scl[:, 1:2], ALU.max, ALU.mult).then_inc(F["quant"], 1)

            def ff_body(c, u, more):
                if more:
                    ff_prepare(c + 1, 1 - u)
                dve.wait_ge(F["x_kept"], c + 1)
                dve.wait_ge(F["out"], c + 1)
                dve.tensor_tensor(xres[:, bass.ts(c, TPC), :], psV[:, :].rearrange("p (n d) -> p n d", n=TPC),
                                  xres[:, bass.ts(c, TPC), :], ALU.add).then_inc(F["taken"], 1)
                dve.wait_ge(F["taken"], c + 1)
                moments(chain, c, F["stat"])

            over_chunks(dve, chain, (2 + 2 + 2, 2 + 2), lambda: ff_prepare(0, 0), ff_body)
            attention(stages[1], wts[1], F["rstd"])
            attention(stages[2], wts[2], S["a1"]["rstd"])

            chain = Chain(dve, G["dve"])

            def g_norm(c, u):
                dve.wait_ge(S["a2"]["rstd"], c + 1)
                if not (isinstance(c, int) and c < 2):
                    dve.wait_ge(G["x_turned"], c - 1)
                for t in range(TPC):
                    n = c * TPC + t
                    dve.tensor_scalar(xs[:, u, t * P:(t + 1) * P], xres[:, n, :], mv[:, n, 0:1],
                                      rstd[:, bass.ts(n, 1)], ALU.subtract, ALU.mult)
                    ins = dve.tensor_scalar(xres[:, n, :], xres[:, n, :], mv[:, n, 0:1],
                                            rstd[:, bass.ts(n, 1)], ALU.subtract, ALU.mult)
                ins.then_inc(G["x_norm"], 1)

            iota = spread(cst[:, C_IOTA:C_IOTA + 8].unsqueeze(1), [P, NT, NEXP])

            def each(a):
                return spread(a.unsqueeze(2), [P, NT, NEXP])

            def g_body(c, u, more):
                if more:
                    g_norm(c + 1, 1 - u)
                dve.wait_ge(G["logit"], c + 1)
                dve.tensor_copy(gl[:, bass.ts(c, TPC), :], psX[:, 0:32].rearrange("p (t g) -> p t g", t=TPC))\
                   .then_inc(G["logit_up"], 1)

            over_chunks(dve, None, (0, 0), lambda: g_norm(0, 0), g_body)
            dve.wait_ge(G["logit_up"], NCH)
            chain.link(dve.tensor_reduce(gm, gl, AX.X, ALU.max))
            chain.link(dve.tensor_tensor(g1, gl, each(gm), ALU.is_equal))
            dve.tensor_tensor(gate[:, :, :], gl, each(gm), ALU.subtract).then_inc(G["shift"], 1)
            chain.link(dve.tensor_tensor(g1, g1, iota, ALU.mult))
            chain.link(dve.tensor_reduce(gn, g1, AX.X, ALU.max))
            chain.link(dve.tensor_tensor(g1, iota, each(gn), ALU.is_equal))
            chain.link(dve.scalar_tensor_tensor(g2, g1, -1e30, gl, ALU.mult, ALU.add))
            chain.link(dve.tensor_reduce(gn, g2, AX.X, ALU.max))
            chain.link(dve.tensor_tensor(g2, g2, each(gn), ALU.is_equal))
            chain.link(dve.tensor_tensor(g2, g2, iota, ALU.mult))
            chain.link(dve.tensor_reduce(gn, g2, AX.X, ALU.max))
            chain.link(dve.tensor_tensor(g2, iota, each(gn), ALU.is_equal))
            chain.link(dve.tensor_tensor(g1, g1, g2, ALU.add))
            dve.wait_ge(G["exp"], 1)
            chain.link(dve.tensor_tensor(g1, g1, gate[:, :, :], ALU.mult))
            chain.link(dve.tensor_reduce(gn, g1, AX.X, ALU.add))
            chain.link(dve.reciprocal(gn, gn))
            chain.link(dve.tensor_tensor(gate[:, :, :], g1, each(gn), ALU.mult))

            NU = NEXP * 3
            fin = Chain(dve, G["fin"])

            def expert_chunk(c, first):
                def take(e):
                    dve.wait_ge(G["out"], c * NEXP + e + 1)
                    if not (first and e == 0):
                        dve.wait_ge(G["taken"], c * NEXP + e)
                    for t in range(TPC):
                        n = c * TPC + t
                        ins = dve.scalar_tensor_tensor(xres[:, n, :], psT[:, (e % 2) * CW + t * P:(e % 2) * CW + (t + 1) * P],
                                                       gate[:, n, e:e + 1], xres[:, n, :], ALU.mult, ALU.add)
                    ins.then_inc(G["taken"], 1)

                for k in range(NU):
                    n = c * NU + k
                    e, p = divmod(k, 3)
                    m = HCS[p]
                    dve.wait_ge(G["sil"], n + 1)
                    dve.wait_ge(G["h2"], n + 1)
                    if p == 0 and not (first and e < 2):
                        dve.wait_ge(G["out"], c * NEXP + e - 1)
                    dve.tensor_tensor(hid(e % 2, p)[0:m, :], sil(k % 2)[0:m, :], psS[k % 2][0:m, CW:2 * CW],
                                      ALU.mult).then_inc(G["hid"], 1)
                    if k >= 5 and k % 3 == 2:
                        take(k // 3 - 1)
                take(NEXP - 1)
                dve.wait_ge(G["taken"], (c + 1) * NEXP)
                moments(fin, c, G["var"])
                dve.wait_ge(G["rstd"], c + 1)
                for t in range(TPC):
                    n = c * TPC + t
                    ins = dve.tensor_scalar(xres[:, n, :], xres[:, n, :], mv[:, n, 0:1], rstd[:, bass.ts(n, 1)],
                                            ALU.subtract, ALU.mult)
                ins.then_inc(G["normed"], 1)

            fin.at(0)
            expert_chunk(0, True)
            with dve.Fori(1, NCH) as c:
                fin.at(c * 2)
                expert_chunk(c, False)


def kernel(**inputs):
    import numpy as np
    import ml_dtypes
    import concourse.bacc as bacc
    from concourse.bass_utils import run_bass_kernel_spmd

    i = {k: np.asarray(v) for k, v in inputs.items()}
    f32 = np.float32
    row_head = np.array([[(8 * half + 2 * (r // 32) + (r // 16) % 2) for r in range(P)] for half in range(2)])
    row_b = np.array([(r // 8) % 2 for r in range(P)])
    row_d = np.array([r % 8 for r in range(P)])
    col = [row_head[h] * 8 + row_d for h in range(2)]
    vcol = np.array([[(2 * j + h2) * 8 + d for j in range(8) for d in range(8)] for h2 in range(2)]).reshape(-1)

    def blob(wq, bq, wk, bk, wv, bv, wo, bo):
        b = np.zeros((P, W_N), f32)
        for h in range(2):
            b[:, W_Q + h * P:W_Q + (h + 1) * P] = wq[:, col[h]]
            b[:, W_K + h * P:W_K + (h + 1) * P] = wk[:, col[h]]
            b[:, W_CK + h * SEQ:W_CK + (h + 1) * SEQ] = bk[col[h]]
            b[:, W_O + h * P:W_O + (h + 1) * P] = wo[col[h]]
            for s in range(2):
                o = W_CQ + (2 * h + s) * SEQ
                mine = row_b == s
                b[mine, o:o + SEQ] = bq[col[h]][mine]
        b[:, W_V:W_V + P] = wv[:, vcol]
        b[:, W_BV:W_BV + P] = np.broadcast_to(bv[vcol], (P, P))
        b[:, W_BO:W_BO + P] = np.broadcast_to(bo, (P, P))
        return b

    def along(v):
        return np.broadcast_to(v[:, None], (P, SEQ))

    slopes = (2.0 ** (-8.0 * np.arange(1, 17) / 16)).astype(f32)
    pos = np.arange(SEQ, dtype=f32)
    wq = np.zeros((P, 16, 8), f32)
    wk = np.zeros((P, 16, 8), f32)
    wq[:, :, 0:4] = i["L0_attn_Wq"].reshape(P, 16, 4)
    wk[:, :, 0:4] = np.tile(i["L0_attn_Wk"], (1, 4)).reshape(P, 16, 4)
    qc = np.zeros((16, 8, SEQ), f32)
    kc = np.zeros((16, 8, SEQ), f32)
    qc[:, 4] = 1.0
    kc[:, 4] = slopes[:, None] * pos
    qc[:, 5] = -pos
    kc[:, 5] = slopes[:, None]
    b0 = blob(wq.reshape(P, P), qc.reshape(P, SEQ), wk.reshape(P, P), kc.reshape(P, SEQ),
              np.tile(i["L0_attn_Wv"], (1, 4)), np.zeros(P, f32), i["L0_attn_Wp"], i["L0_attn_bp"])
    qkv, bqkv = i["L1_attn_Wqkv_w"], i["L1_attn_Wqkv_b"]
    b1 = blob(qkv[0:P].T, along(bqkv[0:P]), qkv[P:2 * P].T, along(bqkv[P:2 * P]), qkv[2 * P:].T, bqkv[2 * P:],
              i["L1_attn_out_w"].T, i["L1_attn_out_b"])
    b2 = blob(i["L1_xattn_w_q"].T, along(i["L1_xattn_b_q"]), i["L1_xattn_w_k"].T, along(i["L1_xattn_b_k"]),
              i["L1_xattn_w_v"].T, i["L1_xattn_b_v"], i["L1_xattn_w_o"].T, i["L1_xattn_b_o"])

    ml = np.zeros((P, 48 + 16 + P), f32)
    for s in range(3):
        ml[:, 16 * s:16 * s + 8] = i["L0_xattn_igate_kernel"][P * s:P * (s + 1)]
        ml[:, 16 * s + 8:16 * s + 16] = i["L0_xattn_fgate_kernel"][P * s:P * (s + 1)]
    ml[:, 48:56] = i["L0_xattn_igate_bias"]
    ml[:, 56:64] = i["L0_xattn_fgate_bias"]
    ml[:, 64:] = i["L0_xattn_outnorm_weight"].reshape(-1)
    ffw = np.zeros((P, P + 1), f32)
    ffw[:, 0:P] = i["L0_ffn_bias"]

    r = np.arange(P)
    c = np.zeros((P, C_N), f32)
    c[:, C_ID:C_ID + P] = np.eye(P)
    c[:, C_MB] = row_b == 0
    c[:, C_MB + 1] = row_b == 1
    c[:, C_ONE:C_ONE + 32] = (r[:, None] // SEQ) == (np.arange(32)[None, :] // 16)
    c[:, C_CUM:C_CUM + P] = (r[:, None] <= r[None, :]) & (r[:, None] // SEQ == r[None, :] // SEQ)
    mcol = np.array([(2 * j + h2) * 16 + d for h2 in range(2) for j in range(4) for d in range(16)])
    c[mcol, C_PV + r] = 1.0
    for t in range(TPC):
        c[8 * t:8 * t + 8, C_SEL + t * SEQ:C_SEL + (t + 1) * SEQ] = 1.0
    c[0:32, C_DEL:C_DEL + 8] = (r[0:32, None] % 8) == np.arange(8)[None, :]
    c[:, C_RST:C_RST + P] = np.where(r % SEQ == 0, f32(-1e30), f32(0))
    c[:, C_HALF:C_HALF + 32] = -0.5
    c[:, C_IOTA:C_IOTA + 8] = 8 - np.arange(8)
    m16 = np.zeros((P, 256), f32)
    m16[:, 0:P] = -80.0 * np.eye(P)
    upper = np.arange(SEQ)[None, :] > (r % SEQ)[:, None]
    m16[:, P:P + SEQ] = 125.0 * upper
    m16[:, P + SEQ:P + 2 * SEQ] = 1e28 * upper
    m16 = m16.astype(ml_dtypes.bfloat16)

    w3 = np.zeros((HCS[0], NEXP, 3, P), f32)
    for p in range(3):
        w3[0:HCS[p], :, p] = i["L1_ffn_W3"][:, :, HO[p]:HO[p] + HCS[p]].transpose(2, 0, 1)
    arrays = {
        "x": i["x"].reshape(-1, P), "ctx": i["ctx_1024"].reshape(-1, P), "c32": c, "c16": m16,
        "w_a0": b0, "w_a1": b1, "w_a2": b2, "w_ml": ml, "w_ff": ffw,
        "w_tern": i["L0_ffn_ternary_weight"], "w_scale": np.broadcast_to(i["L0_ffn_act_scale"].reshape(1, 1), (P, 1)),
        "w_gate": i["L1_ffn_Wg"].T,
        "w_e1": i["L1_ffn_W1"].reshape(-1, P).T, "w_e2": i["L1_ffn_W2"].reshape(-1, P).T,
        "w_e3": w3.reshape(HCS[0], -1),
    }
    arrays = {k: np.ascontiguousarray(v) for k, v in arrays.items()}
    nc = bacc.Bacc("TRN2", target_bir_lowering=False, num_devices=1)
    a = {k: nc.dram_tensor(f"in_{k}", v.shape, mybir.dt.from_np(v.dtype), kind="ExternalInput").ap()
         for k, v in arrays.items()}
    o = nc.dram_tensor("out_0", (NT * P, P), F32, kind="ExternalOutput").ap()
    decoder(nc, a["x"], a["ctx"], a["c32"], a["c16"], [a["w_a0"], a["w_a1"], a["w_a2"]], a["w_ml"], a["w_ff"],
            a["w_tern"], a["w_scale"], a["w_gate"], a["w_e1"], a["w_e2"], a["w_e3"], o)
    res = run_bass_kernel_spmd(nc, [{f"in_{k}": v for k, v in arrays.items()}], core_ids=[0])
    return res.results[0]["out_0"].reshape(64, SEQ, P)
```

```python
from contextlib import ExitStack

import concourse.bass as bass
from concourse import mybir

ALU = mybir.AluOpType
ACT = mybir.ActivationFunctionType
AX = mybir.AxisListType
F32 = mybir.dt.float32
BF16 = mybir.dt.bfloat16
U32 = mybir.dt.uint32

P = 128
SEQ = 64
TPC = 4
CW = TPC * P
NCH = 8
NT = NCH * TPC
HALVES = 2
DH = 8
LN_EPS = 1e-5
ROUND = 12582912.0
FMAX = 3.4028234663852886e38
NEXP = 8
HID = 341
HCS = [114, 114, 113]
HO = [0, 114, 228]

C_ID, C_MB, C_CUM, C_PV, C_SEL, C_DEL, C_RST, C_HALF, C_IOTA = 0, 128, 130, 258, 386, 642, 650, 778, 810
C_N = 818
W_Q, W_CQ, W_K, W_CK, W_V, W_BV, W_O, W_BO, W_N = 0, 256, 512, 768, 896, 1024, 1152, 1408, 1536


def need(eng, sem, value):
    if isinstance(value, int) and value <= 0:
        return
    eng.wait_ge(sem, value)


def of_parity(c, u, each):
    return c * (each // 2) + (each - u * (each // 2))


def spread(ap, shape):
    return ap.broadcast_to(shape)


class Chain:

    def __init__(self, eng, sem):
        self.eng, self.sem, self.base, self.n = eng, sem, 0, 0

    def at(self, base):
        self.base, self.n = base, 0

    def link(self, ins):
        ins.then_inc(self.sem, 1)
        self.n += 1
        self.eng.wait_ge(self.sem, self.base + self.n)


def over_chunks(eng, chain, lens, prologue, body, epilogue=None):
    first, each = lens
    prologue()
    body(0, 0, True)
    if chain:
        assert chain.n == first, (chain.n, first)
    with eng.Fori(0, (NCH - 2) // 2) as it:
        for u in range(2):
            if chain:
                chain.at(it * (2 * each) + (u * each + first))
            body(it * 2 + (1 + u), (1 + u) % 2, True)
            if chain:
                assert chain.n == each, (chain.n, each)
    if chain:
        chain.at((NCH - 2) * each + first)
    body(NCH - 1, (NCH - 1) % 2, False)
    if epilogue:
        epilogue()


def behind(c, u, i, lag, steps, what):
    k = i - lag
    if k >= 0:
        what(c * steps + k, u, k)
    elif not is_first(c):
        what(c * steps + k, 1 - u, k + steps)


def before_next(prepare, *phases):
    if prepare:
        for ph in phases:
            prepare(0, 0, ph)


def is_first(c):
    return isinstance(c, int) and c == 0


MP = ["x", "pre", "cum", "a", "v", "m"]
NP_ = len(MP)
MSLOT = {(0, 1): "x", (1, 0): "pre", (2, 0): "cum", (2, 1): "a", (3, 0): "v", (3, 1): "m"}


class Attn:

    def __init__(self, name, reps, scale, mask, kv_ctx, first):
        self.name, self.reps, self.scale, self.mask, self.kv_ctx, self.first = name, reps, scale, mask, kv_ctx, first
        self.steps = reps * TPC
        self.on_dve = ("k0", "k1", "q0", "q1") if first else ("v",) if reps > 1 else ("v", "q1")
        self.phases = ["x"] + (["ctx"] if first else []) + ["k0", "k1", "v", "q0", "q1"]
        if reps > 1:
            self.slots = {(0, 1): "x", (1, 0): "k0", (2, 1): "out", (3, 0): "k1", (4, 0): "v", (5, 0): "q0", (6, 0): "q1"}
        else:
            self.slots = {(0, 1): "x", (1, 0): "k0", (1, 1): "k1", (2, 0): "v", (2, 1): "out", (3, 0): "q0", (3, 1): "q1"}
            if first:
                self.slots.update({(0, 0): "x", (0, 1): "ctx"})

        def order(prev, more):
            uses = []
            for i in range(self.steps):
                for at in (0, 1):
                    ph = self.slots.get((i, at))
                    if ph == "out" and prev or ph not in (None, "out") and more:
                        uses.append(ph)
            return uses
        self.orders = {"first": order(False, True), "mid": order(True, True), "last": order(True, False)}

    def base(self, c):
        n = len(self.phases)
        if is_first(c):
            return n
        return (c - 1) * len(self.orders["mid"]) + (n + len(self.orders["first"]))

    def use(self, c, key):
        kind = "first" if is_first(c) else "last" if isinstance(c, int) and c == NCH - 1 else "mid"
        return self.base(c) + self.orders[kind].index(key)

    def prep(self, c, phase):
        if is_first(c):
            return self.phases.index(phase)
        return self.use(c - 1, phase)

    def tail(self):
        return self.base(NCH - 1) + len(self.orders["last"])


def decoder(nc, x_in, ctx_in, c32, c16, attn_w, ml_w, ffn_w, ffn_t, ffn_s, moe_g, moe_w1, moe_w2, moe_w3, out):
    x_t = x_in.rearrange("(n p) d -> p n d", p=P)
    ctx_t = ctx_in.rearrange("(n p) d -> p n d", p=P)
    out_t = out.rearrange("(n p) d -> p n d", p=P)
    with ExitStack() as stack:
        def sb(name, shape, dt=F32):
            return stack.enter_context(nc.sbuf_tensor(name, shape, dt))

        def sem(name):
            return stack.enter_context(nc.semaphore(name))

        cst = sb("cst", [P, C_N])
        cmask = sb("cmask", [P, 256], BF16)
        wts = [sb(f"wts{i}", [P, W_N]) for i in range(3)]
        mlw = sb("mlw", [P, 48 + 16 + P])
        ffw = sb("ffw", [P, P + 1])
        fft = sb("fft", [P, P], mybir.dt.int32)
        fftf = sb("fftf", [P, P])
        ffT = sb("ffT", [P, P])
        scl = sb("scl", [P, 8])
        mog = sb("mog", [P, NEXP])
        w3 = sb("w3", [HCS[0], 3 * NEXP * P])
        xres = sb("xres", [P, NT, P])
        ctxT = sb("ctxT", [P, NT * P])
        xs = sb("xs", [P, 2, CW])
        xT = sb("xT", [P, 2, CW])
        kd = sb("kd", [P, 2, HALVES, CW])
        q = sb("q", [P, 2, HALVES, CW])
        kbd = [sb(f"kbd{i}", [P, HALVES, 8, CW]) for i in range(2)]
        vbd = sb("vbd", [P, 2, TPC, 8, 32])
        vm = sb("vm", [P, 2, TPC, 4, 66])
        work = sb("work", [P, 8 * CW])
        abd = q[:, :, :, :].rearrange("p u h k -> p u (h k)").rearrange("p u (b a k) -> p u b a k", b=2, a=8)
        gT = sb("gT", [P, 2 * P])
        tmp = sb("tmp", [P, 2, CW])
        tmp2 = sb("tmp2", [P, CW])
        small = sb("small", [P, 16 * 64])
        stats = sb("stats", [P, TPC, 6])
        spare = sb("spare", [P, 2])
        mvs = sb("mvs", [P, TPC, 2])
        mv = sb("mv", [P, NT, 2])
        rstd = sb("rstd", [P, NT])
        gate = sb("gate", [P, NT, NEXP])

        psS = [stack.enter_context(nc.psum_tensor(f"psS{i}", [P, 2 * CW], F32)) for i in range(2)]
        psT = stack.enter_context(nc.psum_tensor("psT", [P, 2 * CW], F32))
        psV = stack.enter_context(nc.psum_tensor("psV", [P, CW], F32))
        psX = stack.enter_context(nc.psum_tensor("psX", [P, CW], F32))

        bank_of = {"x": psX[:, :], "ctx": psS[0][:, 0:CW], "v": psS[0][:, CW:2 * CW], "q0": psS[1][:, 0:CW],
                   "q1": psS[1][:, CW:2 * CW], "k0": psT[:, 0:CW], "k1": psT[:, CW:2 * CW]}

        ident = cst[:, C_ID:C_ID + P]
        prob = [work[:, i * 2 * CW:(i + 1) * 2 * CW] for i in range(2)]
        probT = [work[:, (2 + i) * 2 * CW:(3 + i) * 2 * CW] for i in range(2)]

        def cols(a, n):
            return small[:, a:a + n]
        rmax = [cols(16 * i, 16) for i in range(2)]
        recip = [cols(32 + 16 * i, 16) for i in range(2)]

        w1v = kbd[0][:, :, :, :].rearrange("p a b c -> p (a b c)")[:, 0:NEXP * HID]
        w2v = kbd[1][:, :, :, :].rearrange("p a b c -> p (a b c)")[:, 0:NEXP * HID]
        ZEROED = 4

        pre = cols(320, 64).rearrange("p (t g) -> p t g", t=TPC)
        fabs = cols(384, 32).rearrange("p (t g) -> p t g", t=TPC)
        flog = cols(416, 32).rearrange("p (t g) -> p t g", t=TPC)
        lf = cols(448, 32).rearrange("p (t g) -> p t g", t=TPC)
        cum = cols(480, 32)
        agate = cols(512, 32)
        negM = [cols(544 + 32 * i, 32).rearrange("p (t g) -> p t g", t=TPC) for i in range(2)]
        enm = [cols(608 + 32 * i, 32).rearrange("p (t g) -> p t g", t=TPC) for i in range(2)]
        aT = gT[0:32, 0:P]
        MT = gT[0:32, P:2 * P]
        nrm = cols(672, 8)
        hmu = cols(680, 32)
        hvar = cols(712, 32)
        hrs = cols(744, 32)
        def ofkeys(a):
            keys = kd[:, :, :, :].rearrange("p u h k -> p (u h k)")
            return keys[:, a:a + NT * NEXP].rearrange("p (t g) -> p t g", t=NT)
        gl, g1, g2 = (ofkeys(k * NT * NEXP) for k in range(3))
        gm, gn = cols(776, NT), cols(776 + NT, NT)

        def head(a):
            return spread(a.unsqueeze(2), [P, 32, 16])

        def hid(par, p):
            return work[:, (3 * par + p) * CW:(3 * par + p + 1) * CW]

        def sil(par):
            return work[:, (6 + par) * CW:(7 + par) * CW]

        kvst = [kd[:, i, 0, :] for i in range(2)]
        ctx_st = [vm[:, i, :, :, :].rearrange("p t j k -> p (t j k)")[:, 0:CW] for i in range(2)]


        w_first = sem("w_first")
        w_in = sem("w_in")
        zeroed = sem("zeroed")
        scaled = sem("scaled")
        w_scaled = sem("w_scaled")
        scl_done = sem("scl_done")
        scl_up = sem("scl_up")
        tern_f = sem("tern_f")
        tern_T = sem("tern_T")
        N_W = 16 * 8

        stages = [Attn("a0", 1, 0.5, 1, False, True),
                  Attn("a1", 3, 8 ** -0.5, 0, False, False),
                  Attn("a2", 1, 8 ** -0.5, None, True, False)]
        S = {}
        for st in stages:
            S[st.name] = {k: sem(f"{st.name}_{k}") for k in (
                "x_in0", "x_in1", "staged", "x_norm", "x_kept", "mix_full", "mix_free", "k_spread0", "k_spread1", "score", "shifted", "prob",
                "recip", "scaled", "turned", "turned_out", "ctx_full", "ctx_done", "stat", "rstd", "dve")}
        M = {k: sem(f"m_{k}") for k in (
            "x_norm", "x_kept", "mix_full", "mix_free", "k_spread0", "k_spread1", "gate_abs", "gate_exp", "gate_ln", "gate_lf",
            "score", "decay", "prod", "turned", "turned_out", "ctx_full", "ctx_done", "nm", "enm", "staged", "ones",
            "pool", "summed", "stat", "rstd", "dve", "var")}
        F = {k: sem(f"f_{k}") for k in (
            "x_norm", "x_kept", "x_turned", "quant", "out", "taken", "stat", "rstd", "dve")}
        G = {k: sem(f"g_{k}") for k in (
            "x_norm", "x_kept", "x_turned", "x_up", "logit", "logit_up", "shift", "exp", "w_in", "h1", "sil", "h2", "hid",
            "out", "taken", "var", "rstd", "dve", "normed", "stored", "fin")}

        block = stack.enter_context(nc.Block())

        def alone(dve):
            dve.memset(spare[:, 0:1], 0.0)

        @block.sync
        def _(sp):
            for dst, src in ((cst, c32), (wts[0], attn_w[0]), (cmask, c16)):
                sp.dma_start(dst[:, :], src).then_inc(w_first, 16)

            raw = [vm[:, i, :, :, :].rearrange("p t j k -> p (t j k)")[:, 0:CW].rearrange("p (n d) -> p n d", n=TPC)
                   for i in range(2)]

            def keys(st, c, u):
                s = S[st.name]
                need(sp, s["score"], c * (2 * st.steps) - 2 * st.steps)
                sp.wait_ge(s["mix_free"], st.prep(c, "k1") + 1)
                for hh in range(8):
                    rows = slice(16 * hh, 16 * hh + 16)
                    sp.dma_start(kbd[u][rows, :, hh, :], kd[rows, u, :, :]).then_inc(s[f"k_spread{u}"], 16)

            def load(st, c, u):
                s = S[st.name]
                if not (isinstance(c, int) and c < 2):
                    sp.wait_ge(s["mix_full"], st.prep(c - 2, "ctx") + 1)
                    sp.wait_ge(s["x_kept"], c * 2 - 2)
                sp.dma_start(xs[:, u, :].rearrange("p (n d) -> p n d", n=TPC),
                             x_t[:, bass.ts(c, TPC), :]).then_inc(s[f"x_in{u}"], 16)
                sp.dma_start(raw[u], ctx_t[:, bass.ts(c, TPC), :]).then_inc(s[f"x_in{u}"], 16)

            st = stages[0]
            load(st, 0, 0)
            load(st, 1, 1)
            for dst, src in ((wts[1], attn_w[1]), (wts[2], attn_w[2]), (mlw, ml_w), (ffw, ffn_w), (fft, ffn_t), (mog, moe_g), (w3, moe_w3)):
                sp.dma_start(dst[:, :], src).then_inc(w_in, 16)
            sp.dma_start(scl[:, 0:1], ffn_s).then_inc(w_in, 16)
            sp.wait_ge(zeroed, ZEROED)
            keys(st, 0, 0)
            load(st, 2, 0)
            keys(st, 1, 1)
            load(st, 3, 1)
            keys(st, 2, 0)
            with sp.Fori(0, (NCH - 4) // 2) as it:
                for u in range(2):
                    load(st, it * 2 + (4 + u), u)
                    keys(st, it * 2 + (3 + u), 1 - u)
            keys(st, NCH - 1, 1)

            sp.wait_ge(S["a0"]["score"], 2 * stages[0].steps * NCH)

            def ml_keys(c, u):
                need(sp, M["score"], (c - 1) * TPC)
                for h in range(8):
                    rows = slice(16 * h, 16 * h + 16)
                    sp.dma_start(kbd[u][rows, 0, h, :], ctxT[rows, bass.ts(c, CW)]).then_inc(M[f"k_spread{u}"], 16)

            sp.wait_ge(S["a0"]["mix_free"], stages[0].prep(NCH - 1, "ctx") + 1)
            over_chunks(sp, None, (0, 0), lambda: ml_keys(0, 0),
                        lambda c, u, more: ml_keys(c + 1, 1 - u) if more else None)
            for st, before, n in ((stages[1], M["score"], TPC), (stages[2], S["a1"]["score"], 2 * stages[1].steps)):
                sp.wait_ge(before, n * (NCH - 1))
                keys(st, 0, 0)
                sp.wait_ge(before, n * NCH)
                over_chunks(sp, None, (0, 0), lambda: None,
                            lambda c, u, more: keys(st, c + 1, 1 - u) if more else None)
            sp.wait_ge(S["a2"]["score"], 2 * stages[2].steps * NCH)
            sp.dma_start(w1v, moe_w1).then_inc(G["w_in"], 16)
            sp.dma_start(w2v, moe_w2).then_inc(G["w_in"], 16)

            def store(c):
                sp.wait_ge(G["normed"], c + 1)
                sp.dma_start(out_t[:, bass.ts(c, TPC), :],
                             xres[:, bass.ts(c, TPC), :]).then_inc(G["stored"], 16)

            with sp.Fori(0, NCH) as c:
                store(c)
            sp.wait_ge(G["stored"], 16 * NCH)

        @block.gpsimd
        def _(g):
            for ap in (vbd[:, :, :, :, :], gT[:, :], kbd[1][:, :, :, :]):
                g.memset(ap, 0.0).then_inc(zeroed, 1)
            g.wait_ge(w_first, 48)

            def rstd_of(c, stat, done):
                g.wait_ge(stat, c + 1)
                g.tensor_tensor(rstd[:, bass.ts(c, TPC)], mv[:, bass.ts(c, TPC), 1], cst[:, C_HALF:C_HALF + TPC],
                                ALU.pow).then_inc(done, 1)

            def keep(c, u, s, bias):
                g.wait_ge(s["x_norm"], c + 1)
                dst = xres[:, bass.ts(c, TPC), :]
                src = xs[:, u, :].rearrange("p (n d) -> p n d", n=TPC)
                if bias is None:
                    g.tensor_copy(dst, src).then_inc(s["x_kept"], 1)
                else:
                    g.tensor_tensor(dst, src, spread(bias.unsqueeze(1), [P, TPC, P]), ALU.add).then_inc(s["x_kept"], 1)

            def stage(c, u, dst, free, done):
                if free is not None:
                    g.wait_ge(*free)
                g.tensor_copy(dst[u], ctxT[:, bass.ts(c, CW)]).then_inc(done, 1)

            def later_weights():
                g.wait_ge(w_in, N_W)
                for i in (1, 2):
                    g.tensor_scalar(wts[i][:, W_K:W_V], wts[i][:, W_K:W_V], stages[i].scale, None, ALU.mult).then_inc(scaled, 1)
                g.tensor_tensor(mlw[:, 16:32], mlw[:, 16:32], mlw[:, 32:48], ALU.add).then_inc(scaled, 1)
                g.tensor_scalar(fftf[:, :], fft[:, :], -1.0, None, ALU.add).then_inc(tern_f, 1)
                g.wait_ge(tern_f, 1)

            def values_place():
                g.wait_ge(S["a0"]["mix_full"], stages[0].prep(NCH - 1, "ctx") + 1)
                g.memset(vm[:, :, :, :, :], 0.0).then_inc(M["ones"], 1)
                g.wait_ge(M["ones"], 1)
                for h2 in range(2):
                    g.memset(vm[h2 * SEQ:(h2 + 1) * SEQ, :, :, :, 64 + h2], 1.0).then_inc(M["ones"], 1)
                g.wait_ge(M["ones"], 3)

            def attn_start(st, wt):
                if st.kv_ctx:
                    stage(0, 0, ctx_st, None, S[st.name]["staged"])
                keep(0, 0, S[st.name], wt[:, W_BO:W_BO + P])

            def attention(st, wt, start_next=None):
                s = S[st.name]
                bias = wt[:, W_BO:W_BO + P]

                def prologue():
                    if st.first:
                        keep_first(0, 0)

                def keep_first(c, u):
                    g.wait_ge(s[f"x_in{u}"], of_parity(c, u, 32))
                    g.tensor_tensor(xres[:, bass.ts(c, TPC), :], xs[:, u, :].rearrange("p (n d) -> p n d", n=TPC),
                                    spread(bias.unsqueeze(1), [P, TPC, P]), ALU.add).then_inc(s["x_kept"], 2)

                def divide(n, i):
                    g.wait_ge(s["recip"], n + 1)
                    for h in range(HALVES):
                        p = prob[i % 2][:, h * CW:(h + 1) * CW].rearrange("p (a k) -> p a k", a=8)
                        g.tensor_tensor(p, p, spread(recip[i % 2][:, 8 * h:8 * h + 8].unsqueeze(2), [P, 8, SEQ]),
                                        ALU.mult).then_inc(s["scaled"], 1)

                def body(c, u, more):
                    for i in range(st.steps):
                        behind(c, u, i, 1, st.steps, lambda n, uu, k: divide(n, k))
                        if i == 0 and more:
                            if st.first:
                                keep_first(c + 1, 1 - u)
                            else:
                                if st.kv_ctx:
                                    stage(c + 1, 1 - u, ctx_st, None if is_first(c) else (s["mix_full"], st.base(c)), s["staged"])
                                keep(c + 1, 1 - u, s, bias)
                        if i == 3 and not is_first(c):
                            rstd_of(c - 1, s["stat"], s["rstd"])
                        if i == 3 and st.first and is_first(c):
                            later_weights()
                        if i == 2 and st.first and not more:
                            values_place()

                def epilogue():
                    divide(NCH * st.steps - 1, st.steps - 1)
                    if start_next:
                        start_next()
                    rstd_of(NCH - 1, s["stat"], s["rstd"])

                over_chunks(g, None, (0, 0), prologue, body, epilogue)

            def ml_start():
                g.wait_ge(S["a0"]["mix_free"], stages[0].prep(NCH - 1, "ctx") + 1)
                for u in range(2):
                    g.wait_ge(S["a0"][f"k_spread{u}"], 128 * NCH // 2)
                stage(0, 0, kvst, None, M["staged"])
                keep(0, 0, M, None)

            attention(stages[0], wts[0], ml_start)

            chain = Chain(g, M["pool"])

            def ml_finish(c, u):
                hb3 = tmp[:, u, :].rearrange("p (g d) -> p g d", g=32)
                h3 = tmp[:, u, :].rearrange("p (t d) -> p t d", t=TPC)
                g.wait_ge(M["var"], c + 1)
                chain.link(g.tensor_tensor(hrs, hvar, cst[:, C_HALF:C_HALF + 32], ALU.pow))
                chain.link(g.tensor_tensor(hb3, hb3, head(hrs), ALU.mult))
                chain.link(g.tensor_tensor(h3, h3, spread(mlw[:, 64:64 + P].unsqueeze(1), [P, TPC, P]), ALU.mult))
                g.wait_ge(M["x_kept"], c + 1)
                g.tensor_tensor(xres[:, bass.ts(c, TPC), :], h3, xres[:, bass.ts(c, TPC), :], ALU.add).then_inc(M["summed"], 1)
                rstd_of(c, M["stat"], M["rstd"])

            def ml_body(c, u, more):
                if more:
                    stage(c + 1, 1 - u, kvst, None if is_first(c) else (M["mix_full"], (c + 1) * NP_), M["staged"])
                    keep(c + 1, 1 - u, M, None)
                if not is_first(c):
                    ml_finish(c - 1, 1 - u)

            over_chunks(g, chain, (0, 3), lambda: None,
                        ml_body)

            def ff_body(c, u, more):
                if more:
                    keep(c + 1, 1 - u, F, ffw[:, 0:P])
                rstd_of(c, F["stat"], F["rstd"])

            over_chunks(g, None, (0, 0), lambda: [keep(0, 0, F, ffw[:, 0:P]), ml_finish(NCH - 1, 1)], ff_body)
            attn_start(stages[1], wts[1])
            attention(stages[1], wts[1], lambda: attn_start(stages[2], wts[2]))
            attention(stages[2], wts[2], lambda: keep(0, 0, G, None))
            over_chunks(g, None, (0, 0), lambda: None,
                        lambda c, u, more: keep(c + 1, 1 - u, G, None) if more else None)
            with g.Fori(0, NCH) as c:
                rstd_of(c, G["var"], G["rstd"])

        @block.tensor
        def _(pe):
            pe.wait_ge(w_first, 48)

            def turn_chunk(src, bank=psX):
                for t in range(TPC):
                    mm = pe.transpose(bank[:, t * P:(t + 1) * P], src[:, t * P:(t + 1) * P], ident)
                return mm

            def values(src, wv, bank=psX):
                for t in range(TPC):
                    for h2 in range(2):
                        for b in range(2):
                            o = t * P + b * SEQ
                            mm = pe.matmul(bank[h2 * SEQ:(h2 + 1) * SEQ, o:o + SEQ], src[:, o:o + SEQ],
                                           wv[:, h2 * SEQ:(h2 + 1) * SEQ], start=True, stop=True)
                return mm

            def preparer(st, wt):
                s = S[st.name]

                def prepare(c, u, ph, own=False):
                    bank = bank_of[ph] if own else psX
                    if not own:
                        need(pe, s["mix_free"], st.prep(c, ph))
                    elif ph[0] == "k":
                        pe.wait_ge(s["mix_free"], 1)
                    elif ph == "v":
                        pe.wait_ge(s["mix_free"], st.prep(0, "k1") + 1)
                    if ph == "x":
                        if st.first:
                            pe.wait_ge(s[f"x_in{u}"], of_parity(c, u, 32))
                        else:
                            pe.wait_ge(s["x_norm"], c + 1)
                        mm = turn_chunk(xs[:, u, :], bank)
                    elif ph == "ctx":
                        mm = turn_chunk(ctx_st[u], bank)
                    elif ph[0] in "kq":
                        if st.first and ph[0] == "k" and is_first(c):
                            pe.wait_ge(w_scaled, 1)
                        w = (W_K if ph[0] == "k" else W_Q) + P * int(ph[1])
                        src = ctxT[:, bass.ts(c, CW)] if st.kv_ctx and ph[0] == "k" else xT[:, u, :]
                        mm = pe.matmul(bank[:, :], wt[:, w:w + P], src, start=True, stop=True)
                    else:
                        if st.kv_ctx:
                            pe.wait_ge(s["staged"], c + 1)
                        mm = values(ctx_st[u] if st.kv_ctx else xT[:, u, :], wt[:, W_V:W_V + P], bank)
                    mm.then_inc(s["mix_full"], 1)

                return prepare

            def attention(st, wt, begun=False, nxt=None):
                s, prepare = S[st.name], preparer(st, wt)
                ready, phase = (nxt[1], nxt[2]) if nxt else (None, [None] * 6)

                def score(c, u, i):
                    n = c * st.steps + i
                    r, t = divmod(i, TPC)
                    if not (is_first(c) and i < 2):
                        pe.wait_ge(s["prob"], n - 1)
                    bank = psS[i % 2]
                    if is_first(c) and i == 0:
                        pe.wait_ge(s["mix_free"], len(st.phases))
                    if st.mask is not None:
                        m = cmask[:, P + SEQ * st.mask:P + SEQ * (st.mask + 1)]
                        for h in range(HALVES):
                            pe.matmul(bank[:, h * CW:(h + 1) * CW].rearrange("p (a k) -> p a k", a=8), cmask[:, 0:P],
                                      spread(m.unsqueeze(1), [P, 8, SEQ]), start=True, stop=False,
                                      skip_group_check=True)
                    if r:
                        pe.wait_ge(s["ctx_done"], n - 3)
                    if i == 0:
                        pe.wait_ge(s[f"k_spread{u}"], of_parity(c, u, 128))
                    for h in range(HALVES):
                        if i == 0:
                            pe.wait_ge(s["mix_free"], st.prep(c, f"q{h}") + 1)
                        for b in range(2):
                            o = t * P + b * SEQ
                            mm = pe.matmul(bank[b * SEQ:(b + 1) * SEQ, h * CW:(h + 1) * CW].rearrange("p (a k) -> p a k", a=8),
                                           q[:, u, h, o:o + SEQ], kbd[u][:, h, :, o:o + SEQ],
                                           start=st.mask is None, stop=True, skip_group_check=True)
                        mm.then_inc(s["score"], 1)

                def turn(n, i):
                    need(pe, s["turned_out"], n)
                    for j in range(8):
                        if j % 4 == 0:
                            pe.wait_ge(s["scaled"], n * 2 + (1 + j // 4))
                        mm = pe.transpose(psT[:, j * P:(j + 1) * P], prob[i % 2][:, j * P:(j + 1) * P], ident)
                    mm.then_inc(s["turned"], 1)

                def mix(n, u, i, c=None):
                    if i == 0:
                        pe.wait_ge(s["mix_free"], st.prep(c, "v") + 1)
                    pe.wait_ge(s["turned_out"], n + 1)
                    need(pe, s["ctx_done"], n)
                    for h in range(HALVES):
                        for j4 in range(4):
                            j = 4 * h + j4
                            mm = pe.matmul(psV[32 * j4:32 * (j4 + 1), h * P:(h + 1) * P], vbd[:, u, i % TPC, j, :],
                                           probT[i % 2][:, j * P:(j + 1) * P], start=True, stop=True,
                                           tile_position=(0, 32 * j4), skip_group_check=True)
                    mm.then_inc(s["ctx_full"], 1)

                def project(u, steps, use):
                    need(pe, s["mix_free"], use)
                    pe.wait_ge(s["ctx_done"], steps)
                    for t in range(TPC):
                        for h in range(HALVES):
                            mm = pe.matmul(psX[:, t * P:(t + 1) * P], q[:, u, h, t * P:(t + 1) * P],
                                           wt[:, W_O + h * P:W_O + (h + 1) * P], start=h == 0, stop=h == 1)
                    mm.then_inc(s["mix_full"], 1)

                def slot(c, u, i, at, more):
                    ph = st.slots.get((i, at))
                    if ph == "out" and not is_first(c):
                        project(1 - u, c * st.steps, st.use(c, "out"))
                    elif ph not in (None, "out") and more:
                        prepare(c + 1, 1 - u, ph)

                def body(c, u, more):
                    for i in range(st.steps):
                        score(c, u, i)
                        behind(c, u, i, 3, st.steps, lambda n, uu, k: mix(n, uu, k, c))
                        slot(c, u, i, 0, more)
                        behind(c, u, i, 2, st.steps, lambda n, uu, k: turn(n, k))
                        slot(c, u, i, 1, more)

                def epilogue():
                    u, n = (NCH - 1) % 2, NCH * st.steps
                    if nxt:
                        pe.wait_ge(s["mix_free"], st.tail())
                    before_next(ready, phase[0])
                    mix(n - 3, u, st.steps - 3)
                    before_next(ready, phase[1])
                    for d in (2, 1):
                        turn(n - d, st.steps - d)
                        mix(n - d, u, st.steps - d)
                        before_next(ready, phase[4 - d])
                    if nxt:
                        pe.wait_ge(nxt[0]["mix_free"], 4)
                    project(u, n, st.tail())
                    if nxt:
                        pe.wait_ge(s["mix_free"], st.tail() + 1)
                    before_next(ready, phase[4], phase[5])

                over_chunks(pe, None, (0, 0), lambda: [prepare(0, 0, ph, True) for ph in st.phases if not begun], body, epilogue)

            def ml_prepare(c, u, ph):
                n = c * NP_ + MP.index(ph)
                need(pe, M["mix_free"], n)
                if ph == "x":
                    pe.wait_ge(M["x_norm"], c + 1)
                    mm = turn_chunk(xs[:, u, :])
                elif ph == "v":
                    mm = values(kvst[u], cst[:, C_PV:C_PV + P])
                elif ph == "pre":
                    if is_first(c):
                        pe.wait_ge(scaled, 3)
                    pe.wait_ge(M["staged"], c + 1)
                    for t in range(TPC):
                        o = psX[:, t * 16:(t + 1) * 16]
                        pe.matmul(o, xT[:, u, t * P:(t + 1) * P], mlw[:, 0:16], start=True, stop=False)
                        mm = pe.matmul(o, kvst[u][:, t * P:(t + 1) * P], mlw[:, 16:32], start=False, stop=True)
                elif ph == "cum":
                    pe.wait_ge(M["gate_lf"], c + 1)
                    mm = pe.matmul(psX[:, 0:32], cst[:, C_CUM:C_CUM + P], lf.rearrange("p t g -> p (t g)"), start=True, stop=True)
                elif ph == "a":
                    mm = pe.transpose(psX[0:32, 0:P], agate, ident)
                else:
                    mm = pe.transpose(psX[:, 0:P], gT[:, P:2 * P], ident)
                mm.then_inc(M["mix_full"], 1)

            attention(stages[0], wts[0], nxt=(M, ml_prepare, MP))

            def ml_score(c, u, t):
                n = c * TPC + t
                if not (isinstance(c, int) and c == 0 and t < 2):
                    pe.wait_ge(M["prod"], n - 1)
                if t == 0:
                    pe.wait_ge(M["mix_free"], (c + 1) * NP_ - 2)
                    pe.wait_ge(M[f"k_spread{u}"], of_parity(c, u, 128))
                bank = psS[t % 2]
                qk = bank[:, 0:CW]
                dec = bank[:, CW:2 * CW].rearrange("p (a k) -> p a k", a=8)
                m = cmask[:, P + SEQ:P + 2 * SEQ]
                for b in range(2):
                    o = t * P + b * SEQ
                    pe.matmul(bank[b * SEQ:(b + 1) * SEQ, 0:CW].rearrange("p (a k) -> p a k", a=8),
                              xT[:, u, o:o + SEQ], kbd[u][:, 0, :, o:o + SEQ], start=True, stop=True,
                              skip_group_check=True)
                pe.matmul(dec, cmask[:, 0:P], spread(m.unsqueeze(1), [P, 8, SEQ]), start=True, stop=False, skip_group_check=True)
                for b in range(2):
                    pe.matmul(bank[b * SEQ:(b + 1) * SEQ, CW:2 * CW].rearrange("p (a k) -> p a k", a=8),
                              cst[0:32, C_SEL + t * SEQ:C_SEL + (t + 1) * SEQ], abd[0:32, u, b, :, :], start=False, stop=False,
                              skip_group_check=True)
                if t == 0:
                    pe.wait_ge(M["mix_free"], (c + 1) * NP_)
                mm = pe.matmul(dec, ident, spread(negM[u][:, t, :].unsqueeze(2), [P, 8, SEQ]), start=False, stop=True,
                          skip_group_check=True)
                mm.then_inc(M["score"], 1)

            def ml_turn(n, t):
                pe.wait_ge(M["prod"], n + 1)
                need(pe, M["turned_out"], n)
                for j in range(4):
                    mm = pe.transpose(psT[:, j * P:(j + 1) * P], prob[t % 2][:, j * P:(j + 1) * P], ident)
                mm.then_inc(M["turned"], 1)

            def ml_mix(n, u, t):
                pe.wait_ge(M["turned_out"], n + 1)
                need(pe, M["ctx_done"], n)
                for j in range(4):
                    mm = pe.matmul(psV[:, j * 66:(j + 1) * 66], probT[t % 2][:, j * P:(j + 1) * P], vm[:, u, t, j, :],
                                   start=True, stop=True)
                mm.then_inc(M["ctx_full"], 1)

            def ml_body(c, u, more):
                for i in range(TPC):
                    ml_score(c, u, i)
                    behind(c, u, i, 1, TPC, lambda n, uu, k: ml_turn(n, k))
                    if more and (i, 0) in MSLOT:
                        ml_prepare(c + 1, 1 - u, MSLOT[i, 0])
                    behind(c, u, i, 2, TPC, ml_mix)
                    if more and (i, 1) in MSLOT:
                        ml_prepare(c + 1, 1 - u, MSLOT[i, 1])

            def ml_epilogue():
                n = NCH * TPC
                ml_turn(n - 1, 3)
                ml_mix(n - 2, 1, 2)
                ml_mix(n - 1, 1, 3)

            over_chunks(pe, None, (0, 0), lambda: None, ml_body, ml_epilogue)

            pe.wait_ge(tern_f, 1)
            pe.wait_ge(M["mix_free"], NCH * NP_)
            pe.transpose(psX[:, 0:P], fftf[:, :], ident).then_inc(tern_T, 1)

            def ff_turn(c, u):
                pe.wait_ge(F["x_norm"], c + 1)
                if not (isinstance(c, int) and c < 2):
                    pe.wait_ge(F["quant"], c - 1)
                for t in range(TPC):
                    mm = pe.transpose(psS[u][:, t * P:(t + 1) * P], xs[:, u, t * P:(t + 1) * P], ident)
                mm.then_inc(F["x_turned"], 1)

            def ff_body(c, u, more):
                pe.wait_ge(F["quant"], c + 1)
                need(pe, F["taken"], c)
                for t in range(TPC):
                    mm = pe.matmul(psV[:, t * P:(t + 1) * P], xT[:, u, t * P:(t + 1) * P], ffT[:, :], start=True, stop=True)
                mm.then_inc(F["out"], 1)
                if more:
                    ff_turn(c + 1, 1 - u)

            over_chunks(pe, None, (0, 0), lambda: ff_turn(0, 0), ff_body)
            attention(stages[1], wts[1], nxt=(S["a2"], preparer(stages[2], wts[2]), stages[2].phases))
            attention(stages[2], wts[2], begun=True)

            def g_turn(c, u):
                pe.wait_ge(G["x_norm"], c + 1)
                if not (isinstance(c, int) and c < 2):
                    pe.wait_ge(G["x_up"], (c - 1) * 2)
                for t in range(TPC):
                    mm = pe.transpose(psS[u][:, t * P:(t + 1) * P], xs[:, u, t * P:(t + 1) * P], ident)
                mm.then_inc(G["x_turned"], 1)

            def g_body(c, u, more):
                if more:
                    g_turn(c + 1, 1 - u)
                pe.wait_ge(G["x_up"], c * 2 + 1)
                need(pe, G["logit_up"], c)
                for t in range(TPC):
                    mm = pe.matmul(psX[:, t * NEXP:(t + 1) * NEXP], xT[:, u, t * P:(t + 1) * P], mog[:, :], start=True, stop=True)
                mm.then_inc(G["logit"], 1)

            g_turn(0, 0)
            pe.wait_ge(S["a2"]["mix_free"], stages[2].tail() + 1)
            over_chunks(pe, None, (0, 0), lambda: None, g_body)

            NU = NEXP * 3
            pe.wait_ge(G["w_in"], 32)
            pe.wait_ge(G["x_up"], 2 * NCH)

            def hidden(c, k, first):
                e, p = divmod(k, 3)
                n = c * NU + k
                m = HCS[p]
                if not (first and k < 2):
                    pe.wait_ge(G["hid"], n - 1)
                w = e * HID + HO[p]
                rhs = ctxT[:, bass.ts(c, CW)]
                pe.matmul(psS[k % 2][0:m, 0:CW], w1v[:, w:w + m], rhs, start=True, stop=True).then_inc(G["h1"], 1)
                pe.matmul(psS[k % 2][0:m, CW:2 * CW], w2v[:, w:w + m], rhs, start=True, stop=True).then_inc(G["h2"], 1)

            def down(c, e, first):
                n = c * NEXP + e
                pe.wait_ge(G["hid"], c * NU + 3 * e + 3)
                if not (first and e < 2):
                    pe.wait_ge(G["taken"], n - 1)
                for t in range(TPC):
                    for p in range(3):
                        m = HCS[p]
                        mm = pe.matmul(psT[:, (e % 2) * CW + t * P:(e % 2) * CW + (t + 1) * P],
                                       hid(e % 2, p)[0:m, t * P:(t + 1) * P], w3[0:m, (e * 3 + p) * P:(e * 3 + p + 1) * P],
                                       start=p == 0, stop=p == 2)
                mm.then_inc(G["out"], 1)

            def expert_chunk(c, first):
                for k in range(NU):
                    hidden(c, k, first)
                    if k >= 3 and k % 3 == 0:
                        down(c, k // 3 - 1, first)
                    if k == 0 and not first:
                        down(c - 1, NEXP - 1, False)

            expert_chunk(0, True)
            with pe.Fori(1, NCH) as c:
                expert_chunk(c, False)
            down(NCH - 1, NEXP - 1, False)

        @block.scalar
        def _(act):
            def preparer(st, wt):
                s = S[st.name]

                def prepare(c, u, ph, own=False):
                    bank = bank_of[ph] if own else psX
                    if ph in st.on_dve:
                        return
                    act.wait_ge(s["mix_full"], st.prep(c, ph) + 1)
                    if ph == "x":
                        ins = act.copy(xT[:, u, :], bank[:, :])
                    elif ph == "ctx":
                        ins = act.copy(ctxT[:, bass.ts(c, CW)], bank[:, :])
                    elif ph == "v":
                        src = bank[:, :].rearrange("p (t b j d) -> p t b j d", t=TPC, b=2, j=8)
                        for h2 in range(2):
                            rows = slice(h2 * SEQ, (h2 + 1) * SEQ)
                            for b in range(2):
                                o = h2 * 16 + b * 8
                                ins = act.copy(vbd[rows, u, :, :, o:o + 8], src[rows, :, b, :, :])
                    elif ph[0] == "k":
                        h = int(ph[1])
                        if h == 0 and not (isinstance(c, int) and c < 2):
                            act.wait_ge(s[f"k_spread{u}"], of_parity(c - 2, u, 128))
                        o = W_CK + h * SEQ
                        ins = act.activation(kd[:, u, h, :], bank[:, :], ACT.Identity, bias=wt[:, o:o + 1])
                    else:
                        h = int(ph[1])
                        for b in range(2):
                            o = W_CQ + (h * 2 + b) * SEQ
                            ins = act.activation(
                                q[:, u, h, :].rearrange("p (t b k) -> p t b k", t=TPC, b=2)[:, :, b, :],
                                bank[:, :].rearrange("p (t b k) -> p t b k", t=TPC, b=2)[:, :, b, :],
                                ACT.Identity, bias=wt[:, o:o + 1], scale=cst[:, C_MB + b:C_MB + b + 1])
                    ins.then_inc(s["mix_free"], 1)

                return prepare

            def attention(st, wt, begun=False, nxt=None):
                s, prepare = S[st.name], preparer(st, wt)
                ready, phase = (nxt[1], nxt[2]) if nxt else (None, [None] * 6)

                def exps(c, i):
                    n = c * st.steps + i
                    act.wait_ge(s["shifted"], n + 1)
                    if not (is_first(c) and i < 2):
                        act.wait_ge(s["turned"], n - 1)
                    act.activation(prob[i % 2], psS[i % 2][:, :], ACT.Exp).then_inc(s["prob"], 1)

                def turned(n, i, early):
                    act.wait_ge(s["turned"], n + 1)
                    if not early:
                        act.wait_ge(s["ctx_full"], n - 1)
                    act.copy(probT[i % 2], psT[:, :]).then_inc(s["turned_out"], 1)

                def context(n, u, i):
                    t = i % TPC
                    act.wait_ge(s["ctx_full"], n + 1)
                    for b in range(2):
                        o = t * P + b * SEQ
                        ins = act.activation(q[:, u, :, o:o + SEQ],
                                             psV[:, 0:2 * P].rearrange("p (h k) -> p h k", h=2)[:, :, b * SEQ:(b + 1) * SEQ],
                                             ACT.Copy, scale=cst[:, C_MB + b:C_MB + b + 1])
                    ins.then_inc(s["ctx_done"], 1)

                def slot(c, u, i, at, more):
                    ph = st.slots.get((i, at))
                    if more and ph not in (None, "out"):
                        prepare(c + 1, 1 - u, ph)

                def body(c, u, more):
                    for i in range(st.steps):
                        behind(c, u, i, 3, st.steps, context)
                        slot(c, u, i, 0, more)
                        behind(c, u, i, 2, st.steps, lambda n, uu, k: turned(n, k, is_first(c) and k < 2))
                        exps(c, i)
                        slot(c, u, i, 1, more)

                def epilogue():
                    u, n = (NCH - 1) % 2, NCH * st.steps
                    before_next(ready, phase[0])
                    context(n - 3, u, st.steps - 3)
                    before_next(ready, phase[1])
                    for d in (2, 1):
                        turned(n - d, st.steps - d, False)
                        context(n - d, u, st.steps - d)
                        before_next(ready, phase[4 - d])
                    before_next(ready, phase[4], phase[5])

                over_chunks(act, None, (0, 0), lambda: [prepare(0, 0, ph, True) for ph in st.phases if not begun], body, epilogue)

            act.wait_ge(zeroed, ZEROED)
            def ml_prepare(c, u, ph):
                n = c * NP_ + MP.index(ph)
                if ph == "x":
                    act.wait_ge(M["mix_full"], n + 1)
                    act.copy(xT[:, u, :], psX[:, :]).then_inc(M["mix_free"], 1)
                elif ph == "pre":
                    act.wait_ge(M["gate_abs"], c + 1)
                    act.activation(flog, fabs, ACT.Exp).then_inc(M["gate_exp"], 1)
                    act.wait_ge(M["gate_exp"], c + 1)
                    act.activation(flog, flog, ACT.Ln, bias=1.0).then_inc(M["gate_ln"], 1)
                elif ph == "m":
                    act.wait_ge(M["nm"], c + 1)
                    act.activation(enm[u], enm[u], ACT.Exp).then_inc(M["enm"], TPC)

            attention(stages[0], wts[0], nxt=(M, ml_prepare, MP))


            def ml_turned(n, t, early):
                act.wait_ge(M["turned"], n + 1)
                if not early:
                    act.wait_ge(M["ctx_full"], n - 1)
                act.copy(probT[t % 2][:, 0:CW], psT[:, 0:CW]).then_inc(M["turned_out"], 1)

            def ml_decay(c, t):
                n = c * TPC + t
                act.wait_ge(M["score"], n + 1)
                if not (is_first(c) and t < 2):
                    act.wait_ge(M["turned"], n - 1)
                act.activation(prob[t % 2][:, 0:CW], psS[t % 2][:, CW:2 * CW], ACT.Exp).then_inc(M["decay"], 1)

            def ml_body(c, u, more):
                for i in range(TPC):
                    ml_decay(c, i)
                    behind(c, u, i, 1, TPC, lambda n, uu, k: ml_turned(n, k, is_first(c) and k < 2))
                    for ph in (("x",), ("pre",), (), ("m",))[i]:
                        if more:
                            ml_prepare(c + 1, 1 - u, ph)

            over_chunks(act, None, (0, 0), lambda: None, ml_body,
                        lambda: ml_turned(NCH * TPC - 1, 3, False))
            attention(stages[1], wts[1], nxt=(S["a2"], preparer(stages[2], wts[2]), stages[2].phases))
            attention(stages[2], wts[2], begun=True)

            def g_turned(c, u):
                act.wait_ge(G["x_turned"], c + 1)
                act.copy(xT[:, u, :], psS[u][:, 0:CW]).then_inc(G["x_up"], 1)
                act.copy(ctxT[:, bass.ts(c, CW)], psS[u][:, 0:CW]).then_inc(G["x_up"], 1)

            def g_body(c, u, more):
                if more:
                    g_turned(c + 1, 1 - u)
                act.wait_ge(G["logit"], c + 1)
                act.copy(gl[:, bass.ts(c, TPC), :], psX[:, 0:32].rearrange("p (t g) -> p t g", t=TPC))\
                   .then_inc(G["logit_up"], 1)

            over_chunks(act, None, (0, 0), lambda: g_turned(0, 0), g_body)
            NU = NEXP * 3

            def sils(c, first):
                for k in range(NU):
                    n = c * NU + k
                    m = HCS[k % 3]
                    act.wait_ge(G["h1"], n + 1)
                    if not (first and k < 2):
                        act.wait_ge(G["hid"], n - 1)
                    act.activation(sil(k % 2)[0:m, :], psS[k % 2][0:m, 0:CW], ACT.Silu).then_inc(G["sil"], 1)
                    if first and k == 1:
                        act.wait_ge(G["shift"], 1)
                        act.activation(gate[:, :, :], gate[:, :, :], ACT.Exp).then_inc(G["exp"], 1)

            sils(0, True)
            with act.Fori(1, NCH) as c:
                sils(c, False)

        @block.vector
        def _(dve):
            dve.memset(kbd[0][:, :, :, :], 0.0).then_inc(zeroed, 1)
            dve.wait_ge(w_first, 48)
            dve.tensor_scalar(wts[0][:, W_K:W_V], wts[0][:, W_K:W_V], stages[0].scale, None, ALU.mult).then_inc(w_scaled, 1)
            dve.wait_ge(zeroed, ZEROED)

            def normalise(c, u, s, prev):
                dve.wait_ge(prev, c + 1)
                if not (isinstance(c, int) and c < 2):
                    dve.wait_ge(s["x_kept"], c - 1)
                for t in range(TPC):
                    n = c * TPC + t
                    ins = dve.tensor_scalar(xs[:, u, t * P:(t + 1) * P], xres[:, n, :], mv[:, n, 0:1],
                                            rstd[:, bass.ts(n, 1)], ALU.subtract, ALU.mult)
                ins.then_inc(s["x_norm"], 1)

            def moments(chain, c, done):
                alone(dve)
                for t in range(TPC):
                    ins = dve.bn_stats(stats[:, t, :], xres[:, c * TPC + t, :])
                chain.link(ins)
                alone(dve)
                for t in range(TPC):
                    ins = dve.bn_aggr(mvs[:, t, :], stats[:, t, :])
                chain.link(ins)
                dve.tensor_scalar(mv[:, bass.ts(c, TPC), 0], mvs[:, :, 0], 0.0, None, ALU.add)
                dve.tensor_scalar(mv[:, bass.ts(c, TPC), 1], mvs[:, :, 1], LN_EPS, None, ALU.add).then_inc(done, 1)

            def values_out(u, wv, s, bank):
                src = bank[:, :].rearrange("p (t b j d) -> p t b j d", t=TPC, b=2, j=8)
                for h2 in range(2):
                    rows = slice(h2 * SEQ, (h2 + 1) * SEQ)
                    for b in range(2):
                        o = h2 * 16 + b * 8
                        bv = wv[rows, h2 * SEQ:(h2 + 1) * SEQ].rearrange("p (j d) -> p j d", j=8)
                        ins = dve.tensor_tensor(vbd[rows, u, :, :, o:o + 8], src[rows, :, b, :, :],
                                                spread(bv.unsqueeze(1), [SEQ, TPC, 8, DH]), ALU.add)
                ins.then_inc(s["mix_free"], 1)

            def preparer(st, wt, prev):
                s = S[st.name]

                def prepare(c, u, ph, own=False):
                    if ph == "norm" and not st.first:
                        normalise(c, u, s, prev)
                    if ph not in st.on_dve:
                        return
                    bank = bank_of[ph] if own else psX
                    dve.wait_ge(s["mix_full"], st.prep(c, ph) + 1)
                    if ph[0] == "k":
                        h = int(ph[1])
                        if h == 0 and not (isinstance(c, int) and c < 2):
                            dve.wait_ge(s[f"k_spread{u}"], of_parity(c - 2, u, 128))
                        ck = wt[:, W_CK + h * SEQ:W_CK + (h + 1) * SEQ]
                        dve.tensor_tensor(kd[:, u, h, :].rearrange("p (b k) -> p b k", b=8),
                                          bank[:, :].rearrange("p (b k) -> p b k", b=8),
                                          spread(ck.unsqueeze(1), [P, 8, SEQ]), ALU.add).then_inc(s["mix_free"], 1)
                    elif ph[0] == "q":
                        h = int(ph[1])
                        for b in range(2):
                            o = W_CQ + (h * 2 + b) * SEQ
                            cq = wt[:, o:o + SEQ]
                            ins = dve.scalar_tensor_tensor(
                                q[:, u, h, :].rearrange("p (t b k) -> p t b k", t=TPC, b=2)[:, :, b, :],
                                bank[:, :].rearrange("p (t b k) -> p t b k", t=TPC, b=2)[:, :, b, :],
                                cst[:, C_MB + b:C_MB + b + 1], spread(cq.unsqueeze(1), [P, TPC, SEQ]), ALU.mult, ALU.add)
                        ins.then_inc(s["mix_free"], 1)
                    else:
                        values_out(u, wt[:, W_BV:W_BV + P], s, bank)

                return prepare

            def attention(st, wt, prev, begun=(), nxt=None, norm_next=None):
                s, prepare = S[st.name], preparer(st, wt, prev)
                chain = Chain(dve, s["dve"])

                def shift(c, i):
                    sc = psS[i % 2][:, :].rearrange("p (h k) -> p h k", h=16)
                    for h in range(HALVES):
                        dve.wait_ge(s["score"], c * (2 * st.steps) + (2 * i + h + 1))
                        ins = dve.tensor_reduce(rmax[i % 2][:, 8 * h:8 * h + 8], sc[:, 8 * h:8 * h + 8, :], AX.X, ALU.max)
                    chain.link(ins)
                    dve.tensor_tensor(sc, sc, spread(rmax[i % 2].unsqueeze(2), [P, 16, SEQ]),
                                      ALU.subtract).then_inc(s["shifted"], 1)

                def total(n, i):
                    dve.wait_ge(s["prob"], n + 1)
                    chain.link(dve.tensor_reduce(recip[i % 2], prob[i % 2].rearrange("p (h k) -> p h k", h=16), AX.X, ALU.add))
                    dve.reciprocal(recip[i % 2], recip[i % 2]).then_inc(s["recip"], 1)

                def residual(c, use):
                    dve.wait_ge(s["x_kept"], c * 2 + 2 if st.first else c + 1)
                    dve.wait_ge(s["mix_full"], use + 1)
                    dve.tensor_tensor(xres[:, bass.ts(c, TPC), :], psX[:, :].rearrange("p (n d) -> p n d", n=TPC),
                                      xres[:, bass.ts(c, TPC), :], ALU.add).then_inc(s["mix_free"], 1)
                    dve.wait_ge(s["mix_free"], use + 1)
                    moments(chain, c, s["stat"])

                def slot(c, u, i, at, more):
                    ph = st.slots.get((i, at))
                    if ph == "out" and not is_first(c):
                        residual(c - 1, st.use(c, "out"))
                    elif ph not in (None, "out") and more:
                        prepare(c + 1, 1 - u, ph)

                def body(c, u, more):
                    for i in range(st.steps):
                        if i == 0 and more:
                            prepare(c + 1, 1 - u, "norm")
                        shift(c, i)
                        slot(c, u, i, 0, more)
                        behind(c, u, i, 1, st.steps, lambda n, uu, k: total(n, k))
                        slot(c, u, i, 1, more)

                def epilogue():
                    if norm_next:
                        norm_next()
                    total(NCH * st.steps - 1, st.steps - 1)
                    ready, early, late = nxt or (None, (), ())
                    before_next(ready, *early)
                    residual(NCH - 1, st.tail())
                    before_next(ready, *late)

                over_chunks(dve, chain, (2 * st.steps - 1, 2 * st.steps + 2),
                            lambda: [prepare(0, 0, ph, True) for ph in ["norm"] + st.phases if ph not in begun], body, epilogue)

            chain = Chain(dve, M["dve"])

            def ml_prepare(c, u, ph):
                n = c * NP_ + MP.index(ph) if ph in MP else None
                if ph == "norm":
                    normalise(c, u, M, S["a0"]["rstd"])
                if ph == "lf":
                    dve.wait_ge(M["gate_ln"], c + 1)
                    dve.scalar_tensor_tensor(lf, pre[:, :, 8:16], 0.0, flog, ALU.min, ALU.subtract).then_inc(M["gate_lf"], 1)
                if ph in ("norm", "lf", "x"):
                    return
                dve.wait_ge(M["mix_full"], n + 1)
                if ph == "v":
                    src = psX[:, :].rearrange("p (t b j d) -> p t b j d", t=TPC, b=2, j=4)
                    for h2 in range(2):
                        rows = slice(h2 * SEQ, (h2 + 1) * SEQ)
                        for b in range(2):
                            o = h2 * 32 + b * 16
                            ins = dve.tensor_copy(vm[rows, u, :, :, o:o + 16], src[rows, :, b, :, :])
                    ins.then_inc(M["mix_free"], 1)
                elif ph == "pre":
                    dve.tensor_tensor(pre, psX[:, 0:64].rearrange("p (t g) -> p t g", t=TPC),
                                      spread(mlw[:, 48:64].unsqueeze(1), [P, TPC, 16]), ALU.add).then_inc(M["mix_free"], 1)
                    dve.wait_ge(M["mix_free"], n + 1)
                    dve.scalar_tensor_tensor(fabs, pre[:, :, 8:16], -1.0, pre[:, :, 8:16], ALU.mult, ALU.min).then_inc(M["gate_abs"], 1)
                elif ph == "cum":
                    chain.link(dve.tensor_copy(cum, psX[:, 0:32]))
                    dve.tensor_tensor(agate.rearrange("p (t g) -> p t g", t=TPC), pre[:, :, 0:8],
                                      cum.rearrange("p (t g) -> p t g", t=TPC), ALU.subtract).then_inc(M["mix_free"], 1)
                elif ph == "a":
                    chain.link(dve.tensor_copy(aT, psX[0:32, 0:P]))
                    chain.link(dve.tensor_tensor_scan(MT, cst[0:32, C_RST:C_RST + P], aT, 0.0, ALU.add, ALU.max))
                    a4 = aT.rearrange("p (b k) -> p b k", b=2).unsqueeze(2)
                    d4 = cst[0:32, C_DEL:C_DEL + 8].unsqueeze(1).unsqueeze(3)
                    dve.tensor_tensor(abd[0:32, u, :, :, :], spread(a4, [32, 2, 8, SEQ]), spread(d4, [32, 2, 8, SEQ]),
                                      ALU.mult).then_inc(M["mix_free"], 1)
                else:
                    dve.tensor_scalar(negM[u], psX[:, 0:32].rearrange("p (t g) -> p t g", t=TPC), -1.0, None,
                                      ALU.mult).then_inc(M["mix_free"], 1)
                    dve.wait_ge(M["mix_free"], n + 1)
                    dve.tensor_tensor(enm[u], negM[u], cum.rearrange("p (t g) -> p t g", t=TPC), ALU.subtract)\
                       .then_inc(M["nm"], 1)

            attention(stages[0], wts[0], None, nxt=(ml_prepare, ("pre", "lf", "cum", "a"), ("v", "m")),
                      norm_next=lambda: ml_prepare(0, 0, "norm"))

            def ml_ctx(n, u, t):
                hb = tmp[:, u, :].rearrange("p (t h d) -> p t h d", t=TPC, h=8)
                dve.wait_ge(M["ctx_full"], n + 1)
                pv = psV[:, 0:264].rearrange("p (j k) -> p j k", j=4)
                nr = nrm.rearrange("p (j k) -> p j k", j=4)
                if t == 0:
                    dve.wait_ge(M["enm"], n + 4)
                en = enm[u][:, t, :].rearrange("p (j k) -> p j k", j=4)
                chain.link(dve.scalar_tensor_tensor(nr, pv[:, :, 64:66], -1.0, en, ALU.mult, ALU.max))
                chain.link(dve.tensor_tensor(nr, pv[:, :, 64:66], nr, ALU.max))
                chain.link(dve.tensor_scalar(nrm, nrm, 1e-6, None, ALU.add))
                chain.link(dve.reciprocal(nrm, nrm))
                for b in range(2):
                    rows = slice(b * SEQ, (b + 1) * SEQ)
                    src = pv[rows, :, 0:64].rearrange("p j (h b d) -> p j h b d", h=2, b=2)[:, :, :, b, :]
                    rec = nrm[rows, :].rearrange("p (j h) -> p j h", j=4).unsqueeze(3)
                    ins = dve.tensor_tensor(hb[rows, t, :, :].rearrange("p (j h) d -> p j h d", j=4), src,
                                            spread(rec, [SEQ, 4, 2, 16]), ALU.mult)
                ins.then_inc(M["ctx_done"], 1)

            def ml_heads(c, u):
                hb3 = tmp[:, u, :].rearrange("p (g d) -> p g d", g=32)
                sq3 = tmp2[:, :].rearrange("p (g d) -> p g d", g=32)
                dve.wait_ge(M["ctx_done"], c * TPC + TPC)
                chain.link(dve.tensor_reduce(hmu, hb3, AX.X, ALU.add))
                chain.link(dve.tensor_scalar(hmu, hmu, 1.0 / 16, None, ALU.mult))
                chain.link(dve.tensor_tensor(hb3, hb3, head(hmu), ALU.subtract))
                chain.link(dve.tensor_tensor(sq3, hb3, hb3, ALU.mult))
                chain.link(dve.tensor_reduce(hvar, sq3, AX.X, ALU.add))
                dve.tensor_scalar(hvar, hvar, 1.0 / 16, 1e-6, ALU.mult, ALU.add).then_inc(M["var"], 1)

            ml_chain = chain

            def ml_moments(c):
                dve.wait_ge(M["summed"], c + 1)
                moments(ml_chain, c, M["stat"])

            def ml_body(c, u, more):
                for i in range(TPC):
                    if more and i == 0:
                        ml_prepare(c + 1, 1 - u, "norm")
                    n = c * TPC + i
                    dve.wait_ge(M["decay"], n + 1)
                    dve.scalar_tensor_tensor(prob[i % 2][:, 0:CW], psS[i % 2][:, 0:CW], 0.25, prob[i % 2][:, 0:CW],
                                             ALU.mult, ALU.mult).then_inc(M["prod"], 1)
                    if more and (i, 0) in MSLOT:
                        ml_prepare(c + 1, 1 - u, MSLOT[i, 0])
                    if more and i == 3:
                        ml_prepare(c + 1, 1 - u, MSLOT[i, 1])
                    behind(c, u, i, 2, TPC, ml_ctx)
                    if more and i < 3 and (i, 1) in MSLOT:
                        ml_prepare(c + 1, 1 - u, MSLOT[i, 1])
                    if more and i == 1:
                        ml_prepare(c + 1, 1 - u, "lf")
                    if i == 1 and not is_first(c):
                        ml_heads(c - 1, 1 - u)
                    if i == 3 and not is_first(c):
                        ml_moments(c - 1)

            def ff_weights():
                dve.wait_ge(w_in, N_W)
                scale, finite = Chain(dve, scl_done), scl[:, 3:4]
                scale.link(dve.memset(scl[:, 1:3], 0.0))
                scale.link(dve.tensor_scalar(scl[:, 4:5], scl[:, 0:1], 1e-5, None, ALU.max))
                scale.link(dve.reciprocal(scl[:, 5:6], scl[:, 4:5]))
                scale.link(dve.tensor_scalar(scl[:, 6:7], scl[:, 4:5], FMAX, None, ALU.is_le))
                scale.link(dve.tensor_tensor(finite, scl[:, 0:1], scl[:, 0:1], ALU.is_equal))
                scale.link(dve.tensor_tensor(finite, finite, scl[:, 6:7], ALU.mult))
                scale.link(dve.copy_predicated(scl[:, 1:2], finite.bitcast(U32), scl[:, 4:5]))
                dve.copy_predicated(scl[:, 2:3], finite.bitcast(U32), scl[:, 5:6]).then_inc(scl_up, 1)
                dve.wait_ge(scl_up, 1)
                dve.wait_ge(tern_T, 1)
                dve.tensor_copy(ffT[:, :], psX[:, 0:P])

            def ml_epilogue():
                ml_ctx(NCH * TPC - 2, 1, 2)
                ml_ctx(NCH * TPC - 1, 1, 3)
                ml_heads(NCH - 1, 1)
                ff_weights()

            over_chunks(dve, chain, (3 + 3 + 8, 3 + 16 + 5 + 2),
                        lambda: None,
                        ml_body, ml_epilogue)

            chain = Chain(dve, F["dve"])

            def ff_quantise(c, u):
                dve.wait_ge(F["x_turned"], c + 1)
                qn = xT[:, u, :]
                chain.link(dve.tensor_scalar(qn, psS[u][:, 0:CW], scl[:, 2:3], ROUND, ALU.mult, ALU.add))
                chain.link(dve.tensor_scalar(qn, qn, -ROUND, 127.0, ALU.add, ALU.min))
                dve.tensor_scalar(xT[:, u, :], qn, -127.0, scl[:, 1:2], ALU.max, ALU.mult).then_inc(F["quant"], 1)

            def ff_body(c, u, more):
                if more:
                    normalise(c + 1, 1 - u, F, M["rstd"])
                else:
                    dve.wait_ge(F["x_kept"], NCH - 1)
                    normalise(0, 0, S["a1"], F["rstd"])
                dve.wait_ge(F["x_kept"], c + 1)
                dve.wait_ge(F["out"], c + 1)
                dve.tensor_tensor(xres[:, bass.ts(c, TPC), :], psV[:, :].rearrange("p (n d) -> p n d", n=TPC),
                                  xres[:, bass.ts(c, TPC), :], ALU.add).then_inc(F["taken"], 1)
                dve.wait_ge(F["taken"], c + 1)
                moments(chain, c, F["stat"])
                if more:
                    ff_quantise(c + 1, 1 - u)
                if is_first(c):
                    ml_moments(NCH - 1)

            over_chunks(dve, chain, (2 + 2 + 2, 2 + 2), lambda: [normalise(0, 0, F, M["rstd"]), ff_quantise(0, 0)], ff_body)
            def g_norm(c, u):
                dve.wait_ge(S["a2"]["rstd"], c + 1)
                if not (isinstance(c, int) and c < 2):
                    dve.wait_ge(G["x_turned"], c - 1)
                    dve.wait_ge(G["x_kept"], c - 1)
                for t in range(TPC):
                    n = c * TPC + t
                    ins = dve.tensor_scalar(xs[:, u, t * P:(t + 1) * P], xres[:, n, :], mv[:, n, 0:1],
                                            rstd[:, bass.ts(n, 1)], ALU.subtract, ALU.mult)
                ins.then_inc(G["x_norm"], 1)

            cross = preparer(stages[2], wts[2], S["a1"]["rstd"])
            attention(stages[1], wts[1], F["rstd"], begun=("norm",), nxt=(cross, ("v",), ("q1",)), norm_next=lambda: cross(0, 0, "norm"))
            attention(stages[2], wts[2], S["a1"]["rstd"], begun=["norm"] + stages[2].phases, norm_next=lambda: g_norm(0, 0))

            chain = Chain(dve, G["dve"])

            iota = spread(cst[:, C_IOTA:C_IOTA + 8].unsqueeze(1), [P, NT, NEXP])

            def each(a):
                return spread(a.unsqueeze(2), [P, NT, NEXP])

            over_chunks(dve, None, (0, 0), lambda: None,
                        lambda c, u, more: g_norm(c + 1, 1 - u) if more else None)
            dve.wait_ge(G["logit_up"], NCH)

            def gates(part):
                if part == 0:
                    chain.link(dve.tensor_reduce(gm, gl, AX.X, ALU.max))
                    chain.link(dve.tensor_tensor(g1, gl, each(gm), ALU.is_equal))
                    dve.tensor_tensor(gate[:, :, :], gl, each(gm), ALU.subtract).then_inc(G["shift"], 1)
                elif part == 1:
                    chain.link(dve.tensor_tensor(g1, g1, iota, ALU.mult))
                    chain.link(dve.tensor_reduce(gn, g1, AX.X, ALU.max))
                    chain.link(dve.tensor_tensor(g1, iota, each(gn), ALU.is_equal))
                elif part == 2:
                    chain.link(dve.scalar_tensor_tensor(g2, g1, -1e30, gl, ALU.mult, ALU.add))
                    chain.link(dve.tensor_reduce(gn, g2, AX.X, ALU.max))
                    chain.link(dve.tensor_tensor(g2, g2, each(gn), ALU.is_equal))
                elif part == 3:
                    chain.link(dve.tensor_tensor(g2, g2, iota, ALU.mult))
                    chain.link(dve.tensor_reduce(gn, g2, AX.X, ALU.max))
                    chain.link(dve.tensor_tensor(g2, iota, each(gn), ALU.is_equal))
                else:
                    chain.link(dve.tensor_tensor(g1, g1, g2, ALU.add))
                    dve.wait_ge(G["exp"], 1)
                    chain.link(dve.tensor_tensor(g1, g1, gate[:, :, :], ALU.mult))
                    chain.link(dve.tensor_reduce(gn, g1, AX.X, ALU.add))
                    chain.link(dve.reciprocal(gn, gn))
                    chain.link(dve.tensor_tensor(gate[:, :, :], g1, each(gn), ALU.mult))

            NU = NEXP * 3
            fin = Chain(dve, G["fin"])

            def take(c, e, first):
                dve.wait_ge(G["out"], c * NEXP + e + 1)
                if first and e == 0:
                    dve.wait_ge(G["x_kept"], NCH)
                else:
                    dve.wait_ge(G["taken"], c * NEXP + e)
                for t in range(TPC):
                    n = c * TPC + t
                    ins = dve.scalar_tensor_tensor(xres[:, n, :], psT[:, (e % 2) * CW + t * P:(e % 2) * CW + (t + 1) * P],
                                                   gate[:, n, e:e + 1], xres[:, n, :], ALU.mult, ALU.add)
                ins.then_inc(G["taken"], 1)

            def out_moments(c):
                take(c, NEXP - 1, False)
                dve.wait_ge(G["taken"], (c + 1) * NEXP)
                moments(fin, c, G["var"])

            def out_norm(c):
                dve.wait_ge(G["rstd"], c + 1)
                for t in range(TPC):
                    n = c * TPC + t
                    ins = dve.tensor_scalar(xres[:, n, :], xres[:, n, :], mv[:, n, 0:1], rstd[:, bass.ts(n, 1)],
                                            ALU.subtract, ALU.mult)
                ins.then_inc(G["normed"], 1)

            def expert_chunk(c, first):
                for k in range(NU):
                    n = c * NU + k
                    e, p = divmod(k, 3)
                    m = HCS[p]
                    dve.wait_ge(G["sil"], n + 1)
                    dve.wait_ge(G["h2"], n + 1)
                    if p == 0 and not (first and e < 2):
                        dve.wait_ge(G["out"], c * NEXP + e - 1)
                    dve.tensor_tensor(hid(e % 2, p)[0:m, :], sil(k % 2)[0:m, :], psS[k % 2][0:m, CW:2 * CW],
                                      ALU.mult).then_inc(G["hid"], 1)
                    if first and k < 5:
                        gates(k)
                    if k >= 5 and k % 3 == 2:
                        take(c, k // 3 - 1, first)
                    if k == 2 and not first:
                        out_moments(c - 1)
                    if k == 6 and not first:
                        out_norm(c - 1)

            expert_chunk(0, True)
            with dve.Fori(1, NCH) as c:
                fin.at(c * 2 - 2)
                expert_chunk(c, False)
            fin.at(2 * NCH - 2)
            out_moments(NCH - 1)
            out_norm(NCH - 1)


def kernel(**inputs):
    import numpy as np
    import ml_dtypes
    import concourse.bacc as bacc
    from concourse.bass_utils import run_bass_kernel_spmd

    i = {k: np.asarray(v) for k, v in inputs.items()}
    f32 = np.float32
    row_head = np.array([[(8 * half + 2 * (r // 32) + (r // 16) % 2) for r in range(P)] for half in range(2)])
    row_b = np.array([(r // 8) % 2 for r in range(P)])
    row_d = np.array([r % 8 for r in range(P)])
    col = [row_head[h] * 8 + row_d for h in range(2)]
    vcol = np.array([[(2 * j + h2) * 8 + d for j in range(8) for d in range(8)] for h2 in range(2)]).reshape(-1)

    def blob(wq, bq, wk, bk, wv, bv, wo, bo):
        b = np.zeros((P, W_N), f32)
        for h in range(2):
            b[:, W_Q + h * P:W_Q + (h + 1) * P] = wq[:, col[h]]
            b[:, W_K + h * P:W_K + (h + 1) * P] = wk[:, col[h]]
            b[:, W_CK + h * SEQ:W_CK + (h + 1) * SEQ] = bk[col[h]]
            b[:, W_O + h * P:W_O + (h + 1) * P] = wo[col[h]]
            for s in range(2):
                o = W_CQ + (2 * h + s) * SEQ
                mine = row_b == s
                b[mine, o:o + SEQ] = bq[col[h]][mine]
        b[:, W_V:W_V + P] = wv[:, vcol]
        b[:, W_BV:W_BV + P] = np.broadcast_to(bv[vcol], (P, P))
        b[:, W_BO:W_BO + P] = np.broadcast_to(bo, (P, P))
        return b

    def along(v):
        return np.broadcast_to(v[:, None], (P, SEQ))

    slopes = (2.0 ** (-8.0 * np.arange(1, 17) / 16)).astype(f32)
    pos = np.arange(SEQ, dtype=f32)
    wq = np.zeros((P, 16, 8), f32)
    wk = np.zeros((P, 16, 8), f32)
    wq[:, :, 0:4] = i["L0_attn_Wq"].reshape(P, 16, 4)
    wk[:, :, 0:4] = np.tile(i["L0_attn_Wk"], (1, 4)).reshape(P, 16, 4)
    qc = np.zeros((16, 8, SEQ), f32)
    kc = np.zeros((16, 8, SEQ), f32)
    qc[:, 4] = 1.0
    kc[:, 4] = slopes[:, None] * pos
    qc[:, 5] = -pos
    kc[:, 5] = slopes[:, None]
    b0 = blob(wq.reshape(P, P), qc.reshape(P, SEQ), wk.reshape(P, P), kc.reshape(P, SEQ),
              np.tile(i["L0_attn_Wv"], (1, 4)), np.zeros(P, f32), i["L0_attn_Wp"], i["L0_attn_bp"])
    qkv, bqkv = i["L1_attn_Wqkv_w"], i["L1_attn_Wqkv_b"]
    b1 = blob(qkv[0:P].T, along(bqkv[0:P]), qkv[P:2 * P].T, along(bqkv[P:2 * P]), qkv[2 * P:].T, bqkv[2 * P:],
              i["L1_attn_out_w"].T, i["L1_attn_out_b"])
    b2 = blob(i["L1_xattn_w_q"].T, along(i["L1_xattn_b_q"]), i["L1_xattn_w_k"].T, along(i["L1_xattn_b_k"]),
              i["L1_xattn_w_v"].T, i["L1_xattn_b_v"], i["L1_xattn_w_o"].T, i["L1_xattn_b_o"])

    ml = np.zeros((P, 48 + 16 + P), f32)
    for s in range(3):
        ml[:, 16 * s:16 * s + 8] = i["L0_xattn_igate_kernel"][P * s:P * (s + 1)]
        ml[:, 16 * s + 8:16 * s + 16] = i["L0_xattn_fgate_kernel"][P * s:P * (s + 1)]
    ml[:, 48:56] = i["L0_xattn_igate_bias"]
    ml[:, 56:64] = i["L0_xattn_fgate_bias"]
    ml[:, 64:] = i["L0_xattn_outnorm_weight"].reshape(-1)
    ffw = np.zeros((P, P + 1), f32)
    ffw[:, 0:P] = i["L0_ffn_bias"]

    r = np.arange(P)
    c = np.zeros((P, C_N), f32)
    c[:, C_ID:C_ID + P] = np.eye(P)
    c[:, C_MB] = row_b == 0
    c[:, C_MB + 1] = row_b == 1
    c[:, C_CUM:C_CUM + P] = (r[:, None] <= r[None, :]) & (r[:, None] // SEQ == r[None, :] // SEQ)
    mcol = np.array([(2 * j + h2) * 16 + d for h2 in range(2) for j in range(4) for d in range(16)])
    c[mcol, C_PV + r] = 1.0
    for t in range(TPC):
        c[8 * t:8 * t + 8, C_SEL + t * SEQ:C_SEL + (t + 1) * SEQ] = 1.0
    c[0:32, C_DEL:C_DEL + 8] = (r[0:32, None] % 8) == np.arange(8)[None, :]
    c[:, C_RST:C_RST + P] = np.where(r % SEQ == 0, f32(-1e30), f32(0))
    c[:, C_HALF:C_HALF + 32] = -0.5
    c[:, C_IOTA:C_IOTA + 8] = 8 - np.arange(8)
    m16 = np.zeros((P, 256), f32)
    m16[:, 0:P] = -80.0 * np.eye(P)
    upper = np.arange(SEQ)[None, :] > (r % SEQ)[:, None]
    m16[:, P:P + SEQ] = 125.0 * upper
    m16[:, P + SEQ:P + 2 * SEQ] = 1e28 * upper
    m16 = m16.astype(ml_dtypes.bfloat16)

    w3 = np.zeros((HCS[0], NEXP, 3, P), f32)
    for p in range(3):
        w3[0:HCS[p], :, p] = i["L1_ffn_W3"][:, :, HO[p]:HO[p] + HCS[p]].transpose(2, 0, 1)
    arrays = {
        "x": i["x"].reshape(-1, P), "ctx": i["ctx_1024"].reshape(-1, P), "c32": c, "c16": m16,
        "w_a0": b0, "w_a1": b1, "w_a2": b2, "w_ml": ml, "w_ff": ffw,
        "w_tern": i["L0_ffn_ternary_weight"], "w_scale": np.broadcast_to(i["L0_ffn_act_scale"].reshape(1, 1), (P, 1)),
        "w_gate": i["L1_ffn_Wg"].T,
        "w_e1": i["L1_ffn_W1"].reshape(-1, P).T, "w_e2": i["L1_ffn_W2"].reshape(-1, P).T,
        "w_e3": w3.reshape(HCS[0], -1),
    }
    arrays = {k: np.ascontiguousarray(v) for k, v in arrays.items()}
    nc = bacc.Bacc("TRN2", target_bir_lowering=False, num_devices=1)
    a = {k: nc.dram_tensor(f"in_{k}", v.shape, mybir.dt.from_np(v.dtype), kind="ExternalInput").ap()
         for k, v in arrays.items()}
    o = nc.dram_tensor("out_0", (NT * P, P), F32, kind="ExternalOutput").ap()
    decoder(nc, a["x"], a["ctx"], a["c32"], a["c16"], [a["w_a0"], a["w_a1"], a["w_a2"]], a["w_ml"], a["w_ff"],
            a["w_tern"], a["w_scale"], a["w_gate"], a["w_e1"], a["w_e2"], a["w_e3"], o)
    res = run_bass_kernel_spmd(nc, [{f"in_{k}": v for k, v in arrays.items()}], core_ids=[0])
    return res.results[0]["out_0"].reshape(64, SEQ, P)
```
